# Optimizing a Trainium2 kernel written in Bass

```python
import numpy as np
import jax
import jax.numpy as jnp

def _softmax(x, axis=-1):
    return jax.nn.softmax(x, axis=axis)

def _gelu(x):
    return jax.nn.gelu(x, approximate=True)

def _silu(x):
    return jax.nn.silu(x)

def _sigmoid(x):
    return jax.nn.sigmoid(x)

def _layernorm(x, axis=-1, eps=1e-05):
    m = jnp.mean(x, axis=axis, keepdims=True)
    v = jnp.var(x, axis=axis, keepdims=True)
    return (x - m) / jnp.sqrt(v + eps)

def _scatter_add(tgt, idx, src, axis=0):
    return tgt.at[idx].add(src)

def _segment_sum(src, seg, n):
    return jax.ops.segment_sum(src, seg, n)
kernel_name = 'mk_decoder_preln_d1_seqx_r8_65db7a'

def setup_inputs(seed: int=0):
    np.random.seed(seed)
    _w = jnp.asarray

    def _rec_inputs():
        import jax
        import jax.numpy as jnp
        _rk = jax.random.key(seed)
        x = -0.0003929 + 0.9999 * jax.random.normal(jax.random.fold_in(_rk, 1), (16, 64, 512), jnp.float32)
        _lenS = 64 - jax.random.randint(jax.random.fold_in(_rk, 7), (16,), 0, max(1, 64 // 4) + 1, jnp.int32)
        _lenS2 = 64 - jax.random.randint(jax.random.fold_in(_rk, 8), (16,), 0, max(1, 64 // 4) + 1, jnp.int32)
        _ctx_4096P = jax.random.normal(jax.random.fold_in(_rk, 11), (16, 16, 512), jnp.float32)
        _ctx_4096c = jax.random.dirichlet(jax.random.fold_in(_rk, 511), 0.3 * jnp.ones((16,), jnp.float32), (16, 64))
        _ctx_4096t = jnp.einsum('bsk,bkd->bsd', _ctx_4096c, _ctx_4096P)
        _ctx_4096t = _ctx_4096t * jax.lax.rsqrt(jnp.mean(jnp.square(_ctx_4096t)) + 1e-12) * 0.953939
        ctx_4096 = 2.81802e-05 + 1.00001 * (_ctx_4096t + 0.3 * jax.random.normal(jax.random.fold_in(_rk, 611), (16, 64, 512), jnp.float32))
        return (x, ctx_4096)
    x, ctx_4096 = _rec_inputs()

    def _L0_attn_setup():
        import jax, jax.numpy as jnp
        import numpy as np
        B, S, D = (2, 128, 512)
        H, KVH, HD = (32, 8, 128)
        GROUPS = H // KVH
        LAT, LH = (128, 32)
        THETA = 10000.0
        SCALE = 1.0 / float(np.sqrt(HD))

        def _rope_cos_sin(seq_len, head_dim, theta):
            inv_freq = 1.0 / theta ** (jnp.arange(0, head_dim, 2, dtype=jnp.float32) / head_dim)
            t = jnp.arange(seq_len, dtype=jnp.float32)
            freqs = jnp.outer(t, inv_freq)
            emb = jnp.concatenate([freqs, freqs], axis=-1)
            return (jnp.cos(emb), jnp.sin(emb))

        def _rotate_half(x):
            h = x.shape[-1] // 2
            return jnp.concatenate([-x[..., h:], x[..., :h]], axis=-1)

        def _apply_rope(x, cos, sin):
            return x * cos[None, None] + _rotate_half(x) * sin[None, None]

        def _causal_attn(q, k, v, scale):
            s = jnp.einsum('bhqd,bhkd->bhqk', q, k) * scale
            mask = jnp.tril(jnp.ones((q.shape[2], k.shape[2]), dtype=bool))
            s = jnp.where(mask[None, None], s, jnp.finfo(s.dtype).min)
            p = jax.nn.softmax(s, axis=-1)
            return jnp.einsum('bhqk,bhkd->bhqd', p, v)
        key = jax.random.key(seed)
        ks = jax.random.split(key, 9)
        sd = 0.02
        mk = lambda k, shape: jax.random.normal(k, shape, dtype=jnp.float32) * sd
        return {'hidden_states': jax.random.normal(ks[0], (B, S, D), dtype=jnp.float32), 'w_q': mk(ks[1], (D, H * HD)), 'w_k': mk(ks[2], (D, KVH * HD)), 'w_v': mk(ks[3], (D, KVH * HD)), 'w_o': mk(ks[4], (H * HD, D)), 'w_lq': mk(ks[5], (D, LAT)), 'w_lk': mk(ks[6], (LAT, LH * HD)), 'w_lv': mk(ks[7], (D, LH * HD)), 'w_lo': mk(ks[8], (LH * HD, D))}
    _L0_attn_all = _L0_attn_setup()
    _L0_attn_in = {k: v for k, v in _L0_attn_all.items() if k in ('w_q', 'w_k', 'w_v', 'w_o', 'w_lq', 'w_lk', 'w_lv', 'w_lo')}
    del _L0_attn_all

    def _L0_xattn_setup():
        import jax, jax.numpy as jnp
        import numpy as np
        DIM = 64
        HEADS = 8
        DIM_HEAD = 64
        HIDDEN = HEADS * DIM_HEAD
        SCALE = DIM_HEAD ** (-0.5)
        key = jax.random.key(seed)
        ks = jax.random.split(key, 9)
        b, n = (8, 512)
        std = 1.0 / np.sqrt(DIM)
        return {'q': jax.random.normal(ks[0], (b, DIM, n), jnp.float32), 'k': jax.random.normal(ks[1], (b, DIM, n), jnp.float32), 'v': jax.random.normal(ks[2], (b, DIM, n), jnp.float32), 'Wq': jax.random.normal(ks[3], (HIDDEN, DIM), jnp.float32) * std, 'Wk': jax.random.normal(ks[4], (HIDDEN, DIM), jnp.float32) * std, 'Wv': jax.random.normal(ks[5], (HIDDEN, DIM), jnp.float32) * std, 'Wo': jax.random.normal(ks[6], (DIM, HIDDEN), jnp.float32) * (1.0 / np.sqrt(HIDDEN)), 'bo': jax.random.normal(ks[7], (DIM,), jnp.float32) * 0.01, 'g': jnp.ones((1, DIM, 1), jnp.float32)}
    _L0_xattn_all = _L0_xattn_setup()
    _L0_xattn_in = {k: v for k, v in _L0_xattn_all.items() if k in ('Wq', 'Wk', 'Wv', 'Wo', 'bo', 'g')}
    del _L0_xattn_all

    def _L0_ffn_setup():
        import jax, jax.numpy as jnp
        import numpy as np
        BLK = 16
        FP8_MAX = 448.0
        GSCALE_DIV = 448.0 * 6.0
        SELECT = 128

        def _ste(x, q):
            return x + jax.lax.stop_gradient(q - x)

        def _fp8_block_qdq(v):
            lead, C = (v.shape[:-1], v.shape[-1])
            vb = v.reshape(*lead, C // BLK, BLK)
            s = jnp.maximum(jnp.max(jnp.abs(vb), axis=-1, keepdims=True) / FP8_MAX, 1e-08)
            q = (vb / s).astype(jnp.float8_e4m3fn).astype(jnp.float32) * s
            return _ste(vb, q).reshape(*lead, C)

        def _int4_block_qdq(w):
            out, C = w.shape
            wb = w.reshape(out, C // BLK, BLK)
            s = jnp.maximum(jnp.max(jnp.abs(wb), axis=-1, keepdims=True) / 7.0, 1e-08)
            q = jnp.round(jnp.clip(wb / s, -8.0, 7.0)) * s
            return _ste(wb, q).reshape(out, C)

        def _quant_act(x2d, reorder_index, select_num):
            g = jnp.maximum(jnp.max(jnp.abs(x2d)) / GSCALE_DIV, 1e-08)
            xr = (x2d / g)[:, reorder_index]
            n = xr.shape[1] - select_num
            normal = _fp8_block_qdq(xr[:, :n])
            outl = xr[:, n:]
            q1 = _fp8_block_qdq(outl)
            q2 = _fp8_block_qdq(outl - q1)
            A = jnp.concatenate([normal, q1, q2], axis=1)
            return (A, g)

        def _quant_w(w, reorder_index, select_num):
            wr = w[:, reorder_index]
            n = wr.shape[1] - select_num
            wq = jnp.concatenate([wr[:, :n], wr[:, n:], wr[:, n:]], axis=1)
            return _int4_block_qdq(wq)
        key = jax.random.key(seed)
        k0, k1, k2, k3 = jax.random.split(key, 4)
        B, L, H, I = (2, 256, 512, 1376)
        return {'x': jax.random.normal(k0, (B, L, H), dtype=jnp.float32), 'w_gate': jax.random.normal(k1, (I, H), dtype=jnp.float32) * 0.02, 'w_up': jax.random.normal(k2, (I, H), dtype=jnp.float32) * 0.02, 'w_down': jax.random.normal(k3, (H, I), dtype=jnp.float32) * 0.02, 'ri_in': jnp.arange(H, dtype=jnp.int32), 'ri_mid': jnp.arange(I, dtype=jnp.int32)}
    _L0_ffn_all = _L0_ffn_setup()
    _L0_ffn_in = {k: v for k, v in _L0_ffn_all.items() if k in ('w_gate', 'w_up', 'w_down', 'ri_in', 'ri_mid')}
    del _L0_ffn_all
    return {'x': x, 'ctx_4096': ctx_4096, 'L0_attn_w_q': _L0_attn_in['w_q'], 'L0_attn_w_k': _L0_attn_in['w_k'], 'L0_attn_w_v': _L0_attn_in['w_v'], 'L0_attn_w_o': _L0_attn_in['w_o'], 'L0_attn_w_lq': _L0_attn_in['w_lq'], 'L0_attn_w_lk': _L0_attn_in['w_lk'], 'L0_attn_w_lv': _L0_attn_in['w_lv'], 'L0_attn_w_lo': _L0_attn_in['w_lo'], 'L0_xattn_Wq': _L0_xattn_in['Wq'], 'L0_xattn_Wk': _L0_xattn_in['Wk'], 'L0_xattn_Wv': _L0_xattn_in['Wv'], 'L0_xattn_Wo': _L0_xattn_in['Wo'], 'L0_xattn_bo': _L0_xattn_in['bo'], 'L0_xattn_g': _L0_xattn_in['g'], 'L0_ffn_w_gate': _L0_ffn_in['w_gate'], 'L0_ffn_w_up': _L0_ffn_in['w_up'], 'L0_ffn_w_down': _L0_ffn_in['w_down'], 'L0_ffn_ri_in': _L0_ffn_in['ri_in'], 'L0_ffn_ri_mid': _L0_ffn_in['ri_mid']}

def reference(x, ctx_4096, L0_attn_w_q, L0_attn_w_k, L0_attn_w_v, L0_attn_w_o, L0_attn_w_lq, L0_attn_w_lk, L0_attn_w_lv, L0_attn_w_lo, L0_xattn_Wq, L0_xattn_Wk, L0_xattn_Wv, L0_xattn_Wo, L0_xattn_bo, L0_xattn_g, L0_ffn_w_gate, L0_ffn_w_up, L0_ffn_w_down, L0_ffn_ri_in, L0_ffn_ri_mid):
    import jax
    import jax.numpy as jnp

    def _L0_attn_ref(hidden_states, w_q, w_k, w_v, w_o, w_lq, w_lk, w_lv, w_lo):
        import jax, jax.numpy as jnp
        import numpy as np
        B, S, D = (2, 128, 512)
        H, KVH, HD = (32, 8, 128)
        GROUPS = H // KVH
        LAT, LH = (128, 32)
        THETA = 10000.0
        SCALE = 1.0 / float(np.sqrt(HD))

        def _rope_cos_sin(seq_len, head_dim, theta):
            inv_freq = 1.0 / theta ** (jnp.arange(0, head_dim, 2, dtype=jnp.float32) / head_dim)
            t = jnp.arange(seq_len, dtype=jnp.float32)
            freqs = jnp.outer(t, inv_freq)
            emb = jnp.concatenate([freqs, freqs], axis=-1)
            return (jnp.cos(emb), jnp.sin(emb))

        def _rotate_half(x):
            h = x.shape[-1] // 2
            return jnp.concatenate([-x[..., h:], x[..., :h]], axis=-1)

        def _apply_rope(x, cos, sin):
            return x * cos[None, None] + _rotate_half(x) * sin[None, None]

        def _causal_attn(q, k, v, scale):
            s = jnp.einsum('bhqd,bhkd->bhqk', q, k) * scale
            mask = jnp.tril(jnp.ones((q.shape[2], k.shape[2]), dtype=bool))
            s = jnp.where(mask[None, None], s, jnp.finfo(s.dtype).min)
            p = jax.nn.softmax(s, axis=-1)
            return jnp.einsum('bhqk,bhkd->bhqd', p, v)
        x = hidden_states
        bsz, q_len, _ = x.shape
        q = (x @ w_q).reshape(bsz, q_len, H, HD).transpose(0, 2, 1, 3)
        k = (x @ w_k).reshape(bsz, q_len, KVH, HD).transpose(0, 2, 1, 3)
        v = (x @ w_v).reshape(bsz, q_len, KVH, HD).transpose(0, 2, 1, 3)
        lq = x @ w_lq
        lk = (lq @ w_lk).reshape(bsz, q_len, LH, HD).transpose(0, 2, 1, 3)
        lv = (x @ w_lv).reshape(bsz, q_len, LH, HD).transpose(0, 2, 1, 3)
        cos, sin = _rope_cos_sin(q_len, HD, THETA)
        q = _apply_rope(q, cos, sin)
        k = _apply_rope(k, cos, sin)
        lk = _apply_rope(lk, cos, sin)
        k = jnp.repeat(k, GROUPS, axis=1)
        v = jnp.repeat(v, GROUPS, axis=1)
        attn = _causal_attn(q, k, v, SCALE)
        lat = _causal_attn(q, lk, lv, SCALE)
        attn = attn.transpose(0, 2, 1, 3).reshape(bsz, q_len, H * HD)
        lat = lat.transpose(0, 2, 1, 3).reshape(bsz, q_len, LH * HD)
        return attn @ w_o + lat @ w_lo

    def _L0_xattn_ref(q, k, v, Wq, Wk, Wv, Wo, bo, g):
        import jax, jax.numpy as jnp
        import numpy as np
        DIM = 64
        HEADS = 8
        DIM_HEAD = 64
        HIDDEN = HEADS * DIM_HEAD
        SCALE = DIM_HEAD ** (-0.5)
        b = q.shape[0]
        qh = jnp.einsum('bcn,oc->bon', q, Wq).reshape(b, HEADS, DIM_HEAD, -1)
        kh = jnp.einsum('bcn,oc->bon', k, Wk).reshape(b, HEADS, DIM_HEAD, -1)
        vh = jnp.einsum('bcn,oc->bon', v, Wv).reshape(b, HEADS, DIM_HEAD, -1)
        qh = jax.nn.softmax(qh, axis=-2) * SCALE
        kh = jax.nn.softmax(kh, axis=-1)
        context = jnp.einsum('bhdn,bhen->bhde', kh, vh)
        out = jnp.einsum('bhde,bhdn->bhen', context, qh)
        out = out.reshape(b, HIDDEN, -1)
        out = jnp.einsum('bcn,oc->bon', out, Wo) + bo[None, :, None]
        norm = jnp.maximum(jnp.sqrt(jnp.sum(out * out, axis=1, keepdims=True)), 1e-12)
        return out / norm * g * np.sqrt(DIM)

    def _L0_ffn_ref(x, w_gate, w_up, w_down, ri_in, ri_mid):
        import jax, jax.numpy as jnp
        import numpy as np
        BLK = 16
        FP8_MAX = 448.0
        GSCALE_DIV = 448.0 * 6.0
        SELECT = 128

        def _ste(x, q):
            return x + jax.lax.stop_gradient(q - x)

        def _fp8_block_qdq(v):
            lead, C = (v.shape[:-1], v.shape[-1])
            vb = v.reshape(*lead, C // BLK, BLK)
            s = jnp.maximum(jnp.max(jnp.abs(vb), axis=-1, keepdims=True) / FP8_MAX, 1e-08)
            q = (vb / s).astype(jnp.float8_e4m3fn).astype(jnp.float32) * s
            return _ste(vb, q).reshape(*lead, C)

        def _int4_block_qdq(w):
            out, C = w.shape
            wb = w.reshape(out, C // BLK, BLK)
            s = jnp.maximum(jnp.max(jnp.abs(wb), axis=-1, keepdims=True) / 7.0, 1e-08)
            q = jnp.round(jnp.clip(wb / s, -8.0, 7.0)) * s
            return _ste(wb, q).reshape(out, C)

        def _quant_act(x2d, reorder_index, select_num):
            g = jnp.maximum(jnp.max(jnp.abs(x2d)) / GSCALE_DIV, 1e-08)
            xr = (x2d / g)[:, reorder_index]
            n = xr.shape[1] - select_num
            normal = _fp8_block_qdq(xr[:, :n])
            outl = xr[:, n:]
            q1 = _fp8_block_qdq(outl)
            q2 = _fp8_block_qdq(outl - q1)
            A = jnp.concatenate([normal, q1, q2], axis=1)
            return (A, g)

        def _quant_w(w, reorder_index, select_num):
            wr = w[:, reorder_index]
            n = wr.shape[1] - select_num
            wq = jnp.concatenate([wr[:, :n], wr[:, n:], wr[:, n:]], axis=1)
            return _int4_block_qdq(wq)
        B, L, H = x.shape
        x2 = x.reshape(B * L, H)
        A, g = _quant_act(x2, ri_in, SELECT)
        Wg = _quant_w(w_gate, ri_in, SELECT)
        Wu = _quant_w(w_up, ri_in, SELECT)
        gate = A @ Wg.T * g
        up = A @ Wu.T * g
        h = jax.nn.silu(gate) * up
        Am, gm = _quant_act(h, ri_mid, SELECT)
        Wd = _quant_w(w_down, ri_mid, SELECT)
        y = Am @ Wd.T * gm
        return y.reshape(B, L, -1)
    x = x + _L0_attn_ref(_layernorm(x, axis=-1), L0_attn_w_q, L0_attn_w_k, L0_attn_w_v, L0_attn_w_o, L0_attn_w_lq, L0_attn_w_lk, L0_attn_w_lv, L0_attn_w_lo)
    x = x + _L0_xattn_ref(_layernorm(x, axis=-1), ctx_4096, ctx_4096, L0_xattn_Wq, L0_xattn_Wk, L0_xattn_Wv, L0_xattn_Wo, L0_xattn_bo, L0_xattn_g)
    x = x + _L0_ffn_ref(_layernorm(x, axis=-1), L0_ffn_w_gate, L0_ffn_w_up, L0_ffn_w_down, L0_ffn_ri_in, L0_ffn_ri_mid)
    return x

_drawn_inputs = setup_inputs


def setup_inputs(seed=0):
    import zlib

    import numpy as np

    out = dict(_drawn_inputs(seed))
    spreads = {'L0_xattn_g': (1.0, 0.2)}
    factors = {'L0_attn_w_k': 2.672, 'L0_attn_w_lq': 8.0, 'L0_attn_w_lk': 8.0}
    for name, (base, spread) in spreads.items():
        noise = np.random.default_rng([zlib.crc32(name.encode()), seed]).standard_normal(out[name].shape)
        drawn = base * np.exp(spread * noise) if base else spread * noise
        out[name] = jnp.asarray(drawn.astype(out[name].dtype))
    for name, factor in factors.items():
        out[name] = (out[name] * factor).astype(out[name].dtype)
    return out
```

```python
from contextlib import ExitStack

import numpy as np

import concourse.bass as bass
from concourse import mybir

P = 128
BATCH, SEQ, DM = 16, 64, 512
TOK = BATCH * SEQ
NT = TOK // P
KT = DM // P
HEADS, KVH, HD = 32, 8, 128
GROUP = HEADS // KVH
HB = 2 * GROUP
ITERS = HEADS // HB
SCALE = 1.0 / float(np.sqrt(HD))
WS = 64.0
EPS = 1e-5
HALF = 512

ALU = mybir.AluOpType
ACT = mybir.ActivationFunctionType
AX = mybir.AxisListType
F32 = mybir.dt.float32
F16 = mybir.dt.float16
I32 = mybir.dt.int32

C_ID, C_COS, C_SIN, C_MASK, C_ONES, C_PICK, C_IOTA, C_END = 0, 128, 192, 256, 320, 352, 480, 484
C_COMMON = C_ONES


def shape_constants():
    c = np.zeros((P, C_END), np.float32)
    c[:, C_ID:C_ID + P] = np.eye(P, dtype=np.float32)
    inv = (np.float32(1.0) / np.float32(10000.0) ** (np.arange(0, HD, 2, dtype=np.float32) / np.float32(HD)))
    freq = np.outer(np.arange(SEQ, dtype=np.float32), inv.astype(np.float32)).astype(np.float32)
    cos, sin = np.cos(freq).T, np.sin(freq).T
    c[0:64, C_COS:C_COS + SEQ] = cos / WS
    c[64:128, C_COS:C_COS + SEQ] = cos / WS
    c[0:64, C_SIN:C_SIN + SEQ] = sin / WS
    c[64:128, C_SIN:C_SIN + SEQ] = -sin / WS
    q = np.arange(P) % SEQ
    c[:, C_MASK:C_MASK + SEQ] = np.where(np.arange(SEQ)[None, :] <= q[:, None], 0.0, -1e30)
    p = np.arange(P)
    c[:, C_ONES:C_ONES + 32] = (p[:, None] // 64 == np.arange(32)[None, :] % 2)
    c[:, C_PICK:C_PICK + P] = (p[:, None] % 32 == p[None, :] // 64)
    c[:, C_IOTA:C_IOTA + KT] = p[:, None] + P * np.arange(KT)[None, :]
    return c


class Chain:

    def __init__(self, engine, sem):
        self.engine, self.sem, self.base, self.n = engine, sem, 0, 0

    def link(self, instruction):
        self.mark(instruction)
        self.wait()

    def mark(self, instruction):
        self.n += 1
        instruction.then_inc(self.sem, 1)

    def wait(self):
        self.engine.wait_ge(self.sem, self.base + self.n)

    def enter(self, start, it, per_body):
        self.base, self.n = it * per_body + start, 0


def layernorm_stats(dve, chain, nc, X, st, mv, rs):
    for t in range(NT):
        chain.link(nc.vector.bn_stats(st[:, t, :], X[:, t, :]))
    for t in range(NT):
        chain.mark(nc.vector.bn_aggr(mv[:, t, :], st[:, t, :]))
    chain.wait()
    return nc.vector.tensor_scalar(rs[:, :], mv[:, :, 1], EPS, None, ALU.add)


def attention_phase(nc, X, const, const_in, x_in, w_q, w_k, w_v, w_o, w_lq, w_lk, w_lv, w_lo, sem):
    with ExitStack() as ctx:
        def sb(name, shape, dt=F32):
            return ctx.enter_context(nc.sbuf_tensor(name, shape, dt))

        def ps(name, shape, dt=F32):
            return ctx.enter_context(nc.psum_tensor(name, shape, dt))

        ident = const[:, C_ID:C_ID + P]
        cos8 = const[:, C_COS:C_COS + SEQ].unsqueeze(1).to_broadcast([P, BATCH, SEQ])
        mask = const[:, C_MASK:C_MASK + SEQ].unsqueeze(1).to_broadcast([P, 2 * NT, SEQ])

        def sin_of(p0):
            return const[p0:p0 + 64, C_SIN:C_SIN + SEQ].unsqueeze(1).to_broadcast([64, BATCH, SEQ])

        XT = sb("XT", [P, 2, KT, TOK], F16)
        LQ = sb("LQ", [P, 2, TOK], F16)
        st = sb("st", [P, NT, 6])
        mv = sb("mv", [P, NT, 2])
        rs = sb("rs", [P, NT])
        NW = 2 * KT + 1
        w_raw = sb("w_raw", [P, 2, NW, P])
        w16 = sb("w16", [P, 2, 2, NW, P], F16)
        kv_raw = sb("kv_raw", [P, 2 * KT, P])
        kv16 = sb("kv16", [P, 2, 2 * KT, P], F16)
        o_raw = sb("o_raw", [P, GROUP, DM])
        o16 = sb("o16", [P, 2, 2 * GROUP, DM], F16)
        q_raw = sb("q_raw", [P, TOK])
        lk_raw = sb("lk_raw", [P, TOK])
        k_raw = sb("k_raw", [P, TOK])
        rt = sb("rt", [P, 2, TOK])
        gt = sb("gt", [P, 2, TOK])
        qT = sb("qT", [P, 2, TOK])
        lkT = sb("lkT", [P, 2, TOK])
        kT = sb("kT", [P, 2, TOK])
        v = sb("v", [P, 2, NT, HD])
        lv = sb("lv", [P, 2, NT, HD])
        s_sb = sb("s_sb", [P, 2 * NT, SEQ])
        rmax = sb("rmax", [P, 2 * NT])
        rsum = sb("rsum", [P, 2 * NT])
        pbd = sb("pbd", [P, 2 * NT, P])
        pT = sb("pT", [P, 2 * NT, P])
        xn = s_sb[:, :, :].rearrange("p a b -> p (a b)").rearrange("p (a b) -> p a b", a=2)
        wlq_raw = pT[:, 0:4, :]
        wlq = pT[:, 4:8, :].bitcast(F16).rearrange("p a (b c) -> p (a b) c", c=P).rearrange("p (a b) c -> p a b c", a=2)
        aT = sb("aT", [P, 2, 2 * GROUP, TOK], F16)

        PJ = [ps(f"PJ{i}", [P, HALF]) for i in range(2)]
        S = ps("S", [P, 2 * NT, SEQ])
        TB = [ps(f"TB{i}", [P, 4, P]) for i in range(2)]
        OB = [ps(f"OB{i}", [P, HALF]) for i in range(2)]

        x_loaded, const_loaded, wlq_loaded = sem("x_loaded"), sem("const_loaded"), sem("wlq_loaded")
        w_loaded = [sem("w_loaded0"), sem("w_loaded1")]
        kv_loaded, o_loaded = sem("kv_loaded"), sem("o_loaded")
        dve_own, pool_own, act_own = sem("dve_own"), sem("pool_own"), sem("act_own")
        var_ready, root_ready, xn_ready = sem("var_ready"), sem("root_ready"), sem("xn_ready")
        xt_psum, xt_hi, xt_lo = sem("xt_psum"), sem("xt_hi"), sem("xt_lo")
        wlq_hi, wlq_lo, lq_psum, lq_hi, lq_lo = (sem(n) for n in ("wlq_hi", "wlq_lo", "lq_psum", "lq_hi", "lq_lo"))
        wt_hi, wt_lo, kv_hi, kv_lo, o_hi, o_lo = (sem(n) for n in ("wt_hi", "wt_lo", "kv_hi", "kv_lo", "o_hi", "o_lo"))
        pj_full, pj_free = sem("pj_full"), sem("pj_free")
        q_evac, lk_evac, k_evac = sem("q_evac"), sem("lk_evac"), sem("k_evac")
        q_roped, lk_roped, k_roped = sem("q_roped"), sem("lk_roped"), sem("k_roped")
        s_full, shifted, exp_done, pbd_ready = sem("s_full"), sem("shifted"), sem("exp_done"), sem("pbd_ready")
        t_full, t_free = sem("t_full"), sem("t_free")
        b_full, b_free, a_hi = sem("b_full"), sem("b_free"), sem("a_hi")
        pbd_zeroed = sem("pbd_zeroed")

        def pj_base(h):
            return 6 * h + (4 if h > 3 else 0)

        PJ_BODY, T_BODY, B_BODY = 6 * HB + 8, 4 * HB, 4 * HB + 2 * NT
        PJ_PRO = 10

        def b_base(h):
            return 4 * h + NT * (h // 4)

        wq_v = w_q.rearrange("(k p) n -> p k n", p=P)
        wlv_v = w_lv.rearrange("(k p) n -> p k n", p=P)
        wk_v = w_k.rearrange("(k p) n -> p k n", p=P)
        wv_v = w_v.rearrange("(k p) n -> p k n", p=P)
        wo_v = w_o.rearrange("(h p) n -> p h n", p=P)
        wlo_v = w_lo.rearrange("(h p) n -> p h n", p=P)

        block = ctx.enter_context(nc.Block())

        @block.sync
        def _(sp):
            def load_head(par, n):
                sp.dma_start(w_raw[:, par, 0:KT, :], wq_v[:, :, bass.ts(n, P)]).then_inc(w_loaded[par], 16)
                sp.dma_start(w_raw[:, par, KT, :], w_lk[:, bass.ts(n, P)]).then_inc(w_loaded[par], 16)
                sp.dma_start(w_raw[:, par, KT + 1:NW, :], wlv_v[:, :, bass.ts(n, P)]).then_inc(w_loaded[par], 16)

            def load_kv(g):
                sp.dma_start(kv_raw[:, 0:KT, :], wk_v[:, :, bass.ts(g, P)]).then_inc(kv_loaded, 16)
                sp.dma_start(kv_raw[:, KT:, :], wv_v[:, :, bass.ts(g, P)]).then_inc(kv_loaded, 16)

            def load_o(g, part):
                src = (wo_v, wlo_v)[part]
                sp.dma_start(o_raw[:, :, :], src[:, bass.ts(g, GROUP), :]).then_inc(o_loaded, 16)

            sp.dma_start(X[:, :, :], x_in.rearrange("(t p) n -> p t n", p=P)).then_inc(x_loaded, 16)
            sp.dma_start(wlq_raw[:, :, :], w_lq.rearrange("(k p) n -> p k n", p=P)).then_inc(wlq_loaded, 16)
            load_kv(0)
            load_head(0, 0)
            load_head(1, 1)
            load_o(0, 0)

            def body(it, last):
                for h in range(HB):
                    if not (last and h >= HB - 2):
                        sp.wait_ge(wt_hi, it * HB + h + 1)
                        sp.wait_ge(wt_lo, it * HB + h + 1)
                        load_head(h % 2, it * HB + h + 2)
                    g = h // 4
                    if h % 4 == 0 and not (last and g == 1):
                        sp.wait_ge(kv_hi, it * 2 + g + 1)
                        sp.wait_ge(kv_lo, it * 2 + g + 1)
                        load_kv(it * 2 + g + 1)
                    if h % 4 == 1 or (h % 4 == 2 and not (last and g == 1)):
                        sp.wait_ge(o_hi, it * 4 + 2 * g + h % 4)
                        sp.wait_ge(o_lo, it * 4 + 2 * g + h % 4)
                        load_o(it * 2 + g + h % 4 - 1, h % 4 % 2)

            with sp.Fori(0, ITERS - 1) as it:
                body(it, False)
            body(ITERS - 1, True)

        @block.scalar
        def _(act):
            def hi_of(dst, src, scale=WS):
                return nc.scalar.activation(dst, src, ACT.Copy, scale=scale)

            def split_head(par, need, m):
                act.wait_ge(w_loaded[par], need)
                hi_of(w16[:, par, 0], w_raw[:, par]).then_inc(wt_hi, 1)

            act.dma_start(const[:, :], const_in[:, 0:C_COMMON]).then_inc(const_loaded, 16)
            act.sem_inc(pj_free, 2)
            act.sem_inc(t_free, 2)
            act.wait_ge(wlq_loaded, 16)
            hi_of(wlq[:, 0], wlq_raw[:, :]).then_inc(wlq_hi, 1)
            act.wait_ge(kv_loaded, 32)
            hi_of(kv16[:, 0], kv_raw[:, :]).then_inc(kv_hi, 1)
            split_head(0, 48, 0)
            split_head(1, 48, 1)
            act.wait_ge(var_ready, 1)
            nc.scalar.activation(rs[:, :], rs[:, :], ACT.Sqrt).then_inc(root_ready, 1)
            for t in range(NT):
                act.wait_ge(xt_psum, t + 1)
                hi_of(XT[:, 0, :, t * P:(t + 1) * P], TB[t % 2][:, :, :], 1.0).then_inc(xt_hi, 1)
            for c in range(2):
                act.wait_ge(lq_psum, c + 1)
                hi_of(LQ[:, 0, c * HALF:(c + 1) * HALF], OB[c][:, :], 1 / WS).then_inc(lq_hi, 1)

            def take(base, k, dst, scale, extra=None):
                act.wait_ge(pj_full, base + k + 1)
                src = PJ[k % 2][:, :]
                if len(dst.shape) == 3:
                    src = src.rearrange("p (t d) -> p t d", d=HD)
                ins = hi_of(dst, src, scale)
                ins.then_inc(pj_free, 1)
                return ins

            def kv_steps(base, k, gp, roped_need):
                if roped_need is not None:
                    act.wait_ge(k_roped, roped_need)
                take(base, k, k_raw[:, 0:HALF], 1.0)
                take(base, k + 1, k_raw[:, HALF:], 1.0)
                take(base, k + 2, v[:, gp, 0:4, :], 1 / WS)
                take(base, k + 3, v[:, gp, 4:8, :], 1 / WS)

            kv_steps(0, 0, 0, None)
            take(0, 4, q_raw[:, 0:HALF], 1.0)
            take(0, 5, q_raw[:, HALF:], 1.0)
            take(0, 6, lk_raw[:, 0:HALF], 1.0)
            take(0, 7, lk_raw[:, HALF:], 1.0)
            take(0, 8, lv[:, 0, 0:4, :], 1 / WS)
            take(0, 9, lv[:, 0, 4:8, :], 1 / WS)

            def body(it, last):
                for h in range(HB):
                    n = it * HB + h
                    more = not (last and h == HB - 1)
                    base = it * PJ_BODY + PJ_PRO
                    k = pj_base(h)
                    if more and h % 4 == 3:
                        kv_steps(base, k, (h // 4 + 1) % 2, it * 2 + h // 4 + 1)
                        k += 4
                    if more:
                        act.wait_ge(q_roped, n + 1)
                        take(base, k, q_raw[:, 0:HALF], 1.0)
                    act.wait_ge(shifted, n + 1)
                    nc.scalar.activation(s_sb[:, :, :], s_sb[:, :, :], ACT.Exp, scale=SCALE).then_inc(exp_done, 1)
                    if more:
                        take(base, k + 1, q_raw[:, HALF:], 1.0)
                        act.wait_ge(lk_roped, n + 1)
                        take(base, k + 2, lk_raw[:, 0:HALF], 1.0)
                        take(base, k + 3, lk_raw[:, HALF:], 1.0)
                        take(base, k + 4, lv[:, (h + 1) % 2, 0:4, :], 1 / WS)
                    if not (last and h >= HB - 2):
                        act.wait_ge(w_loaded[h % 2], (it * (HB // 2) + h // 2 + 2) * 48)
                        hi_of(w16[:, h % 2, 0], w_raw[:, h % 2]).then_inc(wt_hi, 1)
                    if h % 4 == 1:
                        g = h // 4
                        if not (last and g == 1):
                            act.wait_ge(kv_loaded, (it * 2 + g + 2) * 32)
                            hi_of(kv16[:, 0], kv_raw[:, :]).then_inc(kv_hi, 1)
                    if h % 4 in (1, 2):
                        part = h % 4 - 1
                        act.wait_ge(o_loaded, (it * 4 + 2 * (h // 4) + part + 1) * 16)
                        hi_of(o16[:, 0, part * GROUP:(part + 1) * GROUP], o_raw[:, :]).then_inc(o_hi, 1)
                    for j in range(4):
                        act.wait_ge(t_full, it * T_BODY + 4 * h + j + 1)
                        nc.scalar.activation(pT[:, 4 * j:4 * j + 4, :], TB[j % 2][:, :, :], ACT.Copy)\
                            .then_inc(t_free, 1)
                    for j in range(4):
                        if j == 2 and more:
                            take(base, k + 5, lv[:, (h + 1) % 2, 4:8, :], 1 / WS)
                        act.wait_ge(b_full, it * B_BODY + b_base(h) + j + 1)
                        kt = (h % 4) + GROUP * (j // 2)
                        hi_of(aT[:, 0, kt, (j % 2) * HALF:(j % 2 + 1) * HALF], OB[j % 2][:, :], 1.0)\
                            .then_inc(a_hi, 1)

            with act.Fori(0, ITERS - 1) as it:
                body(it, False)
            body(ITERS - 1, True)

        @block.gpsimd
        def _(pool):
            own = Chain(pool, pool_own)
            nc.gpsimd.memset(pbd[:, :, :], 0.0).then_inc(pbd_zeroed, 1)
            pool.wait_ge(const_loaded, 16)

            def rope(dst, src, ready):
                s3 = src.rearrange("p (b t) -> p b t", t=SEQ)
                g3 = [gt[:, i, :].rearrange("p (b t) -> p b t", t=SEQ) for i in range(2)]
                own.link(nc.gpsimd.tensor_tensor(g3[0], s3, cos8, ALU.mult))
                own.link(nc.gpsimd.tensor_tensor(g3[1][0:64], s3[64:128], sin_of(64), ALU.mult))
                own.link(nc.gpsimd.tensor_tensor(g3[1][64:128], s3[0:64], sin_of(0), ALU.mult))
                nc.gpsimd.tensor_tensor(dst, gt[:, 0, :], gt[:, 1, :], ALU.add).then_inc(ready, 1)

            pool.wait_ge(pj_free, 2 + 8)
            rope(lkT[:, 0, :], lk_raw[:, :], lk_roped)

            def body(it, last):
                own.enter(3, it, 3 * HB)
                for h in range(HB):
                    if last and h == HB - 1:
                        break
                    k = pj_base(h) + (4 if h % 4 == 3 else 0) + 4
                    pool.wait_ge(pj_free, it * PJ_BODY + PJ_PRO + 2 + k)
                    pool.wait_ge(lk_roped, it * HB + h + 1)
                    pool.wait_ge(s_full, it * HB + h + 1)
                    rope(lkT[:, (h + 1) % 2, :], lk_raw[:, :], lk_roped)

            with pool.Fori(0, ITERS - 1) as it:
                body(it, False)
            body(ITERS - 1, True)

        @block.vector
        def _(dve):
            own = Chain(dve, dve_own)

            def lo_of(dst, src, hi, scale):
                return nc.vector.scalar_tensor_tensor(dst, src, scale, hi, ALU.mult, ALU.subtract)

            def rope(dst, src, ready):
                s3 = src.rearrange("p (b t) -> p b t", t=SEQ)
                g3 = [rt[:, i, :].rearrange("p (b t) -> p b t", t=SEQ) for i in range(2)]
                own.mark(nc.vector.tensor_tensor(g3[0], s3, cos8, ALU.mult))
                own.mark(nc.vector.tensor_tensor(g3[1][0:64], s3[64:128], sin_of(64), ALU.mult))
                own.mark(nc.vector.tensor_tensor(g3[1][64:128], s3[0:64], sin_of(0), ALU.mult))
                own.wait()
                ins = nc.vector.tensor_tensor(dst, rt[:, 0, :], rt[:, 1, :], ALU.add)
                ins.then_inc(ready, 1)

            dve.sem_inc(b_free, 2)
            dve.wait_ge(x_loaded, 16)
            ins = layernorm_stats(dve, own, nc, X, st, mv, rs)
            ins.then_inc(var_ready, 1)
            dve.wait_ge(root_ready, 1)
            own.link(nc.vector.reciprocal(rs[:, :], rs[:, :]))
            for t in range(NT):
                if t >= 2:
                    dve.wait_ge(xt_psum, t - 1)
                nc.vector.tensor_scalar(xn[:, t % 2, :], X[:, t, :], mv[:, t, 0:1], rs[:, t:t + 1],
                                        ALU.subtract, ALU.mult).then_inc(xn_ready, 1)
                if t >= 1:
                    dve.wait_ge(xt_hi, t)
                    lo_of(XT[:, 1, :, (t - 1) * P:t * P], TB[(t - 1) % 2][:, :, :],
                          XT[:, 0, :, (t - 1) * P:t * P], 1.0).then_inc(xt_lo, 1)
            dve.wait_ge(xt_hi, NT)
            lo_of(XT[:, 1, :, (NT - 1) * P:], TB[(NT - 1) % 2][:, :, :],
                  XT[:, 0, :, (NT - 1) * P:], 1.0).then_inc(xt_lo, 1)
            dve.wait_ge(wlq_hi, 1)
            lo_of(wlq[:, 1], wlq_raw[:, :], wlq[:, 0], WS).then_inc(wlq_lo, 1)
            dve.wait_ge(kv_hi, 1)
            lo_of(kv16[:, 1], kv_raw[:, :], kv16[:, 0], WS).then_inc(kv_lo, 1)
            for par in range(2):
                dve.wait_ge(wt_hi, par + 1)
                lo_of(w16[:, par, 1], w_raw[:, par], w16[:, par, 0], WS).then_inc(wt_lo, 1)
            for c in range(2):
                dve.wait_ge(lq_hi, c + 1)
                lo_of(LQ[:, 1, c * HALF:(c + 1) * HALF], OB[c][:, :],
                      LQ[:, 0, c * HALF:(c + 1) * HALF], 1 / WS).then_inc(lq_lo, 1)
            dve.wait_ge(const_loaded, 16)
            dve.wait_ge(pj_free, 2 + 2)
            rope(kT[:, 0, :], k_raw[:, :], k_roped)
            dve.wait_ge(k_roped, 1)
            dve.wait_ge(pj_free, 2 + 6)
            rope(qT[:, 0, :], q_raw[:, :], q_roped)
            dve.wait_ge(pbd_zeroed, 1)
            PRO = own.n
            D_BODY = 4 * HB + 3 * HB + 3 * 2

            def body(it, last):
                own.enter(PRO, it, D_BODY)
                for h in range(HB):
                    n = it * HB + h
                    more = not (last and h == HB - 1)
                    k = pj_base(h)
                    dve.wait_ge(s_full, n + 1)
                    own.link(nc.vector.tensor_tensor(s_sb[:, :, :], S[:, :, :], mask, ALU.add))
                    own.link(nc.vector.tensor_reduce(rmax[:, :], s_sb[:, :, :], AX.X, ALU.max))
                    nc.vector.tensor_tensor(s_sb[:, :, :], s_sb[:, :, :],
                                            rmax[:, :].unsqueeze(2).to_broadcast([P, 2 * NT, SEQ]),
                                            ALU.subtract).then_inc(shifted, 1)
                    dve.wait_ge(exp_done, n + 1)
                    own.link(nc.vector.tensor_reduce(rsum[:, :], s_sb[:, :, :], AX.X, ALU.add))
                    own.link(nc.vector.reciprocal(rsum[:, :], rsum[:, :]))
                    for s in range(2):
                        r = slice(64 * s, 64 * s + 64)
                        ins = nc.vector.tensor_tensor(pbd[r, :, 64 * s:64 * s + 64], s_sb[r, :, :],
                                                      rsum[r, :].unsqueeze(2).to_broadcast([64, 2 * NT, SEQ]),
                                                      ALU.mult)
                    ins.then_inc(pbd_ready, 1)
                    base = it * PJ_BODY + PJ_PRO + 2
                    if more and h % 4 == 3:
                        g = h // 4
                        dve.wait_ge(pj_free, base + k + 2)
                        dve.wait_ge(q_roped, n + 1)
                        rope(kT[:, (g + 1) % 2, :], k_raw[:, :], k_roped)
                        dve.wait_ge(k_roped, it * 2 + g + 2)
                        k += 4
                    if more:
                        dve.wait_ge(pj_free, base + k + 2)
                        dve.wait_ge(q_roped, n + 1)
                        rope(qT[:, (h + 1) % 2, :], q_raw[:, :], q_roped)
                    for j in range(4):
                        if j == 2:
                            if not (last and h >= HB - 2):
                                dve.wait_ge(wt_hi, n + 3)
                                lo_of(w16[:, h % 2, 1], w_raw[:, h % 2], w16[:, h % 2, 0], WS).then_inc(wt_lo, 1)
                            if h % 4 == 1:
                                g = h // 4
                                if not (last and g == 1):
                                    dve.wait_ge(kv_hi, it * 2 + g + 2)
                                    lo_of(kv16[:, 1], kv_raw[:, :], kv16[:, 0], WS).then_inc(kv_lo, 1)
                            if h % 4 in (1, 2):
                                c = slice((h % 4 - 1) * GROUP, (h % 4) * GROUP)
                                dve.wait_ge(o_hi, it * 4 + 2 * (h // 4) + h % 4)
                                lo_of(o16[:, 1, c], o_raw[:, :], o16[:, 0, c], WS).then_inc(o_lo, 1)
                        kt = (h % 4) + GROUP * (j // 2)
                        c = slice((j % 2) * HALF, (j % 2 + 1) * HALF)
                        dve.wait_ge(a_hi, n * 4 + j + 1)
                        lo_of(aT[:, 1, kt, c], OB[j % 2][:, :], aT[:, 0, kt, c], 1.0).then_inc(b_free, 1)
                    if h % 4 == 3:
                        for t in range(NT):
                            dve.wait_ge(b_full, it * B_BODY + b_base(h) + 4 + t + 1)
                            nc.vector.scalar_tensor_tensor(X[:, t, :], OB[t % 2][:, :], 1 / WS, X[:, t, :],
                                                           ALU.mult, ALU.add).then_inc(b_free, 1)
                if last:
                    assert own.n == D_BODY - 6, (own.n, D_BODY)
                else:
                    assert own.n == D_BODY, (own.n, D_BODY)

            with dve.Fori(0, ITERS - 1) as it:
                body(it, False)
            body(ITERS - 1, True)

        @block.tensor
        def _(pe):
            PASSES = ((0, 0), (0, 1), (1, 0))

            def project(out, pairs, done=None):
                n, last = 0, None
                for lhs, rhs in pairs:
                    for a, b in PASSES:
                        last = nc.tensor.matmul(out, lhs(a), rhs(b), start=(n == 0), stop=(n == 3 * len(pairs) - 1))
                        n += 1
                return last

            def head_w(par, i):
                return lambda a: w16[:, par, a, i, :]

            def kv_w(i):
                return lambda a: kv16[:, a, i, :]

            def xt(kt, c, w):
                return lambda b: XT[:, b, kt, c:c + w]

            pe.wait_ge(const_loaded, 16)
            for t in range(NT):
                pe.wait_ge(xn_ready, t + 1)
                if t >= 2:
                    pe.wait_ge(xt_lo, t - 1)
                for c in range(KT):
                    ins = nc.tensor.transpose(TB[t % 2][:, c, :], xn[:, t % 2, c * P:(c + 1) * P], ident)
                ins.then_inc(xt_psum, 1)
            pe.wait_ge(xt_lo, NT)
            pe.wait_ge(wlq_lo, 1)
            for c in range(2):
                project(OB[c][:, :], [(lambda a, i=i: wlq[:, a, i, :], xt(i, c * HALF, HALF)) for i in range(KT)])\
                    .then_inc(lq_psum, 1)

            def step(base, k, emit):
                pe.wait_ge(pj_free, base + k + 1)
                emit(PJ[k % 2]).then_inc(pj_full, 1)

            def feature_major(w, c):
                return lambda out: project(out[:, :], [(w(i), xt(i, c * HALF, HALF)) for i in range(KT)])

            def token_major(w, c):
                def emit(out):
                    for t in range(4):
                        ins = project(out[:, t * HD:(t + 1) * HD],
                                      [(xt(i, (4 * c + t) * P, P), w(i)) for i in range(KT)])
                    return ins
                return emit

            def kv_steps(base, k):
                step(base, k, feature_major(kv_w, 0))
                step(base, k + 1, feature_major(kv_w, 1))
                step(base, k + 2, token_major(lambda i: kv_w(KT + i), 0))
                step(base, k + 3, token_major(lambda i: kv_w(KT + i), 1))

            def q_lk_steps(base, k, par):
                step(base, k, feature_major(lambda i: head_w(par, i), 0))
                step(base, k + 1, feature_major(lambda i: head_w(par, i), 1))
                for c in range(2):
                    step(base, k + 2 + c, lambda out, c=c: project(
                        out[:, :], [(head_w(par, KT), lambda b: LQ[:, b, c * HALF:(c + 1) * HALF])]))

            def lv_step(base, k, par, c):
                step(base, k, token_major(lambda i: head_w(par, KT + 1 + i), c))

            pe.wait_ge(kv_lo, 1)
            kv_steps(0, 0)
            pe.wait_ge(wt_lo, 1)
            pe.wait_ge(lq_lo, 2)
            q_lk_steps(0, 4, 0)
            lv_step(0, 8, 0, 0)
            lv_step(0, 9, 0, 1)

            def body(it, last):
                for h in range(HB):
                    n = it * HB + h
                    g = h // 4
                    par = h % 2
                    more = not (last and h == HB - 1)
                    base = it * PJ_BODY + PJ_PRO
                    k = pj_base(h)
                    pe.wait_ge(k_roped, it * 2 + g + 1)
                    pe.wait_ge(q_roped, n + 1)
                    pe.wait_ge(lk_roped, n + 1)
                    for t in range(NT):
                        for kind, keys in enumerate((kT[:, g % 2, :], lkT[:, par, :])):
                            for s in range(2):
                                c = slice(t * P + 64 * s, t * P + 64 * s + 64)
                                ins = nc.tensor.matmul(S[64 * s:64 * s + 64, 2 * t + kind, :], qT[:, par, c],
                                                       keys[:, c], start=True, stop=True)
                    ins.then_inc(s_full, 1)
                    if more:
                        if h % 4 == 3:
                            pe.wait_ge(kv_lo, it * 2 + g + 2)
                            kv_steps(base, k)
                            k += 4
                        pe.wait_ge(wt_lo, n + 2)
                        q_lk_steps(base, k, 1 - par)
                        lv_step(base, k + 4, 1 - par, 0)
                    pe.wait_ge(pbd_ready, n + 1)
                    for j in range(4):
                        pe.wait_ge(t_free, it * T_BODY + 4 * h + j + 1)
                        for u in range(4):
                            ins = nc.tensor.transpose(TB[j % 2][:, u, :], pbd[:, 4 * j + u, :], ident)
                        ins.then_inc(t_full, 1)
                    for j in range(4):
                        if j == 2 and more:
                            lv_step(base, k + 5, 1 - par, 1)
                        pe.wait_ge(b_free, it * B_BODY + b_base(h) + j + 1)
                        if j < 2:
                            pe.wait_ge(t_free, it * T_BODY + 4 * h + 2 * j + 2 + 2)
                        for t in range(4 * (j % 2), 4 * (j % 2) + 4):
                            vals = v[:, g % 2, t, :] if j < 2 else lv[:, par, t, :]
                            ins = nc.tensor.matmul(OB[j % 2][:, (t % 4) * P:(t % 4 + 1) * P], vals,
                                                   pT[:, 2 * t + j // 2, :], start=True, stop=True)
                        ins.then_inc(b_full, 1)
                    if h % 4 == 3:
                        pe.wait_ge(o_lo, it * 4 + 2 * g + 2)
                        order = [0, GROUP, 1, GROUP + 1, 2, GROUP + 2, 3, GROUP + 3]
                        for t in range(NT):
                            pe.wait_ge(b_free, it * B_BODY + b_base(h) + 4 + max(t, 1) + 1)
                            project(OB[t % 2][:, :], [
                                (lambda a, i=i: aT[:, a, i, t * P:(t + 1) * P],
                                 lambda b, i=i: o16[:, b, i, :]) for i in order]).then_inc(b_full, 1)

            with pe.Fori(0, ITERS - 1) as it:
                body(it, False)
            body(ITERS - 1, True)


def cross_phase(nc, X, const, const_in, ctx_in, ctxT_in, WqT, WkT, Wv, WoT, bo, gain, sem):
    with ExitStack() as stack:
        def sb(name, shape, dt=F32):
            return stack.enter_context(nc.sbuf_tensor(name, shape, dt))

        def ps(name, shape, dt=F32):
            return stack.enter_context(nc.psum_tensor(name, shape, dt))

        CH = SEQ
        XH, XD = 8, 64
        HID = XH * XD
        JT = HID // P
        NN = DM // P
        ident = const[:, C_ID:C_ID + P]
        const_x = sb("x_const", [P, C_END - C_ONES])
        ones2 = const_x[:, 0:32]
        pick2 = const_x[:, 32:32 + P]

        st = sb("x_st", [P, NT, 6])
        mv = sb("x_mv", [P, NT, 2])
        rs = sb("x_rs", [P, NT])
        xn = sb("x_xn", [P, 2, DM])
        ctx_raw = sb("x_ctx", [P, NT, DM])
        XS = sb("x_XS", [P, BATCH, DM], F16)
        CS = sb("x_CS", [P, BATCH, DM], F16)
        w_raw = sb("x_wraw", [P, 2, HID])
        w16 = sb("x_w16", [P, 2, 2, HID], F16)
        wv_sb = sb("x_wv", [64, XH, CH])
        wo_sb = sb("x_wo", [64, XH, CH])
        U = sb("x_U_sb", [64, HID])
        bo_sb = sb("x_bias", [P, 1])
        g_raw = sb("x_graw", [P, 1])
        g8 = sb("x_g8", [P, 1])
        ct = sb("x_ct", [P, 2, NN, CH])
        kmax = sb("x_kmax", [P, 2, JT])
        knmax = sb("x_knmax", [P, 2, JT])
        ksum = sb("x_ksum", [P, 2, JT])
        krec = sb("x_krec", [P, JT])
        ek = sb("x_ek", [P, 2, JT, DM])
        eT = sb("x_eT", [P, NN, HID])
        qmax = sb("x_qmax", [P, NN, XH])
        qsum = sb("x_qsum", [P, 2, NN, XH])
        qs = sb("x_qs", [P, 2, NN, HID])
        qT = sb("x_qT", [P, JT, DM])
        GT = sb("x_GT", [64, HID])
        MT = sb("x_MT", [P, JT, CH])
        y = sb("x_y", [P, NT, DM])
        sq = sb("x_sq", [P, 2, DM])
        root = sb("x_root", [P, 2, DM])
        scaled = sb("x_scaled", [P, 2, DM])

        KB = [ps(f"x_KB{i}", [P, DM]) for i in range(2)]
        QB = [ps(f"x_QB{i}", [P, DM]) for i in range(2)]
        TB = [ps(f"x_TB{i}", [P, 4, P]) for i in range(2)]
        GB = ps("x_GB", [P, DM])
        YB = ps("x_YB", [P, DM])

        names = ("ctx_loaded wqk_loaded wvo_loaded small_loaded own var_ready root_ready xn_ready xs_hi xs_lo cs_hi cs_lo "
                 "wqk_hi wqk_lo u_full u_ready k_full k_free kneg_ready ek_ready q_full q_free q_exp "
                 "qrec_ready q_normed t_full t_free g_full gt_ready m_full mt_ready y_full y_free sq_ready "
                 "ss_full rec_ready bc_full bc_free ssroot_ready const2").split()
        s = {n: sem("x_" + n) for n in names}
        ct_loaded = [sem("x_ct_loaded0"), sem("x_ct_loaded1")]
        block = stack.enter_context(nc.Block())

        @block.sync
        def _(sp):
            sp.dma_start(w_raw[0:64, 0, :], WqT).then_inc(s["wqk_loaded"], 16)
            sp.dma_start(w_raw[64:128, 0, :], WqT).then_inc(s["wqk_loaded"], 16)
            sp.dma_start(w_raw[0:64, 1, :], WkT).then_inc(s["wqk_loaded"], 16)
            sp.dma_start(w_raw[64:128, 1, :], WkT).then_inc(s["wqk_loaded"], 16)
            sp.dma_start(ctx_raw[:, :, :], ctx_in.rearrange("(t p) n -> p t n", p=P)).then_inc(s["ctx_loaded"], 16)
            sp.dma_start(wv_sb[:, :, :], Wv.rearrange("(h e) c -> e h c", e=XD)).then_inc(s["wvo_loaded"], 16)
            sp.dma_start(wo_sb[:, :, :], WoT.rearrange("(h e) c -> e h c", e=XD)).then_inc(s["wvo_loaded"], 16)
            for r in range(2):
                sp.dma_start(bo_sb[64 * r:64 * r + 64, :], bo.rearrange("(c o) -> c o", o=1)).then_inc(s["small_loaded"], 16)
                sp.dma_start(g_raw[64 * r:64 * r + 64, :], gain.rearrange("a c o -> (a c) o")).then_inc(s["small_loaded"], 16)

            sp.dma_start(const_x[:, :], const_in[:, C_ONES:C_END]).then_inc(s["const2"], 16)

            def load_ct(par, b):
                src = ctxT_in[bass.ds(b, 1), :, :].rearrange("o (k p) c -> p (o k) c", p=P)
                sp.dma_start(ct[:, par], src).then_inc(ct_loaded[par], 16)

            load_ct(0, 0)
            load_ct(1, 1)
            with sp.Fori(0, NT - 1) as it:
                for par in range(2):
                    sp.wait_ge(s["g_full"], it * 2 + par + 1)
                    load_ct(par, it * 2 + par + 2)

        @block.scalar
        def _(act):
            def copy(dst, src, scale=1.0):
                return nc.scalar.activation(dst, src, ACT.Copy, scale=scale)

            act.sem_inc(s["k_free"], 2)
            act.sem_inc(s["t_free"], 2)
            act.wait_ge(s["wqk_loaded"], 64)
            copy(w16[:, :, 0, :], w_raw[:, :, :], WS).then_inc(s["wqk_hi"], 1)
            act.wait_ge(s["ctx_loaded"], 16)
            for r in range(2):
                c = slice(64 * r, 64 * r + 64)
                copy(CS[c, r:BATCH:2, :], ctx_raw[c, :, :]).then_inc(s["cs_hi"], 1)
            act.wait_ge(s["u_full"], 1)
            copy(U[:, :], GB[0:64, :]).then_inc(s["u_ready"], 1)
            act.wait_ge(s["var_ready"], 1)
            nc.scalar.activation(rs[:, :], rs[:, :], ACT.Sqrt).then_inc(s["root_ready"], 1)
            for t in range(NT):
                act.wait_ge(s["xn_ready"], t + 1)
                for r in range(2):
                    c = slice(64 * r, 64 * r + 64)
                    copy(XS[c, 2 * t + r, :], xn[c, t % 2, :]).then_inc(s["xs_hi"], 1)

            def k_exp(n, par, j):
                act.wait_ge(s["kneg_ready"], n * JT + j + 1)
                nc.scalar.activation(ek[:, par, j, :], KB[j % 2][:, :], ACT.Exp, scale=1 / WS,
                                     bias=knmax[:, par, j:j + 1],
                                     accum_out=ksum[:, par, j:j + 1]).then_inc(s["k_free"], 1)

            def q_exp(n, par, half):
                act.wait_ge(s["q_free"], n * NN + 2 * half + 2 + 2)
                c = slice(2 * half, 2 * half + 2)
                nc.scalar.activation(qs[:, par, c, :], qs[:, par, c, :], ACT.Exp, scale=1 / WS)\
                    .then_inc(s["q_exp"], 1)

            def transposed(n, k, dst):
                act.wait_ge(s["t_full"], n * 8 + k + 1)
                copy(dst, TB[k % 2][:, :, :]).then_inc(s["t_free"], 1)

            for j in range(JT):
                k_exp(0, 0, j)
            for half in range(2):
                q_exp(0, 0, half)

            def body(it, last):
                for par in range(2):
                    n = it * 2 + par
                    more = not (last and par == 1)
                    if more:
                        k_exp(n + 1, 1 - par, 0)
                        k_exp(n + 1, 1 - par, 1)
                    for k in range(4):
                        transposed(n, k, eT[:, k, :].rearrange("p (a b) -> p a b", b=P))
                    if more:
                        q_exp(n + 1, 1 - par, 0)
                        k_exp(n + 1, 1 - par, 2)
                        k_exp(n + 1, 1 - par, 3)
                    act.wait_ge(s["g_full"], n + 1)
                    copy(GT[:, :], GB[0:64, :]).then_inc(s["gt_ready"], 1)
                    for k in range(4):
                        transposed(n, 4 + k, qT[:, k, :].rearrange("p (a b) -> p a b", b=P))
                    if more:
                        q_exp(n + 1, 1 - par, 1)

            with act.Fori(0, NT - 1) as it:
                body(it, False)
            body(NT - 1, True)
            for t in range(NT):
                act.wait_ge(s["y_free"], NT + 1)
                if t >= 2:
                    act.wait_ge(s["ss_full"], t - 1)
                nc.scalar.activation(sq[:, t % 2, :], y[:, t, :], ACT.Square).then_inc(s["sq_ready"], 1)
            act.wait_ge(s["ss_full"], NT)
            for i, bank in enumerate((KB[0], QB[0])):
                nc.scalar.activation(root[:, i, :], bank[:, :], ACT.Sqrt).then_inc(s["ssroot_ready"], 1)

        @block.gpsimd
        def _(pool):
            def norm(n, par, half):
                pool.wait_ge(s["qrec_ready"], n * 2 + half + 1)
                c = slice(2 * half, 2 * half + 2)
                v3 = qs[:, par, c, :].rearrange("p a (h d) -> p (a h) d", d=XD)
                r3 = qsum[:, par, c, :].rearrange("p a h -> p (a h)").unsqueeze(2).to_broadcast([P, 2 * XH, XD])
                nc.gpsimd.tensor_tensor(v3, v3, r3, ALU.mult).then_inc(s["q_normed"], 1)

            norm(0, 0, 0)
            norm(0, 0, 1)

            def body(it, last):
                for par in range(2):
                    if not (last and par == 1):
                        norm(it * 2 + par + 1, 1 - par, 0)
                        norm(it * 2 + par + 1, 1 - par, 1)

            with pool.Fori(0, NT - 1) as it:
                body(it, False)
            body(NT - 1, True)

        @block.vector
        def _(dve):
            own = Chain(dve, s["own"])
            dve.sem_inc(s["q_free"], 2)
            dve.sem_inc(s["y_free"], 1)
            dve.sem_inc(s["mt_ready"], 1)
            dve.sem_inc(s["bc_free"], 2)
            ins = layernorm_stats(dve, own, nc, X, st, mv, rs)
            ins.then_inc(s["var_ready"], 1)
            dve.wait_ge(s["wqk_hi"], 1)
            nc.vector.scalar_tensor_tensor(w16[:, :, 1, :], w_raw[:, :, :], WS, w16[:, :, 0, :],
                                           ALU.mult, ALU.subtract).then_inc(s["wqk_lo"], 1)
            for r in range(2):
                a, b = slice(64 * r, 64 * r + 64), slice(64 - 64 * r, 128 - 64 * r)
                dve.wait_ge(s["cs_hi"], r + 1)
                nc.vector.tensor_tensor(CS[b, r:BATCH:2, :], ctx_raw[a, :, :], CS[a, r:BATCH:2, :],
                                        ALU.subtract).then_inc(s["cs_lo"], 1)
            dve.wait_ge(s["small_loaded"], 64)
            own.link(nc.vector.tensor_scalar(g8[:, :], g_raw[:, :], float(np.sqrt(CH)), None, ALU.mult))
            dve.wait_ge(s["root_ready"], 1)
            own.link(nc.vector.reciprocal(rs[:, :], rs[:, :]))
            for t in range(NT):
                if t >= 2:
                    dve.wait_ge(s["xs_lo"], 2 * (t - 1))
                    dve.wait_ge(s["xs_hi"], 2 * (t - 1))
                nc.vector.tensor_scalar(xn[:, t % 2, :], X[:, t, :], mv[:, t, 0:1], rs[:, t:t + 1],
                                        ALU.subtract, ALU.mult).then_inc(s["xn_ready"], 1)
                dve.wait_ge(s["xn_ready"], t + 1)
                for r in range(2):
                    a, b = slice(64 * r, 64 * r + 64), slice(64 - 64 * r, 128 - 64 * r)
                    dve.wait_ge(s["xs_hi"], 2 * t + r + 1)
                    nc.vector.tensor_tensor(XS[b, 2 * t + r, :], xn[a, t % 2, :], XS[a, 2 * t + r, :],
                                            ALU.subtract).then_inc(s["xs_lo"], 1)

            def k_max(n, par, j):
                dve.wait_ge(s["k_full"], n * JT + j + 1)
                own.link(nc.vector.tensor_reduce(kmax[:, par, j:j + 1], KB[j % 2][:, :], AX.X, ALU.max))
                nc.vector.tensor_scalar(knmax[:, par, j:j + 1], kmax[:, par, j:j + 1], -1 / WS, None,
                                        ALU.mult).then_inc(s["kneg_ready"], 1)

            def q_shift(n, par, i):
                dve.wait_ge(s["q_full"], n * NN + i + 1)
                v3 = QB[i % 2][:, :].rearrange("p (h d) -> p h d", d=XD)
                own.link(nc.vector.tensor_reduce(qmax[:, i, :], v3, AX.X, ALU.max))
                nc.vector.tensor_tensor(qs[:, par, i, :].rearrange("p (h d) -> p h d", d=XD), v3,
                                        qmax[:, i, :].unsqueeze(2).to_broadcast([P, XH, XD]),
                                        ALU.subtract).then_inc(s["q_free"], 1)

            def q_sum(n, par, half):
                dve.wait_ge(s["q_exp"], n * 2 + half + 1)
                c = slice(2 * half, 2 * half + 2)
                v3 = qs[:, par, c, :].rearrange("p a (h d) -> p (a h) d", d=XD)
                r2 = qsum[:, par, c, :].rearrange("p a h -> p (a h)")
                own.link(nc.vector.tensor_reduce(r2, v3, AX.X, ALU.add))
                nc.vector.reciprocal(r2, r2).then_inc(s["qrec_ready"], 1)

            for j in range(JT):
                k_max(0, 0, j)
            for i in range(NN):
                q_shift(0, 0, i)
                if i % 2:
                    q_sum(0, 0, i // 2)
            PRO = own.n
            BODY = 2 * (JT + NN + 2) + 2 * 2

            def body(it, last):
                own.enter(PRO, it, BODY)
                for par in range(2):
                    n = it * 2 + par
                    more = not (last and par == 1)
                    if more:
                        k_max(n + 1, 1 - par, 0)
                        k_max(n + 1, 1 - par, 1)
                        q_shift(n + 1, 1 - par, 0)
                        q_shift(n + 1, 1 - par, 1)
                        k_max(n + 1, 1 - par, 2)
                        k_max(n + 1, 1 - par, 3)
                        q_sum(n + 1, 1 - par, 0)
                        q_shift(n + 1, 1 - par, 2)
                        q_shift(n + 1, 1 - par, 3)
                    dve.wait_ge(s["k_free"], n * JT + JT + 2)
                    own.link(nc.vector.reciprocal(krec[:, :], ksum[:, par, :]))
                    own.link(nc.vector.tensor_scalar(krec[:, :], krec[:, :], XD ** -0.5, None, ALU.mult))
                    dve.wait_ge(s["m_full"], n + 1)
                    for r in range(2):
                        c = slice(64 * r, 64 * r + 64)
                        ins = nc.vector.tensor_tensor(
                            MT[c, :, :], GB[c, :].rearrange("p (j a o) -> p j a o", a=2, o=CH)[:, :, r, :],
                            krec[c, :].unsqueeze(2).to_broadcast([64, JT, CH]), ALU.mult)
                    ins.then_inc(s["mt_ready"], 1)
                    if more:
                        q_sum(n + 1, 1 - par, 1)
                dve.wait_ge(s["y_full"], it + 1)
                yt = y[:, bass.ds(it, 1), :].rearrange("p o n -> p (o n)")
                nc.vector.tensor_scalar(yt, YB[:, :], bo_sb[:, :], None, ALU.add).then_inc(s["y_free"], 1)
                if not last:
                    assert own.n == BODY, (own.n, BODY)

            with dve.Fori(0, NT - 1) as it:
                body(it, False)
            body(NT - 1, True)
            for i in range(2):
                dve.wait_ge(s["ssroot_ready"], i + 1)
                own.link(nc.vector.tensor_scalar(root[:, i, :], root[:, i, :], 1e-12, None, ALU.max))
                nc.vector.reciprocal(root[:, i, :], root[:, i, :]).then_inc(s["rec_ready"], 1)
            for t in range(NT):
                dve.wait_ge(s["bc_full"], t + 1)
                ins = nc.vector.scalar_tensor_tensor(scaled[:, t % 2, :], y[:, t, :], g8[:, :], TB_flat(TB[t % 2]),
                                                     ALU.mult, ALU.mult)
                ins.then_inc(s["bc_free"], 1)
                dve.wait_ge(s["bc_free"], t + 3)
                own.mark(nc.vector.tensor_tensor(X[:, t, :], X[:, t, :], scaled[:, t % 2, :], ALU.add))
            own.wait()

        @block.tensor
        def _(pe):
            pe.wait_ge(s["wvo_loaded"], 32)
            for h in range(XH):
                ins = nc.tensor.matmul(GB[0:64, h * CH:(h + 1) * CH], wv_sb[:, h, :], wo_sb[:, h, :],
                                       start=True, stop=True)
            ins.then_inc(s["u_full"], 1)
            pe.wait_ge(s["wqk_lo"], 1)
            pe.wait_ge(s["cs_lo"], 2)
            pe.wait_ge(s["u_ready"], 1)

            def k_proj(n, j):
                pe.wait_ge(s["k_free"], n * JT + j + 1)
                mov = CS[:, bass.ds(n, 1), :].rearrange("p o n -> p (o n)")
                for a in range(2):
                    ins = nc.tensor.matmul(KB[j % 2][:, :], w16[:, 1, a, j * P:(j + 1) * P], mov,
                                           start=(a == 0), stop=(a == 1))
                ins.then_inc(s["k_full"], 1)

            def q_proj(n, i):
                pe.wait_ge(s["q_free"], n * NN + i + 1)
                stat = XS[:, bass.ds(n, 1), i * P:(i + 1) * P].rearrange("p o n -> p (o n)")
                for a in range(2):
                    ins = nc.tensor.matmul(QB[i % 2][:, :], stat, w16[:, 0, a, :], start=(a == 0), stop=(a == 1))
                ins.then_inc(s["q_full"], 1)

            def k_transposes(n, par, k):
                pe.wait_ge(s["t_free"], n * 8 + k + 1)
                for j in range(JT):
                    ins = nc.tensor.transpose(TB[k % 2][:, j, :], ek[:, par, j, k * P:(k + 1) * P], ident)
                ins.then_inc(s["t_full"], 1)

            def q_transposes(n, par, k):
                pe.wait_ge(s["t_free"], n * 8 + 4 + k + 1)
                for i in range(NN):
                    ins = nc.tensor.transpose(TB[k % 2][:, i, :], qs[:, par, i, k * P:(k + 1) * P], ident)
                ins.then_inc(s["t_full"], 1)

            for j in range(JT):
                k_proj(0, j)
            pe.wait_ge(s["xs_lo"], 2 * NT)
            for i in range(NN):
                q_proj(0, i)

            def body(it, last):
                for par in range(2):
                    n = it * 2 + par
                    more = not (last and par == 1)
                    if more:
                        k_proj(n + 1, 0)
                        k_proj(n + 1, 1)
                        q_proj(n + 1, 0)
                        q_proj(n + 1, 1)
                    pe.wait_ge(s["k_free"], n * JT + JT + 2)
                    for k in range(NN):
                        k_transposes(n, par, k)
                    if more:
                        k_proj(n + 1, 2)
                        k_proj(n + 1, 3)
                        q_proj(n + 1, 2)
                        q_proj(n + 1, 3)
                    pe.wait_ge(s["t_free"], n * 8 + 4 + 2)
                    pe.wait_ge(ct_loaded[par], (it + 1) * 16)
                    pe.wait_ge(s["mt_ready"], n + 1)
                    for k in range(NN):
                        ins = nc.tensor.matmul(GB[0:64, :], ct[:, par, k, :], eT[:, k, :],
                                               start=(k == 0), stop=(k == NN - 1))
                    ins.then_inc(s["g_full"], 1)
                    pe.wait_ge(s["q_normed"], n * 2 + 2)
                    q_transposes(n, par, 0)
                    q_transposes(n, par, 1)
                    pe.wait_ge(s["gt_ready"], n + 1)
                    for j in range(JT):
                        ins = nc.tensor.matmul(GB[:, j * P:(j + 1) * P], GT[:, j * P:(j + 1) * P],
                                               U[:, j * P:(j + 1) * P], start=True, stop=True)
                    ins.then_inc(s["m_full"], 1)
                    q_transposes(n, par, 2)
                    q_transposes(n, par, 3)
                    pe.wait_ge(s["mt_ready"], n + 2)
                    pe.wait_ge(s["t_free"], n * 8 + 8 + 2)
                    if par == 0:
                        pe.wait_ge(s["y_free"], it + 1)
                    for j in range(JT):
                        ins = nc.tensor.matmul(YB[64 * par:64 * par + 64, :], MT[:, j, :], qT[:, j, :],
                                               start=(j == 0), stop=(j == JT - 1))
                ins.then_inc(s["y_full"], 1)

            with pe.Fori(0, NT - 1) as it:
                body(it, False)
            body(NT - 1, True)
            pe.wait_ge(s["const2"], 16)
            for t in range(NT):
                pe.wait_ge(s["sq_ready"], t + 1)
                r = 32 * (t % 4)
                nc.tensor.matmul((KB[0], QB[0])[t // 4][r:r + 32, :], ones2, sq[:, t % 2, :],
                                 start=True, stop=True).then_inc(s["ss_full"], 1)
            for t in range(NT):
                pe.wait_ge(s["rec_ready"], t // 4 + 1)
                pe.wait_ge(s["bc_free"], t + 1)
                r = 32 * (t % 4)
                nc.tensor.matmul(TB_flat(TB[t % 2]), pick2[r:r + 32, :], root[r:r + 32, t // 4, :],
                                 start=True, stop=True).then_inc(s["bc_full"], 1)


def TB_flat(t):
    return t[:, :, :].rearrange("p a b -> p (a b)")


FF = 1376
FT = -(-FF // P)
QB16 = 16
SPLIT = 128
FP8_MAX = 448.0
GSCALE = 448.0 * 6.0
TINY = 1e-8
ROUND = 1.5 * 2.0 ** 23
R4 = 1.5 * 2.0 ** 20
EXPONENT = 0x7F800000
RMAX = bass.bass_isa.ReduceOp.max


def rows_of(i):
    return min(P, FF - i * P)


def blocks(ap):
    return ap.rearrange("p (b e) -> p b e", e=QB16)


def spread(scales, parts, n):
    return scales.unsqueeze(2).to_broadcast([parts, n, QB16])


def weight_phase(nc, const, w16, wd16, wT, wdT, scratch, ri_in_cols, ri_mid_cols, ri_mid_last, sem):
    with ExitStack() as stack:
        def sb(name, shape, dt=F32):
            return stack.enter_context(nc.sbuf_tensor(name, shape, dt))

        def ps(name, shape, dt=F32):
            return stack.enter_context(nc.psum_tensor(name, shape, dt))

        ident = const[:, C_ID:C_ID + P]
        idx_in = sb("p_idx_in", [P, KT], I32)
        idx_mid = sb("p_idx_mid", [P, FT], I32)
        gathered = sb("p_gathered", [P, 2, FT * DM])
        down = sb("p_down", [P, FT, DM])
        down_q = sb("p_down_q", [P, KT, FF])
        amax = sb("p_amax", [P, 2, 32])
        scale = sb("p_scale", [P, 2, 32])
        rec = sb("p_rec", [P, 2, 32])
        ratio = sb("p_ratio", [P, 2, DM])
        quant = sb("p_quant", [P, 2, DM])
        AB = [ps(f"p_AB{i}", [P, DM]) for i in range(2)]
        BB = [ps(f"p_BB{i}", [P, DM]) for i in range(2)]

        idx_loaded, g_in, g_down = sem("p_idx_loaded"), [sem("p_g_in0"), sem("p_g_in1")], sem("p_g_down")
        stored = [[sem("p_stored00"), sem("p_stored01")], [sem("p_stored10"), sem("p_stored11")]]
        g_mid = [sem("p_g_mid0"), sem("p_g_mid1")]
        a_full, a_read, q_ready, own_sem = sem("p_a_full"), sem("p_a_read"), sem("p_q_ready"), sem("p_own")
        b_full, b_hi, b_lo = sem("p_b_full"), sem("p_b_hi"), sem("p_b_lo")
        ROWS = [(m, i) for m in range(2) for i in range(FT)]
        DOWN = [(o, c) for o in range(KT) for c in range(3)]
        NR, NQ = len(ROWS), len(ROWS) + len(DOWN)
        block = stack.enter_context(nc.Block())

        @block.gpsimd
        def _(pool):
            pool.dma_start(idx_in[:, :], ri_in_cols).then_inc(idx_loaded, 16)
            pool.dma_start(idx_mid[:, 0:FT - 1], ri_mid_cols).then_inc(idx_loaded, 16)
            pool.dma_start(idx_mid[0:rows_of(FT - 1), FT - 1:FT], ri_mid_last).then_inc(idx_loaded, 16)
            pool.wait_ge(idx_loaded, 48)
            for m in range(2):
                for k in range(KT):
                    pool.indirect_dma_start(
                        out=gathered[:, m, k * FF:(k + 1) * FF], out_offset=None, in_=wT[m][:, :],
                        in_offset=bass.IndirectOffsetOnAxis(ap=idx_in[:, k:k + 1], axis=0)).then_inc(g_in[m], 16)
            for i in range(FT):
                n = rows_of(i)
                pool.indirect_dma_start(
                    out=down[0:n, i, :], out_offset=None, in_=wdT[:, :],
                    in_offset=bass.IndirectOffsetOnAxis(ap=idx_mid[0:n, i:i + 1], axis=0)).then_inc(g_down, 16)
            for m in range(2):
                for par in range(2):
                    pool.wait_ge(stored[m][par], 16 * len([r for j, r in enumerate(ROWS) if r[0] == m and j % 2 == par]))
                pool.wait_ge(a_full, (m + 1) * FT)
                for i in range(FT):
                    n = rows_of(i)
                    pool.indirect_dma_start(
                        out=gathered[0:n, m, i * DM:(i + 1) * DM], out_offset=None, in_=scratch[m][:, :],
                        in_offset=bass.IndirectOffsetOnAxis(ap=idx_mid[0:n, i:i + 1], axis=0)).then_inc(g_mid[m], 16)

        @block.sync
        def _(sp):
            for j, (m, i) in enumerate(ROWS):
                n = rows_of(i)
                sp.wait_ge(q_ready, j + 1)
                sp.dma_start(scratch[m][i * P:i * P + n, :], quant[0:n, j % 2, :]).then_inc(stored[m][j % 2], 16)

        @block.tensor
        def _(pe):
            for j, (m, i) in enumerate(ROWS):
                n = rows_of(i)
                pe.wait_ge(g_in[m], 16 * KT)
                if j >= 2:
                    pe.wait_ge(a_read, j - 1)
                for k in range(KT):
                    ins = nc.tensor.transpose(AB[j % 2][0:n, k * P:(k + 1) * P],
                                              gathered[:, m, k * FF + i * P:k * FF + i * P + n], ident)
                ins.then_inc(a_full, 1)
            pe.wait_ge(g_down, 16 * FT)
            for j, (o, c) in enumerate(DOWN, NR):
                pe.wait_ge(a_read, j - 1)
                for i in range(4 * c, min(4 * c + 4, FT)):
                    n = rows_of(i)
                    ins = nc.tensor.transpose(AB[j % 2][:, (i - 4 * c) * P:(i - 4 * c) * P + n],
                                              down[0:n, i, o * P:(o + 1) * P], ident[0:n, 0:n])
                ins.then_inc(a_full, 1)
            for j in range(3 * FT):
                m, i = divmod(j, FT)
                n = rows_of(i)
                if j >= 2:
                    pe.wait_ge(b_lo, j - 1)
                if m < 2:
                    pe.wait_ge(g_mid[m], 16 * FT)
                    for k in range(KT):
                        ins = nc.tensor.transpose(BB[j % 2][:, k * P:k * P + n],
                                                  gathered[0:n, m, i * DM + k * P:i * DM + (k + 1) * P],
                                                  ident[0:n, 0:n])
                else:
                    pe.wait_ge(q_ready, NQ)
                    for o in range(KT):
                        ins = nc.tensor.transpose(BB[j % 2][0:n, o * P:(o + 1) * P],
                                                  down_q[:, o, i * P:i * P + n], ident)
                ins.then_inc(b_full, 1)

        def split_of(j):
            m, i = divmod(j, FT)
            n = rows_of(i)
            if m < 2:
                bank = BB[j % 2][:, :].rearrange("p (k c) -> p k c", c=P)[:, :, 0:n]
                return bank, [w16[:, m, a, :, i * P:i * P + n] for a in range(2)]
            return BB[j % 2][0:n, :], [wd16[0:n, a, i, :] for a in range(2)]

        @block.scalar
        def _(act):
            for j in range(3 * FT):
                bank, dst = split_of(j)
                act.wait_ge(b_full, j + 1)
                nc.scalar.activation(dst[0], bank, ACT.Copy, scale=WS).then_inc(b_hi, 1)

        @block.vector
        def _(dve):
            own = Chain(dve, own_sem)

            def quantise(j, n, nb, dst, signal):
                b = j % 2
                bank = blocks(AB[b][0:n, 0:nb * QB16])
                r = blocks(ratio[0:n, b, 0:nb * QB16])
                dve.wait_ge(a_full, j + 1)
                own.link(nc.vector.tensor_reduce(amax[0:n, b, 0:nb], bank, AX.X, ALU.max, apply_absolute_value=True))
                own.link(nc.vector.tensor_scalar(scale[0:n, b, 0:nb], amax[0:n, b, 0:nb], 1 / 7.0, TINY,
                                                 ALU.mult, ALU.max))
                own.link(nc.vector.reciprocal(rec[0:n, b, 0:nb], scale[0:n, b, 0:nb]))
                nc.vector.tensor_tensor(r, bank, spread(rec[0:n, b, 0:nb], n, nb), ALU.mult).then_inc(a_read, 1)
                dve.wait_ge(a_read, j + 1)
                own.link(nc.vector.tensor_scalar(r, r, 7.0, ROUND, ALU.min, ALU.add))
                nc.vector.scalar_tensor_tensor(dst, r, ROUND, spread(scale[0:n, b, 0:nb], n, nb),
                                               ALU.subtract, ALU.mult).then_inc(signal, 1)

            for j, (m, i) in enumerate(ROWS):
                n = rows_of(i)
                if j >= 2:
                    pm = ROWS[j - 2][0]
                    dve.wait_ge(stored[pm][j % 2], 16 * len([1 for q in range(j - 1) if ROWS[q][0] == pm and q % 2 == j % 2]))
                quantise(j, n, 32, blocks(quant[0:n, j % 2, :]), q_ready)
            for j, (o, c) in enumerate(DOWN, NR):
                w = min(512, FF - 512 * c)
                quantise(j, P, w // QB16, blocks(down_q[:, o, 512 * c:512 * c + w]), q_ready)
            for j in range(3 * FT):
                bank, dst = split_of(j)
                dve.wait_ge(b_hi, j + 1)
                ins = nc.vector.scalar_tensor_tensor(dst[1], bank, WS, dst[0], ALU.mult, ALU.subtract)
                ins.then_inc(b_lo, 1)


def round_fp8(nc, own, y, m):
    own.link(nc.vector.tensor_scalar(m.bitcast(I32), y.bitcast(I32), EXPONENT, None, ALU.bitwise_and))
    own.link(nc.vector.tensor_scalar(m, m, 2.0 ** -6, R4, ALU.max, ALU.mult))
    own.link(nc.vector.tensor_tensor(y, y, m, ALU.add))
    own.link(nc.vector.tensor_tensor(y, y, m, ALU.subtract))


def transposed_parts(c):
        return [(P, 4, 4 * c)] if c < 2 else [(P, FT - 9, 8), (rows_of(FT - 1), 1, FT - 1)]


def feed_forward_phase(nc, X, const, const_in, w16, wd16, ri_in, out, sem):
    with ExitStack() as stack:
        def sb(name, shape, dt=F32):
            return stack.enter_context(nc.sbuf_tensor(name, shape, dt))

        def ps(name, shape, dt=F32):
            return stack.enter_context(nc.psum_tensor(name, shape, dt))

        ident = const[:, C_ID:C_ID + P]
        NB = DM // QB16
        NBH = FF // QB16
        ON = (DM - SPLIT) // QB16
        OH = (FF - SPLIT) // QB16
        CW = 344
        NC = FF // CW
        assert NC * CW == FF

        st = sb("f_st", [P, NT, 6])
        mv = sb("f_mv", [P, NT, 2])
        rs = sb("f_rs", [P, NT])
        iota = sb("f_iota", [P, KT])
        ri_raw = sb("f_ri", [P, DM], I32)
        rif = sb("f_rif", [P, DM])
        hot = sb("f_hot", [P, KT, DM])
        xn = sb("f_xn", [P, 2, DM])
        gmax = sb("f_gmax", [P, NT])
        g1 = sb("f_g1", [P, 1])
        gall = sb("f_gall", [P, 1])
        floor = sb("f_floor", [P, 1])
        amax = sb("f_amax", [P, NB])
        scale = sb("f_scale", [P, NB])
        rec = sb("f_rec", [P, NB])
        xq = sb("f_xq", [P, 2, DM])
        mm = sb("f_mm", [P, FF])
        A16 = sb("f_A16", [P, 2, KT, TOK], F16)
        th = sb("f_th", [P, 2, CW])
        gate = sb("f_gate", [P, 2, CW])
        H = sb("f_H", [P, NT, FF])
        xT = [H[:, t, 0:DM].rearrange("p (k c) -> p k c", c=P) for t in range(NT)]
        hmax = sb("f_hmax", [P, NT, NBH])
        h1 = sb("f_h1", [P, 1])
        hall = sb("f_hall", [P, 1])
        hfloor = sb("f_hfloor", [P, 1])
        gm = sb("f_gm", [P, 3])
        hs = sb("f_hs", [P, 3, NBH])
        o_amax = sb("f_o_amax", [P, 3, SPLIT // QB16])
        res = sb("f_res", [P, 2, SPLIT])
        hq = sb("f_hq", [P, FF])
        hT = sb("f_hT", [P, 2, FT, P], F16)

        TB = [ps(f"f_TB{i}", [P, 4, P]) for i in range(3)]
        GA = [ps(f"f_GA{i}", [P, DM]) for i in range(2)]
        UA = [ps(f"f_UA{i}", [P, DM]) for i in range(2)]
        YB = ps("f_YB", [P, DM])

        names = ("idx const own var_ready root_ready xn_ready xt_full xt_ready xp_full xp_read gmax_ready gall_ready "
                 "aq_ready at_full a_hi a_lo gu_full th_ready gu_free hmax_ready hall_ready hq_ready ht_full ht_hi "
                 "ht_lo y_full y_read y_stored ratio_ready").split()
        s = {n: sem("f_" + n) for n in names}
        block = stack.enter_context(nc.Block())

        @block.sync
        def _(sp):
            sp.dma_start(ri_raw[:, :], ri_in.rearrange("(o n) -> o n", o=1).to_broadcast([P, DM])).then_inc(s["idx"], 16)
            sp.dma_start(iota[:, :], const_in[:, C_IOTA:C_IOTA + KT]).then_inc(s["const"], 16)
            with sp.Fori(0, NT) as t:
                sp.wait_ge(s["y_read"], t + 2)
                sp.dma_start(out[bass.ts(t, P), :], X[:, bass.ds(t, 1), :].rearrange("p o n -> p (o n)"))\
                    .then_inc(s["y_stored"], 16)
            sp.wait_ge(s["y_stored"], 16 * NT)

        @block.gpsimd
        def _(pool):
            pool.wait_ge(s["gmax_ready"], 1)
            nc.gpsimd.partition_all_reduce(gall[:, :], g1[:, :], P, RMAX).then_inc(s["gall_ready"], 1)
            pool.wait_ge(s["hmax_ready"], 1)
            nc.gpsimd.partition_all_reduce(hall[:, :], h1[:, :], P, RMAX).then_inc(s["hall_ready"], 1)

        @block.scalar
        def _(act):
            def copy(dst, src, scale=1.0):
                return nc.scalar.activation(dst, src, ACT.Copy, scale=scale)

            act.wait_ge(s["var_ready"], 1)
            nc.scalar.activation(rs[:, :], rs[:, :], ACT.Sqrt).then_inc(s["root_ready"], 1)
            for t in range(NT):
                act.wait_ge(s["xt_full"], t + 1)
                copy(xT[t], TB[t % 2][:, :, :]).then_inc(s["xt_ready"], 1)
            for t in range(NT):
                act.wait_ge(s["at_full"], t + 1)
                copy(A16[:, 0, :, t * P:(t + 1) * P], tiles4(UA[t % 2])).then_inc(s["a_hi"], 1)
            with act.Fori(0, NT) as t:
                for c in range(NC):
                    act.wait_ge(s["gu_full"], t * NC + c + 1)
                    nc.scalar.activation(th[:, c % 2, :], GA[c % 2][:, 0:CW], ACT.Tanh, scale=0.5 / WS)\
                        .then_inc(s["th_ready"], 1)
            with act.Fori(0, NT) as t:
                for c in range(3):
                    act.wait_ge(s["ht_full"], t * 3 + c + 1)
                    for n, w, lo in transposed_parts(c):
                        ins = copy(hT[0:n, 0, lo:lo + w, :], TB[c][0:n, lo - 4 * c:lo - 4 * c + w, :])
                    ins.then_inc(s["ht_hi"], 1)

        @block.vector
        def _(dve):
            own = Chain(dve, s["own"])
            dve.sem_inc(s["gu_free"], 2)
            dve.sem_inc(s["y_read"], 1)
            ins = layernorm_stats(dve, own, nc, X, st, mv, rs)
            ins.then_inc(s["var_ready"], 1)
            dve.wait_ge(s["idx"], 16)
            dve.wait_ge(s["const"], 16)
            own.link(nc.vector.tensor_copy(rif[:, :], ri_raw[:, :]))
            for k in range(KT):
                own.mark(nc.vector.tensor_scalar(hot[:, k, :], rif[:, :], iota[:, k:k + 1], None, ALU.is_equal))
            own.wait()
            dve.wait_ge(s["root_ready"], 1)
            own.link(nc.vector.reciprocal(rs[:, :], rs[:, :]))
            for t in range(NT):
                if t >= 2:
                    dve.wait_ge(s["xt_full"], t - 1)
                nc.vector.tensor_scalar(xn[:, t % 2, :], X[:, t, :], mv[:, t, 0:1], rs[:, t:t + 1],
                                        ALU.subtract, ALU.mult).then_inc(s["xn_ready"], 1)
                dve.wait_ge(s["xn_ready"], t + 1)
                own.mark(nc.vector.tensor_reduce(gmax[:, t:t + 1], xn[:, t % 2, :], AX.X, ALU.max,
                                                 apply_absolute_value=True))
            own.wait()
            nc.vector.tensor_reduce(g1[:, :], gmax[:, :], AX.X, ALU.max).then_inc(s["gmax_ready"], 1)
            dve.wait_ge(s["gall_ready"], 1)
            own.link(nc.vector.tensor_scalar(floor[:, :], gall[:, :], 1 / GSCALE, TINY, ALU.mult, ALU.max))
            own.link(nc.vector.tensor_scalar(floor[:, :], floor[:, :], TINY, None, ALU.mult))

            def scales(dst_s, dst_r, amax_, floor_):
                own.link(nc.vector.tensor_scalar(dst_s, amax_, 1 / FP8_MAX, floor_, ALU.mult, ALU.max))
                own.link(nc.vector.reciprocal(dst_r, dst_s))

            def second(rest, floor_):
                nb = SPLIT // QB16
                own.link(nc.vector.tensor_reduce(o_amax[:, 0, :], blocks(rest), AX.X, ALU.max,
                                                 apply_absolute_value=True))
                scales(o_amax[:, 1, :], o_amax[:, 2, :], o_amax[:, 0, :], floor_)
                own.link(nc.vector.tensor_tensor(blocks(rest), blocks(rest), spread(o_amax[:, 2, :], P, nb), ALU.mult))
                round_fp8(nc, own, rest, mm[:, 0:SPLIT])
                own.link(nc.vector.tensor_tensor(blocks(rest), blocks(rest), spread(o_amax[:, 1, :], P, nb), ALU.mult))

            def a_lo(t):
                dve.wait_ge(s["a_hi"], t + 1)
                nc.vector.tensor_tensor(A16[:, 1, :, t * P:(t + 1) * P], tiles4(UA[t % 2]),
                                        A16[:, 0, :, t * P:(t + 1) * P], ALU.subtract).then_inc(s["a_lo"], 1)

            for t in range(NT):
                dve.wait_ge(s["xp_full"], t + 1)
                if t >= 2:
                    dve.wait_ge(s["at_full"], t - 1)
                bank = GA[t % 2][:, :]
                q = xq[:, t % 2, :]
                own.link(nc.vector.tensor_reduce(amax[:, :], blocks(bank), AX.X, ALU.max, apply_absolute_value=True))
                scales(scale[:, :], rec[:, :], amax[:, :], floor[:, :])
                own.link(nc.vector.tensor_tensor(blocks(q), blocks(bank), spread(rec[:, :], P, NB), ALU.mult))
                round_fp8(nc, own, q, mm[:, 0:DM])
                own.link(nc.vector.tensor_tensor(blocks(q), blocks(q), spread(scale[:, :], P, NB), ALU.mult))
                rest = res[:, 0, :]
                nc.vector.tensor_tensor(rest, bank[:, DM - SPLIT:], q[:, DM - SPLIT:], ALU.subtract)\
                    .then_inc(s["xp_read"], 1)
                dve.wait_ge(s["xp_read"], t + 1)
                second(rest, floor[:, :])
                nc.vector.tensor_tensor(q[:, DM - SPLIT:], q[:, DM - SPLIT:], rest, ALU.add).then_inc(s["aq_ready"], 1)
                if t >= 1:
                    a_lo(t - 1)
            a_lo(NT - 1)

            PRO = own.n
            with dve.Fori(0, NT) as t:
                own.enter(PRO, t, NC)
                for c in range(NC):
                    dve.wait_ge(s["th_ready"], t * NC + c + 1)
                    own.link(nc.vector.scalar_tensor_tensor(gate[:, c % 2, :], th[:, c % 2, :], 1.0, GA[c % 2][:, 0:CW],
                                                            ALU.add, ALU.mult))
                    ht = H[:, bass.ds(t, 1), c * CW:(c + 1) * CW].rearrange("p o n -> p (o n)")
                    nc.vector.scalar_tensor_tensor(ht, gate[:, c % 2, :], 0.5 / WS / WS, UA[c % 2][:, 0:CW],
                                                   ALU.mult, ALU.mult).then_inc(s["gu_free"], 1)
                    if c % 2:
                        dve.wait_ge(s["gu_free"], t * NC + c + 3)
                        hb = H[:, bass.ds(t, 1), (c - 1) * CW:(c + 1) * CW]\
                            .rearrange("p o (b e) -> p (o b) e", e=QB16)
                        mb = hmax[:, bass.ds(t, 1), (c - 1) * CW // QB16:(c + 1) * CW // QB16]\
                            .rearrange("p o b -> p (o b)")
                        nc.vector.tensor_reduce(mb, hb, AX.X, ALU.max, apply_absolute_value=True)\
                            .then_inc(s["ratio_ready"], 1)
            dve.wait_ge(s["ratio_ready"], 2 * NT)
            own.enter(PRO + NC * NT, 0, 0)
            nc.vector.tensor_reduce(h1[:, :], hmax[:, :, :], AX.XY, ALU.max).then_inc(s["hmax_ready"], 1)
            dve.wait_ge(s["hall_ready"], 1)
            own.link(nc.vector.tensor_scalar(gm[:, 0:1], hall[:, :], 1 / GSCALE, TINY, ALU.mult, ALU.max))
            own.link(nc.vector.tensor_scalar(hfloor[:, :], gm[:, 0:1], TINY, None, ALU.mult))
            own.link(nc.vector.reciprocal(gm[:, 1:2], gm[:, 0:1]))
            own.link(nc.vector.tensor_scalar(gm[:, 2:3], gm[:, 0:1], 1 / WS, None, ALU.mult))
            PRO2 = PRO + NC * NT + 4
            BODY = 2 + 1 + 4 + 3 + 1 + 2 + 1 + 4 + 1 + 1
            with dve.Fori(0, NT) as t:
                own.enter(PRO2, t, BODY)
                h = H[:, bass.ds(t, 1), :].rearrange("p o n -> p (o n)")
                ho = H[:, bass.ds(t, 1), FF - SPLIT:].rearrange("p o n -> p (o n)")
                hm = hmax[:, bass.ds(t, 1), :].rearrange("p o n -> p (o n)")
                hb = H[:, bass.ds(t, 1), :].rearrange("p o (b e) -> p (o b) e", e=QB16)
                scales(hs[:, 0, :], hs[:, 1, :], hm, hfloor[:, :])
                own.link(nc.vector.tensor_tensor(blocks(hq[:, :]), hb, spread(hs[:, 1, :], P, NBH), ALU.mult))
                round_fp8(nc, own, hq[:, :], mm[:, :])
                own.link(nc.vector.tensor_tensor(blocks(res[:, 0, :]), blocks(hq[:, FF - SPLIT:]),
                                                 spread(hs[:, 0, OH:], P, SPLIT // QB16), ALU.mult))
                own.link(nc.vector.tensor_tensor(res[:, 0, :], ho, res[:, 0, :], ALU.subtract))
                own.link(nc.vector.tensor_scalar(hs[:, 2, :], hs[:, 0, :], gm[:, 1:2], None, ALU.mult))
                own.link(nc.vector.tensor_tensor(blocks(hq[:, :]), blocks(hq[:, :]), spread(hs[:, 2, :], P, NBH),
                                                 ALU.mult))
                second(res[:, 0, :], hfloor[:, :])
                nc.vector.scalar_tensor_tensor(hq[:, FF - SPLIT:], res[:, 0, :], gm[:, 1:2], hq[:, FF - SPLIT:],
                                               ALU.mult, ALU.add).then_inc(s["hq_ready"], 1)
                for c in range(3):
                    dve.wait_ge(s["ht_hi"], t * 3 + c + 1)
                    for n, w, lo in transposed_parts(c):
                        ins = nc.vector.tensor_tensor(hT[0:n, 1, lo:lo + w, :], TB[c][0:n, lo - 4 * c:lo - 4 * c + w, :],
                                                      hT[0:n, 0, lo:lo + w, :], ALU.subtract)
                    ins.then_inc(s["ht_lo"], 1)
                dve.wait_ge(s["y_full"], t + 1)
                xt = X[:, bass.ds(t, 1), :].rearrange("p o n -> p (o n)")
                nc.vector.scalar_tensor_tensor(xt, YB[:, :], gm[:, 2:3], xt, ALU.mult, ALU.add)\
                    .then_inc(s["y_read"], 1)
                assert own.n == BODY, (own.n, BODY)

        @block.tensor
        def _(pe):
            PASSES = ((0, 0), (0, 1), (1, 0))

            for t in range(NT):
                pe.wait_ge(s["xn_ready"], t + 1)
                if t >= 2:
                    pe.wait_ge(s["xt_ready"], t - 1)
                for k in range(KT):
                    ins = nc.tensor.transpose(TB[t % 2][:, k, :], xn[:, t % 2, k * P:(k + 1) * P], ident)
                ins.then_inc(s["xt_full"], 1)

            def gather(t):
                pe.wait_ge(s["xt_ready"], t + 1)
                if t >= 2:
                    pe.wait_ge(s["xp_read"], t - 1)
                for k in range(KT):
                    ins = nc.tensor.matmul(GA[t % 2][:, :], xT[t][:, k, :], hot[:, k, :],
                                           start=(k == 0), stop=(k == KT - 1))
                ins.then_inc(s["xp_full"], 1)

            gather(0)
            gather(1)
            for t in range(NT):
                pe.wait_ge(s["aq_ready"], t + 1)
                if t >= 2:
                    pe.wait_ge(s["a_lo"], t - 1)
                for k in range(KT):
                    ins = nc.tensor.transpose(UA[t % 2][:, k * P:(k + 1) * P], xq[:, t % 2, k * P:(k + 1) * P], ident)
                ins.then_inc(s["at_full"], 1)
                if t + 2 < NT:
                    gather(t + 2)
            pe.wait_ge(s["a_lo"], NT)
            with pe.Fori(0, NT) as t:
                for c in range(NC):
                    pe.wait_ge(s["gu_free"], t * NC + c + 1)
                    for m, bank in enumerate((GA[c % 2], UA[c % 2])):
                        for k in range(KT):
                            for q, (a, b) in enumerate(PASSES):
                                ins = nc.tensor.matmul(bank[:, 0:CW], A16[:, a, k, bass.ts(t, P)],
                                                       w16[:, m, b, k, c * CW:(c + 1) * CW],
                                                       start=(k == 0 and q == 0), stop=(k == KT - 1 and q == 2))
                    ins.then_inc(s["gu_full"], 1)
            with pe.Fori(0, NT) as t:
                pe.wait_ge(s["hq_ready"], t + 1)
                for c in range(3):
                    for i in range(4 * c, min(4 * c + 4, FT)):
                        n = rows_of(i)
                        ins = nc.tensor.transpose(TB[c][0:n, i - 4 * c, :], hq[:, i * P:i * P + n], ident)
                    ins.then_inc(s["ht_full"], 1)
                pe.wait_ge(s["ht_lo"], t * 3 + 3)
                pe.wait_ge(s["y_read"], t + 1)
                for i in range(FT):
                    n = rows_of(i)
                    for q, (a, b) in enumerate(PASSES):
                        ins = nc.tensor.matmul(YB[:, :], hT[0:n, a, i, :], wd16[0:n, b, i, :],
                                               start=(i == 0 and q == 0), stop=(i == FT - 1 and q == 2))
                ins.then_inc(s["y_full"], 1)


def tiles4(bank):
    return bank[:, :].rearrange("p (k c) -> p k c", c=P)


def decoder_layer(nc, const_in, x_in, ctx_in, ctxT_in, w_q, w_k, w_v, w_o, w_lq, w_lk, w_lv, w_lo,
                  x_WqT, x_WkT, x_Wv, x_WoT, x_bo, x_g, w_gateT, w_upT, w_downT, ri_in, ri_in_cols, ri_mid_cols, ri_mid_last, out):
    scratch = [nc.dram_tensor(f"scratch{m}", (FF, DM), F32, kind="Internal").ap() for m in range(2)]
    with ExitStack() as ctx:
        def sem(name):
            return ctx.enter_context(nc.semaphore(name))

        X = ctx.enter_context(nc.sbuf_tensor("X", [P, NT, DM], F32))
        const = ctx.enter_context(nc.sbuf_tensor("const", [P, C_COMMON], F32))
        attention_phase(nc, X, const, const_in, x_in, w_q, w_k, w_v, w_o, w_lq, w_lk, w_lv, w_lo, sem)
        cross_phase(nc, X, const, const_in, ctx_in, ctxT_in, x_WqT, x_WkT, x_Wv, x_WoT, x_bo, x_g, sem)
        w16 = ctx.enter_context(nc.sbuf_tensor("w16_ffn", [P, 2, 2, KT, FF], F16))
        wd16 = ctx.enter_context(nc.sbuf_tensor("wd16_ffn", [P, 2, FT, DM], F16))
        weight_phase(nc, const, w16, wd16, (w_gateT, w_upT), w_downT, scratch, ri_in_cols, ri_mid_cols, ri_mid_last, sem)
        feed_forward_phase(nc, X, const, const_in, w16, wd16, ri_in, out, sem)


def kernel(**inputs):
    import concourse.bacc as bacc
    from concourse.bass_utils import run_bass_kernel_spmd

    nc = bacc.Bacc("TRN2", target_bir_lowering=False, num_devices=1)
    arrays, args = {}, []

    def give(name, a):
        a = np.ascontiguousarray(a)
        arrays[name] = a
        args.append(nc.dram_tensor(name, a.shape, mybir.dt.from_np(a.dtype), kind="ExternalInput").ap())

    give("shape_constants", shape_constants())
    give("x", np.asarray(inputs["x"]).reshape(TOK, DM))
    give("ctx", np.asarray(inputs["ctx_4096"]).reshape(TOK, DM))
    give("ctxT", np.asarray(inputs["ctx_4096"]).transpose(0, 2, 1))
    for n in ("w_q", "w_k", "w_v", "w_o", "w_lq", "w_lk", "w_lv", "w_lo"):
        give(n, np.asarray(inputs["L0_attn_" + n]))
    for n, flip in (("Wq", True), ("Wk", True), ("Wv", False), ("Wo", True), ("bo", False), ("g", False)):
        a = np.asarray(inputs["L0_xattn_" + n])
        give("x_" + n, a.T if flip else a)
    for n in ("w_gate", "w_up", "w_down"):
        give(n, np.asarray(inputs["L0_ffn_" + n]).T)
    ri_in, ri_mid = np.asarray(inputs["L0_ffn_ri_in"]), np.asarray(inputs["L0_ffn_ri_mid"])
    whole = (FT - 1) * P
    give("ri_in", ri_in)
    give("ri_in_cols", ri_in.reshape(KT, P).T)
    give("ri_mid_cols", ri_mid[:whole].reshape(FT - 1, P).T)
    give("ri_mid_last", ri_mid[whole:].reshape(FF - whole, 1))
    args.append(nc.dram_tensor("out", (TOK, DM), F32, kind="ExternalOutput").ap())
    decoder_layer(nc, *args)
    r = run_bass_kernel_spmd(nc, [arrays], core_ids=[0])
    return r.results[0]["out"].reshape(BATCH, SEQ, DM)
```

```python
from contextlib import ExitStack

import numpy as np

import concourse.bass as bass
from concourse import mybir

P = 128
BATCH, SEQ, DM = 16, 64, 512
TOK = BATCH * SEQ
NT = TOK // P
KT = DM // P
HEADS, KVH, HD = 32, 8, 128
GROUP = HEADS // KVH
HB = 2 * GROUP
ITERS = HEADS // HB
SCALE = 1.0 / float(np.sqrt(HD))
WS = 64.0
EPS = 1e-5
HALF = 512

ALU = mybir.AluOpType
ACT = mybir.ActivationFunctionType
AX = mybir.AxisListType
F32 = mybir.dt.float32
F16 = mybir.dt.float16
I32 = mybir.dt.int32

C_ID, C_COS, C_SIN, C_MASK, C_ONES, C_PICK, C_IOTA, C_END = 0, 128, 192, 256, 320, 352, 480, 484
C_COMMON = C_ONES


def shape_constants():
    c = np.zeros((P, C_END), np.float32)
    c[:, C_ID:C_ID + P] = np.eye(P, dtype=np.float32)
    inv = (np.float32(1.0) / np.float32(10000.0) ** (np.arange(0, HD, 2, dtype=np.float32) / np.float32(HD)))
    freq = np.outer(np.arange(SEQ, dtype=np.float32), inv.astype(np.float32)).astype(np.float32)
    cos, sin = np.cos(freq).T, np.sin(freq).T
    c[0:64, C_COS:C_COS + SEQ] = cos / WS
    c[64:128, C_COS:C_COS + SEQ] = cos / WS
    c[0:64, C_SIN:C_SIN + SEQ] = sin / WS
    c[64:128, C_SIN:C_SIN + SEQ] = -sin / WS
    q = np.arange(P) % SEQ
    c[:, C_MASK:C_MASK + SEQ] = np.where(np.arange(SEQ)[None, :] <= q[:, None], 0.0, -1e30)
    p = np.arange(P)
    c[:, C_ONES:C_ONES + 32] = (p[:, None] // 64 == np.arange(32)[None, :] % 2)
    c[:, C_PICK:C_PICK + P] = (p[:, None] % 32 == p[None, :] // 64)
    c[:, C_IOTA:C_IOTA + KT] = p[:, None] + P * np.arange(KT)[None, :]
    return c


class Chain:

    def __init__(self, engine, sem):
        self.engine, self.sem, self.base, self.n = engine, sem, 0, 0

    def link(self, instruction):
        self.mark(instruction)
        self.wait()

    def mark(self, instruction):
        self.n += 1
        instruction.then_inc(self.sem, 1)

    def wait(self):
        self.engine.wait_ge(self.sem, self.base + self.n)

    def enter(self, start, it, per_body):
        self.base, self.n = it * per_body + start, 0


def layernorm_stats(dve, chain, nc, X, st, mv, rs):
    for t in range(NT):
        chain.link(nc.vector.bn_stats(st[:, t, :], X[:, t, :]))
    for t in range(NT):
        chain.mark(nc.vector.bn_aggr(mv[:, t, :], st[:, t, :]))
    chain.wait()
    return nc.vector.tensor_scalar(rs[:, :], mv[:, :, 1], EPS, None, ALU.add)


def attention_phase(nc, X, const, const_in, x_in, w_q, w_k, w_v, w_o, w_lq, w_lk, w_lv, w_lo, sem):
    with ExitStack() as ctx:
        def sb(name, shape, dt=F32):
            return ctx.enter_context(nc.sbuf_tensor(name, shape, dt))

        def ps(name, shape, dt=F32):
            return ctx.enter_context(nc.psum_tensor(name, shape, dt))

        ident = const[:, C_ID:C_ID + P]
        cos8 = const[:, C_COS:C_COS + SEQ].unsqueeze(1).to_broadcast([P, BATCH, SEQ])
        mask = const[:, C_MASK:C_MASK + SEQ].unsqueeze(1).to_broadcast([P, 2 * NT, SEQ])

        def sin_of(p0):
            return const[p0:p0 + 64, C_SIN:C_SIN + SEQ].unsqueeze(1).to_broadcast([64, BATCH, SEQ])

        XT = sb("XT", [P, 2, KT, TOK], F16)
        LQ = sb("LQ", [P, 2, TOK], F16)
        st = sb("st", [P, NT, 6])
        mv = sb("mv", [P, NT, 2])
        rs = sb("rs", [P, NT])
        NW = 2 * KT + 1
        w_raw = sb("w_raw", [P, 2, NW, P])
        w16 = sb("w16", [P, 2, 2, NW, P], F16)
        kv_raw = sb("kv_raw", [P, 2 * KT, P])
        kv16 = sb("kv16", [P, 2, 2 * KT, P], F16)
        o_raw = sb("o_raw", [P, GROUP, DM])
        o16 = sb("o16", [P, 2, 2 * GROUP, DM], F16)
        q_raw = sb("q_raw", [P, TOK])
        lk_raw = sb("lk_raw", [P, TOK])
        k_raw = sb("k_raw", [P, TOK])
        rt = sb("rt", [P, 2, TOK])
        gt = sb("gt", [P, 2, TOK])
        qT = sb("qT", [P, 2, TOK])
        lkT = sb("lkT", [P, 2, TOK])
        kT = sb("kT", [P, 2, TOK])
        v = sb("v", [P, 2, NT, HD])
        lv = sb("lv", [P, 2, NT, HD])
        s_sb = sb("s_sb", [P, 2 * NT, SEQ])
        rmax = sb("rmax", [P, 2 * NT])
        rsum = sb("rsum", [P, 2 * NT])
        pbd = sb("pbd", [P, 2 * NT, P])
        pT = sb("pT", [P, 2 * NT, P])
        xn = s_sb[:, :, :].rearrange("p a b -> p (a b)").rearrange("p (a b) -> p a b", a=2)
        wlq_raw = pT[:, 0:4, :]
        wlq = pT[:, 4:8, :].bitcast(F16).rearrange("p a (b c) -> p (a b) c", c=P).rearrange("p (a b) c -> p a b c", a=2)
        aT = sb("aT", [P, 2, 2 * GROUP, TOK], F16)

        PJ = [ps(f"PJ{i}", [P, HALF]) for i in range(2)]
        S = ps("S", [P, 2 * NT, SEQ])
        TB = [ps(f"TB{i}", [P, 4, P]) for i in range(2)]
        OB = [ps(f"OB{i}", [P, HALF]) for i in range(2)]

        x_loaded, const_loaded, wlq_loaded = sem("x_loaded"), sem("const_loaded"), sem("wlq_loaded")
        w_loaded = [sem("w_loaded0"), sem("w_loaded1")]
        kv_loaded, o_loaded = sem("kv_loaded"), sem("o_loaded")
        dve_own, pool_own, act_own = sem("dve_own"), sem("pool_own"), sem("act_own")
        var_ready, root_ready, xn_ready = sem("var_ready"), sem("root_ready"), sem("xn_ready")
        xt_psum, xt_hi, xt_lo = sem("xt_psum"), sem("xt_hi"), sem("xt_lo")
        wlq_hi, wlq_lo, lq_psum, lq_hi, lq_lo = (sem(n) for n in ("wlq_hi", "wlq_lo", "lq_psum", "lq_hi", "lq_lo"))
        wt_hi, wt_lo, kv_hi, kv_lo, o_hi, o_lo = (sem(n) for n in ("wt_hi", "wt_lo", "kv_hi", "kv_lo", "o_hi", "o_lo"))
        pj_full, pj_free = sem("pj_full"), sem("pj_free")
        q_evac, lk_evac, k_evac = sem("q_evac"), sem("lk_evac"), sem("k_evac")
        q_roped, lk_roped, k_roped = sem("q_roped"), sem("lk_roped"), sem("k_roped")
        s_full, shifted, exp_done, pbd_ready = sem("s_full"), sem("shifted"), sem("exp_done"), sem("pbd_ready")
        t_full, t_free = sem("t_full"), sem("t_free")
        b_full, b_free, a_hi = sem("b_full"), sem("b_free"), sem("a_hi")
        pbd_zeroed = sem("pbd_zeroed")

        def pj_base(h):
            return 6 * h + (4 if h > 3 else 0)

        PJ_BODY, T_BODY, B_BODY = 6 * HB + 8, 4 * HB, 4 * HB + 2 * NT
        PJ_PRO = 10

        def b_base(h):
            return 4 * h + NT * (h // 4)

        wq_v = w_q.rearrange("(k p) n -> p k n", p=P)
        wlv_v = w_lv.rearrange("(k p) n -> p k n", p=P)
        wk_v = w_k.rearrange("(k p) n -> p k n", p=P)
        wv_v = w_v.rearrange("(k p) n -> p k n", p=P)
        wo_v = w_o.rearrange("(h p) n -> p h n", p=P)
        wlo_v = w_lo.rearrange("(h p) n -> p h n", p=P)

        block = ctx.enter_context(nc.Block())

        @block.sync
        def _(sp):
            def load_head(par, n):
                sp.dma_start(w_raw[:, par, 0:KT, :], wq_v[:, :, bass.ts(n, P)]).then_inc(w_loaded[par], 16)
                sp.dma_start(w_raw[:, par, KT, :], w_lk[:, bass.ts(n, P)]).then_inc(w_loaded[par], 16)
                sp.dma_start(w_raw[:, par, KT + 1:NW, :], wlv_v[:, :, bass.ts(n, P)]).then_inc(w_loaded[par], 16)

            def load_kv(g):
                sp.dma_start(kv_raw[:, 0:KT, :], wk_v[:, :, bass.ts(g, P)]).then_inc(kv_loaded, 16)
                sp.dma_start(kv_raw[:, KT:, :], wv_v[:, :, bass.ts(g, P)]).then_inc(kv_loaded, 16)

            def load_o(g, part):
                src = (wo_v, wlo_v)[part]
                sp.dma_start(o_raw[:, :, :], src[:, bass.ts(g, GROUP), :]).then_inc(o_loaded, 16)

            sp.dma_start(X[:, :, :], x_in.rearrange("(t p) n -> p t n", p=P)).then_inc(x_loaded, 16)
            sp.dma_start(wlq_raw[:, :, :], w_lq.rearrange("(k p) n -> p k n", p=P)).then_inc(wlq_loaded, 16)
            load_kv(0)
            load_head(0, 0)
            load_head(1, 1)
            load_o(0, 0)

            def body(it, last):
                for h in range(HB):
                    if not (last and h >= HB - 2):
                        sp.wait_ge(wt_hi, it * HB + h + 1)
                        sp.wait_ge(wt_lo, it * HB + h + 1)
                        load_head(h % 2, it * HB + h + 2)
                    g = h // 4
                    if h % 4 == 0 and not (last and g == 1):
                        sp.wait_ge(kv_hi, it * 2 + g + 1)
                        sp.wait_ge(kv_lo, it * 2 + g + 1)
                        load_kv(it * 2 + g + 1)
                    if h % 4 == 1 or (h % 4 == 2 and not (last and g == 1)):
                        sp.wait_ge(o_hi, it * 4 + 2 * g + h % 4)
                        sp.wait_ge(o_lo, it * 4 + 2 * g + h % 4)
                        load_o(it * 2 + g + h % 4 - 1, h % 4 % 2)

            with sp.Fori(0, ITERS - 1) as it:
                body(it, False)
            body(ITERS - 1, True)

        @block.scalar
        def _(act):
            def hi_of(dst, src, scale=WS):
                return nc.scalar.activation(dst, src, ACT.Copy, scale=scale)

            def split_head(par, need, m):
                act.wait_ge(w_loaded[par], need)
                hi_of(w16[:, par, 0], w_raw[:, par]).then_inc(wt_hi, 1)

            act.dma_start(const[:, :], const_in[:, 0:C_COMMON]).then_inc(const_loaded, 16)
            act.sem_inc(pj_free, 2)
            act.sem_inc(t_free, 2)
            act.wait_ge(wlq_loaded, 16)
            hi_of(wlq[:, 0], wlq_raw[:, :]).then_inc(wlq_hi, 1)
            act.wait_ge(kv_loaded, 32)
            hi_of(kv16[:, 0], kv_raw[:, :]).then_inc(kv_hi, 1)
            split_head(0, 48, 0)
            split_head(1, 48, 1)
            act.wait_ge(var_ready, 1)
            nc.scalar.activation(rs[:, :], rs[:, :], ACT.Sqrt).then_inc(root_ready, 1)
            for t in range(NT):
                act.wait_ge(xt_psum, t + 1)
                hi_of(XT[:, 0, :, t * P:(t + 1) * P], TB[t % 2][:, :, :], 1.0).then_inc(xt_hi, 1)
            for c in range(2):
                act.wait_ge(lq_psum, c + 1)
                hi_of(LQ[:, 0, c * HALF:(c + 1) * HALF], OB[c][:, :], 1 / WS).then_inc(lq_hi, 1)

            def take(base, k, dst, scale, extra=None):
                act.wait_ge(pj_full, base + k + 1)
                src = PJ[k % 2][:, :]
                if len(dst.shape) == 3:
                    src = src.rearrange("p (t d) -> p t d", d=HD)
                ins = hi_of(dst, src, scale)
                ins.then_inc(pj_free, 1)
                return ins

            def kv_steps(base, k, gp, roped_need):
                if roped_need is not None:
                    act.wait_ge(k_roped, roped_need)
                take(base, k, k_raw[:, 0:HALF], 1.0)
                take(base, k + 1, k_raw[:, HALF:], 1.0)
                take(base, k + 2, v[:, gp, 0:4, :], 1 / WS)
                take(base, k + 3, v[:, gp, 4:8, :], 1 / WS)

            kv_steps(0, 0, 0, None)
            take(0, 4, q_raw[:, 0:HALF], 1.0)
            take(0, 5, q_raw[:, HALF:], 1.0)
            take(0, 6, lk_raw[:, 0:HALF], 1.0)
            take(0, 7, lk_raw[:, HALF:], 1.0)
            take(0, 8, lv[:, 0, 0:4, :], 1 / WS)
            take(0, 9, lv[:, 0, 4:8, :], 1 / WS)

            def body(it, last):
                for h in range(HB):
                    n = it * HB + h
                    more = not (last and h == HB - 1)
                    base = it * PJ_BODY + PJ_PRO
                    k = pj_base(h)
                    if more and h % 4 == 3:
                        kv_steps(base, k, (h // 4 + 1) % 2, it * 2 + h // 4 + 1)
                        k += 4
                    if more:
                        act.wait_ge(q_roped, n + 1)
                        take(base, k, q_raw[:, 0:HALF], 1.0)
                    act.wait_ge(shifted, n + 1)
                    nc.scalar.activation(s_sb[:, :, :], s_sb[:, :, :], ACT.Exp, scale=SCALE).then_inc(exp_done, 1)
                    if more:
                        take(base, k + 1, q_raw[:, HALF:], 1.0)
                        act.wait_ge(lk_roped, n + 1)
                        take(base, k + 2, lk_raw[:, 0:HALF], 1.0)
                        take(base, k + 3, lk_raw[:, HALF:], 1.0)
                        take(base, k + 4, lv[:, (h + 1) % 2, 0:4, :], 1 / WS)
                    if not (last and h >= HB - 2):
                        act.wait_ge(w_loaded[h % 2], (it * (HB // 2) + h // 2 + 2) * 48)
                        hi_of(w16[:, h % 2, 0], w_raw[:, h % 2]).then_inc(wt_hi, 1)
                    if h % 4 == 1:
                        g = h // 4
                        if not (last and g == 1):
                            act.wait_ge(kv_loaded, (it * 2 + g + 2) * 32)
                            hi_of(kv16[:, 0], kv_raw[:, :]).then_inc(kv_hi, 1)
                    if h % 4 in (1, 2):
                        part = h % 4 - 1
                        act.wait_ge(o_loaded, (it * 4 + 2 * (h // 4) + part + 1) * 16)
                        hi_of(o16[:, 0, part * GROUP:(part + 1) * GROUP], o_raw[:, :]).then_inc(o_hi, 1)
                    for j in range(4):
                        act.wait_ge(t_full, it * T_BODY + 4 * h + j + 1)
                        nc.scalar.activation(pT[:, 4 * j:4 * j + 4, :], TB[j % 2][:, :, :], ACT.Copy)\
                            .then_inc(t_free, 1)
                    for j in range(4):
                        if j == 2 and more:
                            take(base, k + 5, lv[:, (h + 1) % 2, 4:8, :], 1 / WS)
                        act.wait_ge(b_full, it * B_BODY + b_base(h) + j + 1)
                        kt = (h % 4) + GROUP * (j // 2)
                        hi_of(aT[:, 0, kt, (j % 2) * HALF:(j % 2 + 1) * HALF], OB[j % 2][:, :], 1.0)\
                            .then_inc(a_hi, 1)

            with act.Fori(0, ITERS - 1) as it:
                body(it, False)
            body(ITERS - 1, True)

        @block.gpsimd
        def _(pool):
            own = Chain(pool, pool_own)
            nc.gpsimd.memset(pbd[:, :, :], 0.0).then_inc(pbd_zeroed, 1)
            pool.wait_ge(const_loaded, 16)

            def rope(dst, src, ready):
                s3 = src.rearrange("p (b t) -> p b t", t=SEQ)
                g3 = [gt[:, i, :].rearrange("p (b t) -> p b t", t=SEQ) for i in range(2)]
                own.link(nc.gpsimd.tensor_tensor(g3[0], s3, cos8, ALU.mult))
                own.link(nc.gpsimd.tensor_tensor(g3[1][0:64], s3[64:128], sin_of(64), ALU.mult))
                own.link(nc.gpsimd.tensor_tensor(g3[1][64:128], s3[0:64], sin_of(0), ALU.mult))
                nc.gpsimd.tensor_tensor(dst, gt[:, 0, :], gt[:, 1, :], ALU.add).then_inc(ready, 1)

            pool.wait_ge(pj_free, 2 + 8)
            rope(lkT[:, 0, :], lk_raw[:, :], lk_roped)

            def body(it, last):
                own.enter(3, it, 3 * HB)
                for h in range(HB):
                    if last and h == HB - 1:
                        break
                    k = pj_base(h) + (4 if h % 4 == 3 else 0) + 4
                    pool.wait_ge(pj_free, it * PJ_BODY + PJ_PRO + 2 + k)
                    pool.wait_ge(lk_roped, it * HB + h + 1)
                    pool.wait_ge(s_full, it * HB + h + 1)
                    rope(lkT[:, (h + 1) % 2, :], lk_raw[:, :], lk_roped)

            with pool.Fori(0, ITERS - 1) as it:
                body(it, False)
            body(ITERS - 1, True)

        @block.vector
        def _(dve):
            own = Chain(dve, dve_own)

            def lo_of(dst, src, hi, scale):
                return nc.vector.scalar_tensor_tensor(dst, src, scale, hi, ALU.mult, ALU.subtract)

            def rope(dst, src, ready):
                s3 = src.rearrange("p (b t) -> p b t", t=SEQ)
                g3 = [rt[:, i, :].rearrange("p (b t) -> p b t", t=SEQ) for i in range(2)]
                own.mark(nc.vector.tensor_tensor(g3[0], s3, cos8, ALU.mult))
                own.mark(nc.vector.tensor_tensor(g3[1][0:64], s3[64:128], sin_of(64), ALU.mult))
                own.mark(nc.vector.tensor_tensor(g3[1][64:128], s3[0:64], sin_of(0), ALU.mult))
                own.wait()
                ins = nc.vector.tensor_tensor(dst, rt[:, 0, :], rt[:, 1, :], ALU.add)
                ins.then_inc(ready, 1)

            dve.sem_inc(b_free, 2)
            dve.wait_ge(x_loaded, 16)
            ins = layernorm_stats(dve, own, nc, X, st, mv, rs)
            ins.then_inc(var_ready, 1)
            dve.wait_ge(root_ready, 1)
            own.link(nc.vector.reciprocal(rs[:, :], rs[:, :]))
            for t in range(NT):
                if t >= 2:
                    dve.wait_ge(xt_psum, t - 1)
                nc.vector.tensor_scalar(xn[:, t % 2, :], X[:, t, :], mv[:, t, 0:1], rs[:, t:t + 1],
                                        ALU.subtract, ALU.mult).then_inc(xn_ready, 1)
                if t >= 1:
                    dve.wait_ge(xt_hi, t)
                    lo_of(XT[:, 1, :, (t - 1) * P:t * P], TB[(t - 1) % 2][:, :, :],
                          XT[:, 0, :, (t - 1) * P:t * P], 1.0).then_inc(xt_lo, 1)
            dve.wait_ge(xt_hi, NT)
            lo_of(XT[:, 1, :, (NT - 1) * P:], TB[(NT - 1) % 2][:, :, :],
                  XT[:, 0, :, (NT - 1) * P:], 1.0).then_inc(xt_lo, 1)
            dve.wait_ge(wlq_hi, 1)
            lo_of(wlq[:, 1], wlq_raw[:, :], wlq[:, 0], WS).then_inc(wlq_lo, 1)
            dve.wait_ge(kv_hi, 1)
            lo_of(kv16[:, 1], kv_raw[:, :], kv16[:, 0], WS).then_inc(kv_lo, 1)
            for par in range(2):
                dve.wait_ge(wt_hi, par + 1)
                lo_of(w16[:, par, 1], w_raw[:, par], w16[:, par, 0], WS).then_inc(wt_lo, 1)
            for c in range(2):
                dve.wait_ge(lq_hi, c + 1)
                lo_of(LQ[:, 1, c * HALF:(c + 1) * HALF], OB[c][:, :],
                      LQ[:, 0, c * HALF:(c + 1) * HALF], 1 / WS).then_inc(lq_lo, 1)
            dve.wait_ge(const_loaded, 16)
            dve.wait_ge(pj_free, 2 + 2)
            rope(kT[:, 0, :], k_raw[:, :], k_roped)
            dve.wait_ge(k_roped, 1)
            dve.wait_ge(pj_free, 2 + 6)
            rope(qT[:, 0, :], q_raw[:, :], q_roped)
            dve.wait_ge(pbd_zeroed, 1)
            PRO = own.n
            D_BODY = 4 * HB + 3 * HB + 3 * 2

            def body(it, last):
                own.enter(PRO, it, D_BODY)
                for h in range(HB):
                    n = it * HB + h
                    more = not (last and h == HB - 1)
                    k = pj_base(h)
                    dve.wait_ge(s_full, n + 1)
                    own.link(nc.vector.tensor_tensor(s_sb[:, :, :], S[:, :, :], mask, ALU.add))
                    own.link(nc.vector.tensor_reduce(rmax[:, :], s_sb[:, :, :], AX.X, ALU.max))
                    nc.vector.tensor_tensor(s_sb[:, :, :], s_sb[:, :, :],
                                            rmax[:, :].unsqueeze(2).to_broadcast([P, 2 * NT, SEQ]),
                                            ALU.subtract).then_inc(shifted, 1)
                    dve.wait_ge(exp_done, n + 1)
                    own.link(nc.vector.tensor_reduce(rsum[:, :], s_sb[:, :, :], AX.X, ALU.add))
                    own.link(nc.vector.reciprocal(rsum[:, :], rsum[:, :]))
                    for s in range(2):
                        r = slice(64 * s, 64 * s + 64)
                        ins = nc.vector.tensor_tensor(pbd[r, :, 64 * s:64 * s + 64], s_sb[r, :, :],
                                                      rsum[r, :].unsqueeze(2).to_broadcast([64, 2 * NT, SEQ]),
                                                      ALU.mult)
                    ins.then_inc(pbd_ready, 1)
                    base = it * PJ_BODY + PJ_PRO + 2
                    if more and h % 4 == 3:
                        g = h // 4
                        dve.wait_ge(pj_free, base + k + 2)
                        dve.wait_ge(q_roped, n + 1)
                        rope(kT[:, (g + 1) % 2, :], k_raw[:, :], k_roped)
                        dve.wait_ge(k_roped, it * 2 + g + 2)
                        k += 4
                    if more:
                        dve.wait_ge(pj_free, base + k + 2)
                        dve.wait_ge(q_roped, n + 1)
                        rope(qT[:, (h + 1) % 2, :], q_raw[:, :], q_roped)
                    for j in range(4):
                        if j == 2:
                            if not (last and h >= HB - 2):
                                dve.wait_ge(wt_hi, n + 3)
                                lo_of(w16[:, h % 2, 1], w_raw[:, h % 2], w16[:, h % 2, 0], WS).then_inc(wt_lo, 1)
                            if h % 4 == 1:
                                g = h // 4
                                if not (last and g == 1):
                                    dve.wait_ge(kv_hi, it * 2 + g + 2)
                                    lo_of(kv16[:, 1], kv_raw[:, :], kv16[:, 0], WS).then_inc(kv_lo, 1)
                            if h % 4 in (1, 2):
                                c = slice((h % 4 - 1) * GROUP, (h % 4) * GROUP)
                                dve.wait_ge(o_hi, it * 4 + 2 * (h // 4) + h % 4)
                                lo_of(o16[:, 1, c], o_raw[:, :], o16[:, 0, c], WS).then_inc(o_lo, 1)
                        kt = (h % 4) + GROUP * (j // 2)
                        c = slice((j % 2) * HALF, (j % 2 + 1) * HALF)
                        dve.wait_ge(a_hi, n * 4 + j + 1)
                        lo_of(aT[:, 1, kt, c], OB[j % 2][:, :], aT[:, 0, kt, c], 1.0).then_inc(b_free, 1)
                    if h % 4 == 3:
                        for t in range(NT):
                            dve.wait_ge(b_full, it * B_BODY + b_base(h) + 4 + t + 1)
                            nc.vector.scalar_tensor_tensor(X[:, t, :], OB[t % 2][:, :], 1 / WS, X[:, t, :],
                                                           ALU.mult, ALU.add).then_inc(b_free, 1)
                if last:
                    assert own.n == D_BODY - 6, (own.n, D_BODY)
                else:
                    assert own.n == D_BODY, (own.n, D_BODY)

            with dve.Fori(0, ITERS - 1) as it:
                body(it, False)
            body(ITERS - 1, True)

        @block.tensor
        def _(pe):
            PASSES = ((0, 0), (0, 1), (1, 0))

            def project(out, pairs, done=None):
                n, last = 0, None
                for lhs, rhs in pairs:
                    for a, b in PASSES:
                        last = nc.tensor.matmul(out, lhs(a), rhs(b), start=(n == 0), stop=(n == 3 * len(pairs) - 1))
                        n += 1
                return last

            def head_w(par, i):
                return lambda a: w16[:, par, a, i, :]

            def kv_w(i):
                return lambda a: kv16[:, a, i, :]

            def xt(kt, c, w):
                return lambda b: XT[:, b, kt, c:c + w]

            pe.wait_ge(const_loaded, 16)
            for t in range(NT):
                pe.wait_ge(xn_ready, t + 1)
                if t >= 2:
                    pe.wait_ge(xt_lo, t - 1)
                for c in range(KT):
                    ins = nc.tensor.transpose(TB[t % 2][:, c, :], xn[:, t % 2, c * P:(c + 1) * P], ident)
                ins.then_inc(xt_psum, 1)
            pe.wait_ge(xt_lo, NT)
            pe.wait_ge(wlq_lo, 1)
            for c in range(2):
                project(OB[c][:, :], [(lambda a, i=i: wlq[:, a, i, :], xt(i, c * HALF, HALF)) for i in range(KT)])\
                    .then_inc(lq_psum, 1)

            def step(base, k, emit):
                pe.wait_ge(pj_free, base + k + 1)
                emit(PJ[k % 2]).then_inc(pj_full, 1)

            def feature_major(w, c):
                return lambda out: project(out[:, :], [(w(i), xt(i, c * HALF, HALF)) for i in range(KT)])

            def token_major(w, c):
                def emit(out):
                    for t in range(4):
                        ins = project(out[:, t * HD:(t + 1) * HD],
                                      [(xt(i, (4 * c + t) * P, P), w(i)) for i in range(KT)])
                    return ins
                return emit

            def kv_steps(base, k):
                step(base, k, feature_major(kv_w, 0))
                step(base, k + 1, feature_major(kv_w, 1))
                step(base, k + 2, token_major(lambda i: kv_w(KT + i), 0))
                step(base, k + 3, token_major(lambda i: kv_w(KT + i), 1))

            def q_lk_steps(base, k, par):
                step(base, k, feature_major(lambda i: head_w(par, i), 0))
                step(base, k + 1, feature_major(lambda i: head_w(par, i), 1))
                for c in range(2):
                    step(base, k + 2 + c, lambda out, c=c: project(
                        out[:, :], [(head_w(par, KT), lambda b: LQ[:, b, c * HALF:(c + 1) * HALF])]))

            def lv_step(base, k, par, c):
                step(base, k, token_major(lambda i: head_w(par, KT + 1 + i), c))

            pe.wait_ge(kv_lo, 1)
            kv_steps(0, 0)
            pe.wait_ge(wt_lo, 1)
            pe.wait_ge(lq_lo, 2)
            q_lk_steps(0, 4, 0)
            lv_step(0, 8, 0, 0)
            lv_step(0, 9, 0, 1)

            def body(it, last):
                for h in range(HB):
                    n = it * HB + h
                    g = h // 4
                    par = h % 2
                    more = not (last and h == HB - 1)
                    base = it * PJ_BODY + PJ_PRO
                    k = pj_base(h)
                    pe.wait_ge(k_roped, it * 2 + g + 1)
                    pe.wait_ge(q_roped, n + 1)
                    pe.wait_ge(lk_roped, n + 1)
                    for t in range(NT):
                        for kind, keys in enumerate((kT[:, g % 2, :], lkT[:, par, :])):
                            for s in range(2):
                                c = slice(t * P + 64 * s, t * P + 64 * s + 64)
                                ins = nc.tensor.matmul(S[64 * s:64 * s + 64, 2 * t + kind, :], qT[:, par, c],
                                                       keys[:, c], start=True, stop=True)
                    ins.then_inc(s_full, 1)
                    if more:
                        if h % 4 == 3:
                            pe.wait_ge(kv_lo, it * 2 + g + 2)
                            kv_steps(base, k)
                            k += 4
                        pe.wait_ge(wt_lo, n + 2)
                        q_lk_steps(base, k, 1 - par)
                        lv_step(base, k + 4, 1 - par, 0)
                    pe.wait_ge(pbd_ready, n + 1)
                    for j in range(4):
                        pe.wait_ge(t_free, it * T_BODY + 4 * h + j + 1)
                        for u in range(4):
                            ins = nc.tensor.transpose(TB[j % 2][:, u, :], pbd[:, 4 * j + u, :], ident)
                        ins.then_inc(t_full, 1)
                    for j in range(4):
                        if j == 2 and more:
                            lv_step(base, k + 5, 1 - par, 1)
                        pe.wait_ge(b_free, it * B_BODY + b_base(h) + j + 1)
                        if j < 2:
                            pe.wait_ge(t_free, it * T_BODY + 4 * h + 2 * j + 2 + 2)
                        for t in range(4 * (j % 2), 4 * (j % 2) + 4):
                            vals = v[:, g % 2, t, :] if j < 2 else lv[:, par, t, :]
                            ins = nc.tensor.matmul(OB[j % 2][:, (t % 4) * P:(t % 4 + 1) * P], vals,
                                                   pT[:, 2 * t + j // 2, :], start=True, stop=True)
                        ins.then_inc(b_full, 1)
                    if h % 4 == 3:
                        pe.wait_ge(o_lo, it * 4 + 2 * g + 2)
                        order = [0, GROUP, 1, GROUP + 1, 2, GROUP + 2, 3, GROUP + 3]
                        for t in range(NT):
                            pe.wait_ge(b_free, it * B_BODY + b_base(h) + 4 + max(t, 1) + 1)
                            project(OB[t % 2][:, :], [
                                (lambda a, i=i: aT[:, a, i, t * P:(t + 1) * P],
                                 lambda b, i=i: o16[:, b, i, :]) for i in order]).then_inc(b_full, 1)

            with pe.Fori(0, ITERS - 1) as it:
                body(it, False)
            body(ITERS - 1, True)


def cross_phase(nc, X, const, const_in, ctx_in, ctxT_in, WqT, WkT, Wv, WoT, bo, gain, sem):
    with ExitStack() as stack:
        def sb(name, shape, dt=F32):
            return stack.enter_context(nc.sbuf_tensor(name, shape, dt))

        def ps(name, shape, dt=F32):
            return stack.enter_context(nc.psum_tensor(name, shape, dt))

        CH = SEQ
        XH, XD = 8, 64
        HID = XH * XD
        JT = HID // P
        NN = DM // P
        ident = const[:, C_ID:C_ID + P]
        const_x = sb("x_const", [P, C_END - C_ONES])
        ones2 = const_x[:, 0:32]
        pick2 = const_x[:, 32:32 + P]

        st = sb("x_st", [P, NT, 6])
        mv = sb("x_mv", [P, NT, 2])
        rs = sb("x_rs", [P, NT])
        xn = sb("x_xn", [P, 2, DM])
        ctx_raw = sb("x_ctx", [P, NT, DM])
        XS = sb("x_XS", [P, BATCH, DM], F16)
        CS = sb("x_CS", [P, BATCH, DM], F16)
        w_raw = sb("x_wraw", [P, 2, HID])
        w16 = sb("x_w16", [P, 2, 2, HID], F16)
        wv_sb = sb("x_wv", [64, XH, CH])
        wo_sb = sb("x_wo", [64, XH, CH])
        U = sb("x_U_sb", [64, HID])
        bo_sb = sb("x_bias", [P, 1])
        g_raw = sb("x_graw", [P, 1])
        g8 = sb("x_g8", [P, 1])
        ct = sb("x_ct", [P, 2, NN, CH])
        kmax = sb("x_kmax", [P, 2, JT])
        knmax = sb("x_knmax", [P, 2, JT])
        ksum = sb("x_ksum", [P, 2, JT])
        krec = sb("x_krec", [P, JT])
        ek = sb("x_ek", [P, 2, JT, DM])
        eT = sb("x_eT", [P, NN, HID])
        qmax = sb("x_qmax", [P, NN, XH])
        qsum = sb("x_qsum", [P, 2, NN, XH])
        qs = sb("x_qs", [P, 2, NN, HID])
        qT = sb("x_qT", [P, JT, DM])
        GT = sb("x_GT", [64, HID])
        MT = sb("x_MT", [P, JT, CH])
        y = sb("x_y", [P, NT, DM])
        sq = sb("x_sq", [P, 2, DM])
        root = sb("x_root", [P, 2, DM])
        scaled = sb("x_scaled", [P, 2, DM])

        KB = [ps(f"x_KB{i}", [P, DM]) for i in range(2)]
        QB = [ps(f"x_QB{i}", [P, DM]) for i in range(2)]
        TB = [ps(f"x_TB{i}", [P, 4, P]) for i in range(2)]
        GB = ps("x_GB", [P, DM])
        YB = ps("x_YB", [P, DM])

        names = ("ctx_loaded wqk_loaded wvo_loaded small_loaded own var_ready root_ready xn_ready xs_hi xs_lo cs_hi cs_lo "
                 "wqk_hi wqk_lo u_full u_ready k_full k_free kneg_ready ek_ready q_full q_free q_exp "
                 "qrec_ready q_normed t_full t_free g_full gt_ready m_full mt_ready y_full y_free sq_ready "
                 "ss_full rec_ready bc_full bc_free ssroot_ready const2").split()
        s = {n: sem("x_" + n) for n in names}
        ct_loaded = [sem("x_ct_loaded0"), sem("x_ct_loaded1")]
        block = stack.enter_context(nc.Block())

        @block.sync
        def _(sp):
            sp.dma_start(w_raw[0:64, 0, :], WqT).then_inc(s["wqk_loaded"], 16)
            sp.dma_start(w_raw[64:128, 0, :], WqT).then_inc(s["wqk_loaded"], 16)
            sp.dma_start(w_raw[0:64, 1, :], WkT).then_inc(s["wqk_loaded"], 16)
            sp.dma_start(w_raw[64:128, 1, :], WkT).then_inc(s["wqk_loaded"], 16)
            sp.dma_start(ctx_raw[:, :, :], ctx_in.rearrange("(t p) n -> p t n", p=P)).then_inc(s["ctx_loaded"], 16)
            sp.dma_start(wv_sb[:, :, :], Wv.rearrange("(h e) c -> e h c", e=XD)).then_inc(s["wvo_loaded"], 16)
            sp.dma_start(wo_sb[:, :, :], WoT.rearrange("(h e) c -> e h c", e=XD)).then_inc(s["wvo_loaded"], 16)
            for r in range(2):
                sp.dma_start(bo_sb[64 * r:64 * r + 64, :], bo.rearrange("(c o) -> c o", o=1)).then_inc(s["small_loaded"], 16)
                sp.dma_start(g_raw[64 * r:64 * r + 64, :], gain.rearrange("a c o -> (a c) o")).then_inc(s["small_loaded"], 16)

            sp.dma_start(const_x[:, :], const_in[:, C_ONES:C_END]).then_inc(s["const2"], 16)

            def load_ct(par, b):
                src = ctxT_in[bass.ds(b, 1), :, :].rearrange("o (k p) c -> p (o k) c", p=P)
                sp.dma_start(ct[:, par], src).then_inc(ct_loaded[par], 16)

            load_ct(0, 0)
            load_ct(1, 1)
            with sp.Fori(0, NT - 1) as it:
                for par in range(2):
                    sp.wait_ge(s["g_full"], it * 2 + par + 1)
                    load_ct(par, it * 2 + par + 2)

        @block.scalar
        def _(act):
            def copy(dst, src, scale=1.0):
                return nc.scalar.activation(dst, src, ACT.Copy, scale=scale)

            act.sem_inc(s["k_free"], 2)
            act.sem_inc(s["t_free"], 2)
            act.wait_ge(s["wqk_loaded"], 64)
            copy(w16[:, :, 0, :], w_raw[:, :, :], WS).then_inc(s["wqk_hi"], 1)
            act.wait_ge(s["ctx_loaded"], 16)
            for r in range(2):
                c = slice(64 * r, 64 * r + 64)
                copy(CS[c, r:BATCH:2, :], ctx_raw[c, :, :]).then_inc(s["cs_hi"], 1)
            act.wait_ge(s["u_full"], 1)
            copy(U[:, :], GB[0:64, :]).then_inc(s["u_ready"], 1)
            act.wait_ge(s["var_ready"], 1)
            nc.scalar.activation(rs[:, :], rs[:, :], ACT.Sqrt).then_inc(s["root_ready"], 1)
            for t in range(NT):
                act.wait_ge(s["xn_ready"], t + 1)
                for r in range(2):
                    c = slice(64 * r, 64 * r + 64)
                    copy(XS[c, 2 * t + r, :], xn[c, t % 2, :]).then_inc(s["xs_hi"], 1)

            def k_exp(n, par, j):
                act.wait_ge(s["kneg_ready"], n * JT + j + 1)
                nc.scalar.activation(ek[:, par, j, :], KB[j % 2][:, :], ACT.Exp, scale=1 / WS,
                                     bias=knmax[:, par, j:j + 1],
                                     accum_out=ksum[:, par, j:j + 1]).then_inc(s["k_free"], 1)

            def q_exp(n, par, half):
                act.wait_ge(s["q_free"], n * NN + 2 * half + 2 + 2)
                c = slice(2 * half, 2 * half + 2)
                nc.scalar.activation(qs[:, par, c, :], qs[:, par, c, :], ACT.Exp, scale=1 / WS)\
                    .then_inc(s["q_exp"], 1)

            def transposed(n, k, dst):
                act.wait_ge(s["t_full"], n * 8 + k + 1)
                copy(dst, TB[k % 2][:, :, :]).then_inc(s["t_free"], 1)

            for j in range(JT):
                k_exp(0, 0, j)
            for half in range(2):
                q_exp(0, 0, half)

            def body(it, last):
                for par in range(2):
                    n = it * 2 + par
                    more = not (last and par == 1)
                    if more:
                        k_exp(n + 1, 1 - par, 0)
                        k_exp(n + 1, 1 - par, 1)
                    for k in range(4):
                        transposed(n, k, eT[:, k, :].rearrange("p (a b) -> p a b", b=P))
                    if more:
                        q_exp(n + 1, 1 - par, 0)
                        k_exp(n + 1, 1 - par, 2)
                        k_exp(n + 1, 1 - par, 3)
                    act.wait_ge(s["g_full"], n + 1)
                    copy(GT[:, :], GB[0:64, :]).then_inc(s["gt_ready"], 1)
                    for k in range(4):
                        transposed(n, 4 + k, qT[:, k, :].rearrange("p (a b) -> p a b", b=P))
                    if more:
                        q_exp(n + 1, 1 - par, 1)

            with act.Fori(0, NT - 1) as it:
                body(it, False)
            body(NT - 1, True)
            for t in range(NT):
                act.wait_ge(s["y_free"], NT + 1)
                if t >= 2:
                    act.wait_ge(s["ss_full"], t - 1)
                nc.scalar.activation(sq[:, t % 2, :], y[:, t, :], ACT.Square).then_inc(s["sq_ready"], 1)
            act.wait_ge(s["ss_full"], NT)
            for i, bank in enumerate((KB[0], QB[0])):
                nc.scalar.activation(root[:, i, :], bank[:, :], ACT.Sqrt).then_inc(s["ssroot_ready"], 1)

        @block.gpsimd
        def _(pool):
            def norm(n, par, half):
                pool.wait_ge(s["qrec_ready"], n * 2 + half + 1)
                c = slice(2 * half, 2 * half + 2)
                v3 = qs[:, par, c, :].rearrange("p a (h d) -> p (a h) d", d=XD)
                r3 = qsum[:, par, c, :].rearrange("p a h -> p (a h)").unsqueeze(2).to_broadcast([P, 2 * XH, XD])
                nc.gpsimd.tensor_tensor(v3, v3, r3, ALU.mult).then_inc(s["q_normed"], 1)

            norm(0, 0, 0)
            norm(0, 0, 1)

            def body(it, last):
                for par in range(2):
                    if not (last and par == 1):
                        norm(it * 2 + par + 1, 1 - par, 0)
                        norm(it * 2 + par + 1, 1 - par, 1)

            with pool.Fori(0, NT - 1) as it:
                body(it, False)
            body(NT - 1, True)

        @block.vector
        def _(dve):
            own = Chain(dve, s["own"])
            dve.sem_inc(s["q_free"], 2)
            dve.sem_inc(s["y_free"], 1)
            dve.sem_inc(s["mt_ready"], 1)
            dve.sem_inc(s["bc_free"], 2)
            ins = layernorm_stats(dve, own, nc, X, st, mv, rs)
            ins.then_inc(s["var_ready"], 1)
            dve.wait_ge(s["wqk_hi"], 1)
            nc.vector.scalar_tensor_tensor(w16[:, :, 1, :], w_raw[:, :, :], WS, w16[:, :, 0, :],
                                           ALU.mult, ALU.subtract).then_inc(s["wqk_lo"], 1)
            for r in range(2):
                a, b = slice(64 * r, 64 * r + 64), slice(64 - 64 * r, 128 - 64 * r)
                dve.wait_ge(s["cs_hi"], r + 1)
                nc.vector.tensor_tensor(CS[b, r:BATCH:2, :], ctx_raw[a, :, :], CS[a, r:BATCH:2, :],
                                        ALU.subtract).then_inc(s["cs_lo"], 1)
            dve.wait_ge(s["small_loaded"], 64)
            own.link(nc.vector.tensor_scalar(g8[:, :], g_raw[:, :], float(np.sqrt(CH)), None, ALU.mult))
            dve.wait_ge(s["root_ready"], 1)
            own.link(nc.vector.reciprocal(rs[:, :], rs[:, :]))
            for t in range(NT):
                if t >= 2:
                    dve.wait_ge(s["xs_lo"], 2 * (t - 1))
                    dve.wait_ge(s["xs_hi"], 2 * (t - 1))
                nc.vector.tensor_scalar(xn[:, t % 2, :], X[:, t, :], mv[:, t, 0:1], rs[:, t:t + 1],
                                        ALU.subtract, ALU.mult).then_inc(s["xn_ready"], 1)
                dve.wait_ge(s["xn_ready"], t + 1)
                for r in range(2):
                    a, b = slice(64 * r, 64 * r + 64), slice(64 - 64 * r, 128 - 64 * r)
                    dve.wait_ge(s["xs_hi"], 2 * t + r + 1)
                    nc.vector.tensor_tensor(XS[b, 2 * t + r, :], xn[a, t % 2, :], XS[a, 2 * t + r, :],
                                            ALU.subtract).then_inc(s["xs_lo"], 1)

            def k_max(n, par, j):
                dve.wait_ge(s["k_full"], n * JT + j + 1)
                own.link(nc.vector.tensor_reduce(kmax[:, par, j:j + 1], KB[j % 2][:, :], AX.X, ALU.max))
                nc.vector.tensor_scalar(knmax[:, par, j:j + 1], kmax[:, par, j:j + 1], -1 / WS, None,
                                        ALU.mult).then_inc(s["kneg_ready"], 1)

            def q_shift(n, par, i):
                dve.wait_ge(s["q_full"], n * NN + i + 1)
                v3 = QB[i % 2][:, :].rearrange("p (h d) -> p h d", d=XD)
                own.link(nc.vector.tensor_reduce(qmax[:, i, :], v3, AX.X, ALU.max))
                nc.vector.tensor_tensor(qs[:, par, i, :].rearrange("p (h d) -> p h d", d=XD), v3,
                                        qmax[:, i, :].unsqueeze(2).to_broadcast([P, XH, XD]),
                                        ALU.subtract).then_inc(s["q_free"], 1)

            def q_sum(n, par, half):
                dve.wait_ge(s["q_exp"], n * 2 + half + 1)
                c = slice(2 * half, 2 * half + 2)
                v3 = qs[:, par, c, :].rearrange("p a (h d) -> p (a h) d", d=XD)
                r2 = qsum[:, par, c, :].rearrange("p a h -> p (a h)")
                own.link(nc.vector.tensor_reduce(r2, v3, AX.X, ALU.add))
                nc.vector.reciprocal(r2, r2).then_inc(s["qrec_ready"], 1)

            for j in range(JT):
                k_max(0, 0, j)
            for i in range(NN):
                q_shift(0, 0, i)
                if i % 2:
                    q_sum(0, 0, i // 2)
            PRO = own.n
            BODY = 2 * (JT + NN + 2) + 2 * 2

            def body(it, last):
                own.enter(PRO, it, BODY)
                for par in range(2):
                    n = it * 2 + par
                    more = not (last and par == 1)
                    if more:
                        k_max(n + 1, 1 - par, 0)
                        k_max(n + 1, 1 - par, 1)
                        q_shift(n + 1, 1 - par, 0)
                        q_shift(n + 1, 1 - par, 1)
                        k_max(n + 1, 1 - par, 2)
                        k_max(n + 1, 1 - par, 3)
                        q_sum(n + 1, 1 - par, 0)
                        q_shift(n + 1, 1 - par, 2)
                        q_shift(n + 1, 1 - par, 3)
                    dve.wait_ge(s["k_free"], n * JT + JT + 2)
                    own.link(nc.vector.reciprocal(krec[:, :], ksum[:, par, :]))
                    own.link(nc.vector.tensor_scalar(krec[:, :], krec[:, :], XD ** -0.5, None, ALU.mult))
                    dve.wait_ge(s["m_full"], n + 1)
                    for r in range(2):
                        c = slice(64 * r, 64 * r + 64)
                        ins = nc.vector.tensor_tensor(
                            MT[c, :, :], GB[c, :].rearrange("p (j a o) -> p j a o", a=2, o=CH)[:, :, r, :],
                            krec[c, :].unsqueeze(2).to_broadcast([64, JT, CH]), ALU.mult)
                    ins.then_inc(s["mt_ready"], 1)
                    if more:
                        q_sum(n + 1, 1 - par, 1)
                dve.wait_ge(s["y_full"], it + 1)
                yt = y[:, bass.ds(it, 1), :].rearrange("p o n -> p (o n)")
                nc.vector.tensor_scalar(yt, YB[:, :], bo_sb[:, :], None, ALU.add).then_inc(s["y_free"], 1)
                if not last:
                    assert own.n == BODY, (own.n, BODY)

            with dve.Fori(0, NT - 1) as it:
                body(it, False)
            body(NT - 1, True)
            for i in range(2):
                dve.wait_ge(s["ssroot_ready"], i + 1)
                own.link(nc.vector.tensor_scalar(root[:, i, :], root[:, i, :], 1e-12, None, ALU.max))
                nc.vector.reciprocal(root[:, i, :], root[:, i, :]).then_inc(s["rec_ready"], 1)
            for t in range(NT):
                dve.wait_ge(s["bc_full"], t + 1)
                ins = nc.vector.scalar_tensor_tensor(scaled[:, t % 2, :], y[:, t, :], g8[:, :], TB_flat(TB[t % 2]),
                                                     ALU.mult, ALU.mult)
                ins.then_inc(s["bc_free"], 1)
                dve.wait_ge(s["bc_free"], t + 3)
                own.mark(nc.vector.tensor_tensor(X[:, t, :], X[:, t, :], scaled[:, t % 2, :], ALU.add))
            own.wait()

        @block.tensor
        def _(pe):
            pe.wait_ge(s["wvo_loaded"], 32)
            for h in range(XH):
                ins = nc.tensor.matmul(GB[0:64, h * CH:(h + 1) * CH], wv_sb[:, h, :], wo_sb[:, h, :],
                                       start=True, stop=True)
            ins.then_inc(s["u_full"], 1)
            pe.wait_ge(s["wqk_lo"], 1)
            pe.wait_ge(s["cs_lo"], 2)
            pe.wait_ge(s["u_ready"], 1)

            def k_proj(n, j):
                pe.wait_ge(s["k_free"], n * JT + j + 1)
                mov = CS[:, bass.ds(n, 1), :].rearrange("p o n -> p (o n)")
                for a in range(2):
                    ins = nc.tensor.matmul(KB[j % 2][:, :], w16[:, 1, a, j * P:(j + 1) * P], mov,
                                           start=(a == 0), stop=(a == 1))
                ins.then_inc(s["k_full"], 1)

            def q_proj(n, i):
                pe.wait_ge(s["q_free"], n * NN + i + 1)
                stat = XS[:, bass.ds(n, 1), i * P:(i + 1) * P].rearrange("p o n -> p (o n)")
                for a in range(2):
                    ins = nc.tensor.matmul(QB[i % 2][:, :], stat, w16[:, 0, a, :], start=(a == 0), stop=(a == 1))
                ins.then_inc(s["q_full"], 1)

            def k_transposes(n, par, k):
                pe.wait_ge(s["t_free"], n * 8 + k + 1)
                for j in range(JT):
                    ins = nc.tensor.transpose(TB[k % 2][:, j, :], ek[:, par, j, k * P:(k + 1) * P], ident)
                ins.then_inc(s["t_full"], 1)

            def q_transposes(n, par, k):
                pe.wait_ge(s["t_free"], n * 8 + 4 + k + 1)
                for i in range(NN):
                    ins = nc.tensor.transpose(TB[k % 2][:, i, :], qs[:, par, i, k * P:(k + 1) * P], ident)
                ins.then_inc(s["t_full"], 1)

            for j in range(JT):
                k_proj(0, j)
            pe.wait_ge(s["xs_lo"], 2 * NT)
            for i in range(NN):
                q_proj(0, i)

            def body(it, last):
                for par in range(2):
                    n = it * 2 + par
                    more = not (last and par == 1)
                    if more:
                        k_proj(n + 1, 0)
                        k_proj(n + 1, 1)
                        q_proj(n + 1, 0)
                        q_proj(n + 1, 1)
                    pe.wait_ge(s["k_free"], n * JT + JT + 2)
                    for k in range(NN):
                        k_transposes(n, par, k)
                    if more:
                        k_proj(n + 1, 2)
                        k_proj(n + 1, 3)
                        q_proj(n + 1, 2)
                        q_proj(n + 1, 3)
                    pe.wait_ge(s["t_free"], n * 8 + 4 + 2)
                    pe.wait_ge(ct_loaded[par], (it + 1) * 16)
                    pe.wait_ge(s["mt_ready"], n + 1)
                    for k in range(NN):
                        ins = nc.tensor.matmul(GB[0:64, :], ct[:, par, k, :], eT[:, k, :],
                                               start=(k == 0), stop=(k == NN - 1))
                    ins.then_inc(s["g_full"], 1)
                    pe.wait_ge(s["q_normed"], n * 2 + 2)
                    q_transposes(n, par, 0)
                    q_transposes(n, par, 1)
                    pe.wait_ge(s["gt_ready"], n + 1)
                    for j in range(JT):
                        ins = nc.tensor.matmul(GB[:, j * P:(j + 1) * P], GT[:, j * P:(j + 1) * P],
                                               U[:, j * P:(j + 1) * P], start=True, stop=True)
                    ins.then_inc(s["m_full"], 1)
                    q_transposes(n, par, 2)
                    q_transposes(n, par, 3)
                    pe.wait_ge(s["mt_ready"], n + 2)
                    pe.wait_ge(s["t_free"], n * 8 + 8 + 2)
                    if par == 0:
                        pe.wait_ge(s["y_free"], it + 1)
                    for j in range(JT):
                        ins = nc.tensor.matmul(YB[64 * par:64 * par + 64, :], MT[:, j, :], qT[:, j, :],
                                               start=(j == 0), stop=(j == JT - 1))
                ins.then_inc(s["y_full"], 1)

            with pe.Fori(0, NT - 1) as it:
                body(it, False)
            body(NT - 1, True)
            pe.wait_ge(s["const2"], 16)
            for t in range(NT):
                pe.wait_ge(s["sq_ready"], t + 1)
                r = 32 * (t % 4)
                nc.tensor.matmul((KB[0], QB[0])[t // 4][r:r + 32, :], ones2, sq[:, t % 2, :],
                                 start=True, stop=True).then_inc(s["ss_full"], 1)
            for t in range(NT):
                pe.wait_ge(s["rec_ready"], t // 4 + 1)
                pe.wait_ge(s["bc_free"], t + 1)
                r = 32 * (t % 4)
                nc.tensor.matmul(TB_flat(TB[t % 2]), pick2[r:r + 32, :], root[r:r + 32, t // 4, :],
                                 start=True, stop=True).then_inc(s["bc_full"], 1)


def TB_flat(t):
    return t[:, :, :].rearrange("p a b -> p (a b)")


FF = 1376
FT = -(-FF // P)
QB16 = 16
SPLIT = 128
FP8_MAX = 448.0
GSCALE = 448.0 * 6.0
TINY = 1e-8
ROUND = 1.5 * 2.0 ** 23
R4 = 1.5 * 2.0 ** 20
EXPONENT = 0x7F800000
RMAX = bass.bass_isa.ReduceOp.max


def rows_of(i):
    return min(P, FF - i * P)


def blocks(ap):
    return ap.rearrange("p (b e) -> p b e", e=QB16)


def spread(scales, parts, n):
    return scales.unsqueeze(2).to_broadcast([parts, n, QB16])


def weight_phase(nc, const, w16, wd16, wT, wdT, scratch, ri_in_cols, ri_mid_cols, ri_mid_last, sem):
    with ExitStack() as stack:
        def sb(name, shape, dt=F32):
            return stack.enter_context(nc.sbuf_tensor(name, shape, dt))

        def ps(name, shape, dt=F32):
            return stack.enter_context(nc.psum_tensor(name, shape, dt))

        RING = 3
        ident = const[:, C_ID:C_ID + P]
        ident16 = sb("p_ident16", [P, P], F16)
        idx_in = sb("p_idx_in", [P, KT], I32)
        idx_mid = sb("p_idx_mid", [P, FT], I32)
        gathered = sb("p_gathered", [P, 2, FT * DM])
        halves = [gathered[:, m, :].bitcast(F16).rearrange("p (i a k) -> p i a k", i=FT, a=2) for m in range(2)]
        down = sb("p_down", [P, FT, DM])
        down16 = sb("p_down16", [P, 2, KT, FF], F16)
        amax = sb("p_amax", [P, 2, 32])
        scale = sb("p_scale", [P, 2, 32])
        rec = sb("p_rec", [P, 2, 32])
        ratio = sb("p_ratio", [P, RING, DM])
        quant = sb("p_quant", [P, RING, DM])
        rows16 = sb("p_rows16", [P, 4, 2, DM], F16)
        AB = [ps(f"p_AB{i}", [P, DM]) for i in range(4)]
        BB = [ps(f"p_BB{i}", [P, 2, KT, P], F16) for i in range(4)]

        idx_loaded, g_in, g_down = sem("p_idx_loaded"), [sem("p_g_in0"), sem("p_g_in1")], sem("p_g_down")
        stored = [[sem(f"p_stored{m}{r}") for r in range(4)] for m in range(2)]
        g_mid = [sem("p_g_mid0"), sem("p_g_mid1")]
        a_full, a_read, rounded, q_ready, own_sem = (sem("p_a_full"), sem("p_a_read"), sem("p_rounded"),
                                                     sem("p_q_ready"), sem("p_own"))
        hi_ready, lo_ready, id_ready = sem("p_hi_ready"), sem("p_lo_ready"), sem("p_id_ready")
        b_full, b_act, b_dve = sem("p_b_full"), sem("p_b_act"), sem("p_b_dve")
        ROWS = [(m, i) for m in range(2) for i in range(FT)]
        DOWN = [(o, c) for c in range(3) for o in range(KT)]
        NR, NQ = len(ROWS), len(ROWS) + len(DOWN)
        BACK = [(0, i) for i in range(FT)] + [(m, i) for i in range(FT) for m in (2, 1)]
        BACK_FROM = NR + 5

        def back_after(j):
            if j < BACK_FROM:
                return range(0)
            return range(min(2 * (j - BACK_FROM), FT), min(2 * (j - BACK_FROM) + 2, FT))

        assert back_after(NQ - 1).stop == FT
        TAIL = range(FT, len(BACK))

        def shape_of(j):
            if j < NR:
                n = rows_of(ROWS[j][1])
                return n, DM, [rows16[0:n, j % 4, a, :] for a in range(2)]
            o, c = DOWN[j - NR]
            w = min(512, FF - 512 * c)
            return P, w, [down16[:, a, o, 512 * c:512 * c + w] for a in range(2)]

        def stores_before(m, r, j):
            return len([1 for q in range(min(j, NR)) if ROWS[q][0] == m and q % 4 == r])

        def back_banks(b):
            m, i = BACK[b]
            n = rows_of(i)
            if m < 2:
                return BB[b % 4][:, :, :, 0:n], w16[:, m, :, :, i * P:i * P + n]
            return (BB[b % 4][0:n].rearrange("p a k c -> p a (k c)"), wd16[0:n, :, i, :])

        block = stack.enter_context(nc.Block())

        @block.gpsimd
        def _(pool):
            pool.dma_start(idx_in[:, :], ri_in_cols).then_inc(idx_loaded, 16)
            pool.dma_start(idx_mid[:, 0:FT - 1], ri_mid_cols).then_inc(idx_loaded, 16)
            pool.dma_start(idx_mid[0:rows_of(FT - 1), FT - 1:FT], ri_mid_last).then_inc(idx_loaded, 16)
            pool.wait_ge(idx_loaded, 48)
            for m in range(2):
                for k in range(KT):
                    pool.indirect_dma_start(
                        out=gathered[:, m, k * FF:(k + 1) * FF], out_offset=None, in_=wT[m][:, :],
                        in_offset=bass.IndirectOffsetOnAxis(ap=idx_in[:, k:k + 1], axis=0)).then_inc(g_in[m], 16)
            for i in range(FT):
                n = rows_of(i)
                pool.indirect_dma_start(
                    out=down[0:n, i, :], out_offset=None, in_=wdT[:, :],
                    in_offset=bass.IndirectOffsetOnAxis(ap=idx_mid[0:n, i:i + 1], axis=0)).then_inc(g_down, 16)

            def gather_halves(m, i):
                if i == 0:
                    for r in range(4):
                        pool.wait_ge(stored[m][r], 16 * stores_before(m, r, NR))
                    pool.wait_ge(a_full, (m + 1) * FT)
                n = rows_of(i)
                pool.indirect_dma_start(
                    out=halves[m][0:n, i].rearrange("p a k -> p (a k)"), out_offset=None, in_=scratch[m][:, :],
                    in_offset=bass.IndirectOffsetOnAxis(ap=idx_mid[0:n, i:i + 1], axis=0)).then_inc(g_mid[m], 16)

            for j in range(NQ):
                n, w, dst = shape_of(j)
                pool.wait_ge(hi_ready, j + 1)
                nc.gpsimd.tensor_tensor(dst[1], quant[0:n, j % RING, 0:w], dst[0], ALU.subtract).then_inc(lo_ready, 1)
                if FT + 2 <= j < 2 * FT + 2:
                    gather_halves(0, j - FT - 2)
                elif NR + 2 <= j < NQ:
                    gather_halves(1, j - NR - 2)
            gather_halves(1, FT - 1)

        @block.sync
        def _(sp):
            for j, (m, i) in enumerate(ROWS):
                n = rows_of(i)
                sp.wait_ge(lo_ready, j + 1)
                sp.dma_start(scratch[m][i * P:i * P + n, :], rows16[0:n, j % 4].rearrange("p a k -> p (a k)"))\
                    .then_inc(stored[m][j % 4], 16)

        @block.tensor
        def _(pe):
            def back(b):
                m, i = BACK[b]
                n = rows_of(i)
                if b == 0:
                    pe.wait_ge(id_ready, 1)
                    pe.wait_ge(g_mid[0], 16 * FT)
                if m == 1 and i == 0:
                    pe.wait_ge(g_mid[1], 16 * FT)
                if m == 2 and i == 0:
                    pe.wait_ge(lo_ready, NQ)
                if b >= 4:
                    pe.wait_ge(b_dve if b % 2 else b_act, (b - 4) // 2 + 1)
                for a in range(2):
                    for k in range(KT):
                        if m < 2:
                            ins = nc.tensor.transpose(BB[b % 4][:, a, k, 0:n], halves[m][0:n, i, a, k * P:(k + 1) * P],
                                                      ident16[0:n, 0:n])
                        else:
                            ins = nc.tensor.transpose(BB[b % 4][0:n, a, k, :], down16[:, a, k, i * P:i * P + n],
                                                      ident16[:, :])
                ins.then_inc(b_full, 1)

            for j in range(NQ):
                if j >= 4:
                    pe.wait_ge(a_read, j - 3)
                if j < NR:
                    m, i = ROWS[j]
                    n = rows_of(i)
                    pe.wait_ge(g_in[m], 16 * KT)
                    for k in range(KT):
                        ins = nc.tensor.transpose(AB[j % 4][0:n, k * P:(k + 1) * P],
                                                  gathered[:, m, k * FF + i * P:k * FF + i * P + n], ident)
                else:
                    o, c = DOWN[j - NR]
                    pe.wait_ge(g_down, 16 * FT)
                    for i in range(4 * c, min(4 * c + 4, FT)):
                        n = rows_of(i)
                        ins = nc.tensor.transpose(AB[j % 4][:, (i - 4 * c) * P:(i - 4 * c) * P + n],
                                                  down[0:n, i, o * P:(o + 1) * P], ident[0:n, 0:n])
                ins.then_inc(a_full, 1)
                for b in back_after(j):
                    back(b)
            for b in TAIL:
                back(b)

        @block.scalar
        def _(act):
            nc.scalar.activation(ident16[:, :], ident, ACT.Copy).then_inc(id_ready, 1)

            def high(j):
                n, w, dst = shape_of(j)
                act.wait_ge(q_ready, j + 1)
                if 4 <= j < NR + 4 and j < NR:
                    m = ROWS[j - 4][0]
                    act.wait_ge(stored[m][j % 4], 16 * stores_before(m, j % 4, j - 3))
                nc.scalar.activation(dst[0], quant[0:n, j % RING, 0:w], ACT.Copy).then_inc(hi_ready, 1)

            def back(b):
                if b % 2 == 0:
                    bank, dst = back_banks(b)
                    act.wait_ge(b_full, b + 1)
                    nc.scalar.activation(dst, bank, ACT.Copy).then_inc(b_act, 1)

            for j in range(NQ):
                n, w, dst = shape_of(j)
                act.wait_ge(a_read, j + 1)
                r = ratio[0:n, j % RING, 0:w]
                nc.scalar.activation(r, r, ACT.Copy, scale=WS, bias=ROUND).then_inc(rounded, 1)
                if j >= 1:
                    high(j - 1)
                for b in back_after(j):
                    back(b)
            high(NQ - 1)
            for b in TAIL:
                back(b)

        @block.vector
        def _(dve):
            own = Chain(dve, own_sem)

            def ratios(j):
                n, w, dst = shape_of(j)
                nb = w // QB16
                bank = blocks(AB[j % 4][0:n, 0:w])
                dve.wait_ge(a_full, j + 1)
                own.link(nc.vector.tensor_reduce(amax[0:n, j % 2, 0:nb], bank, AX.X, ALU.max,
                                                 apply_absolute_value=True))
                own.link(nc.vector.tensor_scalar(scale[0:n, j % 2, 0:nb], amax[0:n, j % 2, 0:nb], WS / 7.0, WS * TINY,
                                                 ALU.mult, ALU.max))
                own.link(nc.vector.reciprocal(rec[0:n, j % 2, 0:nb], scale[0:n, j % 2, 0:nb]))
                nc.vector.tensor_tensor(blocks(ratio[0:n, j % RING, 0:w]), bank, spread(rec[0:n, j % 2, 0:nb], n, nb),
                                        ALU.mult).then_inc(a_read, 1)

            def products(j):
                n, w, dst = shape_of(j)
                nb = w // QB16
                dve.wait_ge(rounded, j + 1)
                if j >= RING:
                    dve.wait_ge(lo_ready, j - RING + 1)
                nc.vector.scalar_tensor_tensor(blocks(quant[0:n, j % RING, 0:w]), blocks(ratio[0:n, j % RING, 0:w]),
                                               ROUND, spread(scale[0:n, j % 2, 0:nb], n, nb),
                                               ALU.subtract, ALU.mult).then_inc(q_ready, 1)

            def back(b):
                if b % 2:
                    bank, dst = back_banks(b)
                    dve.wait_ge(b_full, b + 1)
                    nc.vector.tensor_copy(dst, bank).then_inc(b_dve, 1)

            for j in range(NQ):
                if j >= 3:
                    dve.wait_ge(q_ready, j - 1)
                ratios(j)
                if j >= 1:
                    products(j - 1)
                for b in back_after(j):
                    back(b)
            products(NQ - 1)
            for b in TAIL:
                back(b)


def round_fp8(nc, own, y, m):
    own.link(nc.vector.tensor_scalar(m.bitcast(I32), y.bitcast(I32), EXPONENT, None, ALU.bitwise_and))
    own.link(nc.vector.tensor_scalar(m, m, 2.0 ** -6, R4, ALU.max, ALU.mult))
    own.link(nc.vector.tensor_tensor(y, y, m, ALU.add))
    own.link(nc.vector.tensor_tensor(y, y, m, ALU.subtract))


def transposed_parts(c):
        return [(P, 4, 4 * c)] if c < 2 else [(P, FT - 9, 8), (rows_of(FT - 1), 1, FT - 1)]


def feed_forward_phase(nc, X, const, const_in, w16, wd16, ri_in, out, sem):
    with ExitStack() as stack:
        def sb(name, shape, dt=F32):
            return stack.enter_context(nc.sbuf_tensor(name, shape, dt))

        def ps(name, shape, dt=F32):
            return stack.enter_context(nc.psum_tensor(name, shape, dt))

        ident = const[:, C_ID:C_ID + P]
        NB = DM // QB16
        NBH = FF // QB16
        ON = (DM - SPLIT) // QB16
        OH = (FF - SPLIT) // QB16
        CW = 344
        NC = FF // CW
        assert NC * CW == FF

        st = sb("f_st", [P, NT, 6])
        mv = sb("f_mv", [P, NT, 2])
        rs = sb("f_rs", [P, NT])
        iota = sb("f_iota", [P, KT])
        ri_raw = sb("f_ri", [P, DM], I32)
        rif = sb("f_rif", [P, DM])
        hot = sb("f_hot", [P, KT, DM])
        xn = sb("f_xn", [P, 2, DM])
        gmax = sb("f_gmax", [P, NT])
        g1 = sb("f_g1", [P, 1])
        gall = sb("f_gall", [P, 1])
        floor = sb("f_floor", [P, 1])
        amax = sb("f_amax", [P, NB])
        scale = sb("f_scale", [P, NB])
        rec = sb("f_rec", [P, NB])
        xq = sb("f_xq", [P, DM])
        mm = sb("f_mm", [P, FF])
        m2 = sb("f_m2", [P, SPLIT])
        A16 = sb("f_A16", [P, 2, KT, TOK], F16)
        th = sb("f_th", [P, 2, CW])
        gate = sb("f_gate", [P, 2, CW])
        H = sb("f_H", [P, NT, FF])
        xT = [H[:, t, 0:DM].rearrange("p (k c) -> p k c", c=P) for t in range(NT)]
        XP = slice(DM, 2 * DM)
        hmax = sb("f_hmax", [P, NT, NBH])
        h1 = sb("f_h1", [P, 1])
        hall = sb("f_hall", [P, 1])
        hfloor = sb("f_hfloor", [P, 1])
        gm = sb("f_gm", [P, 3])
        hs = sb("f_hs", [P, 3, NT, NBH])
        h_split = sb("f_h_split", [P, NT, SPLIT])
        o_amax = sb("f_o_amax", [P, 3, SPLIT // QB16])
        res = sb("f_res", [P, SPLIT])
        hq = sb("f_hq", [P, FF])
        hT = sb("f_hT", [P, 2, FT, P], F16)
        WP = 32 * QB16

        TB = [ps(f"f_TB{i}", [P, 4, P]) for i in range(3)]
        GA = [ps(f"f_GA{i}", [P, DM]) for i in range(2)]
        UA = [ps(f"f_UA{i}", [P, DM]) for i in range(2)]
        YB = ps("f_YB", [P, DM])

        names = ("idx const own var_ready root_ready xn_ready xt_full xt_ready xp_full xp_read gmax_ready gall_ready "
                 "aq_ready at_full a_hi a_lo gu_full th_ready gu_free hmax_ready hall_ready hq_ready ht_full ht_hi "
                 "ht_lo y_full y_read y_stored max_ready scales_ready y8_ready m_ready hp_ready pool_own").split()
        s = {n: sem("f_" + n) for n in names}
        block = stack.enter_context(nc.Block())

        @block.sync
        def _(sp):
            sp.dma_start(ri_raw[:, :], ri_in.rearrange("(o n) -> o n", o=1).to_broadcast([P, DM])).then_inc(s["idx"], 16)
            sp.dma_start(iota[:, :], const_in[:, C_IOTA:C_IOTA + KT]).then_inc(s["const"], 16)
            with sp.Fori(0, NT) as t:
                sp.wait_ge(s["y_read"], t + 1)
                sp.dma_start(out[bass.ts(t, P), :], X[:, bass.ds(t, 1), :].rearrange("p o n -> p (o n)"))\
                    .then_inc(s["y_stored"], 16)
            sp.wait_ge(s["y_stored"], 16 * NT)

        @block.gpsimd
        def _(pool):
            pool.wait_ge(s["gmax_ready"], 1)
            nc.gpsimd.partition_all_reduce(gall[:, :], g1[:, :], P, RMAX).then_inc(s["gall_ready"], 1)
            pool.wait_ge(s["hmax_ready"], 1)
            nc.gpsimd.partition_all_reduce(hall[:, :], h1[:, :], P, RMAX).then_inc(s["hall_ready"], 1)
            own = Chain(pool, s["pool_own"])

            def over_scale(t):
                hb = H[:, bass.ds(t, 1), :].rearrange("p o (b e) -> p (o b) e", e=QB16)
                nc.gpsimd.tensor_tensor(hb, hb, spread(row(hs[:, 1, bass.ds(t, 1), :]), P, NBH), ALU.mult)\
                    .then_inc(s["y8_ready"], 1)

            def body(t, last):
                if not last:
                    over_scale(t + 1)
                pool.wait_ge(s["m_ready"], t + 1)
                h = row(H[:, bass.ds(t, 1), 0:WP])
                own.link(nc.gpsimd.tensor_tensor(h, h, mm[:, 0:WP], ALU.add))
                own.link(nc.gpsimd.tensor_tensor(h, h, mm[:, 0:WP], ALU.subtract))
                if t >= 1:
                    pool.wait_ge(s["ht_full"], t * 3)
                hb = H[:, bass.ds(t, 1), 0:WP].rearrange("p o (b e) -> p (o b) e", e=QB16)
                nc.gpsimd.tensor_tensor(blocks(hq[:, 0:WP]), hb,
                                        spread(row(hs[:, 2, bass.ds(t, 1), 0:WP // QB16]), P, WP // QB16),
                                        ALU.mult).then_inc(s["hp_ready"], 1)

            pool.wait_ge(s["scales_ready"], 1)
            over_scale(0)
            for t in range(NT):
                body(t, t == NT - 1)

        @block.scalar
        def _(act):
            def copy(dst, src, scale=1.0):
                return nc.scalar.activation(dst, src, ACT.Copy, scale=scale)

            act.wait_ge(s["var_ready"], 1)
            nc.scalar.activation(rs[:, :], rs[:, :], ACT.Sqrt).then_inc(s["root_ready"], 1)
            for t in range(NT):
                act.wait_ge(s["xt_full"], t + 1)
                copy(xT[t], TB[t % 2][:, :, :]).then_inc(s["xt_ready"], 1)
            for t in range(NT):
                act.wait_ge(s["xp_full"], t + 1)
                copy(H[:, t, XP], GA[t % 2][:, :]).then_inc(s["xp_read"], 1)

            def high(t):
                act.wait_ge(s["at_full"], t + 1)
                copy(A16[:, 0, :, bass.ts(t, P)], TB[0][:, :, :]).then_inc(s["a_hi"], 1)

            def body(t, last):
                for c in range(NC):
                    if c == NC - 1 and not last:
                        high(t + 1)
                    act.wait_ge(s["gu_full"], t * NC + c + 1)
                    nc.scalar.activation(th[:, c % 2, :], GA[c % 2][:, 0:CW], ACT.Tanh, scale=0.5 / WS)\
                        .then_inc(s["th_ready"], 1)

            high(0)
            with act.Fori(0, NT - 1) as t:
                body(t, False)
            body(NT - 1, True)
            with act.Fori(0, NT) as t:
                for c in range(3):
                    act.wait_ge(s["ht_full"], t * 3 + c + 1)
                    for n, w, lo in transposed_parts(c):
                        ins = copy(hT[0:n, 0, lo:lo + w, :], TB[c][0:n, lo - 4 * c:lo - 4 * c + w, :])
                    ins.then_inc(s["ht_hi"], 1)

        @block.vector
        def _(dve):
            own = Chain(dve, s["own"])
            dve.sem_inc(s["gu_free"], 2)
            ins = layernorm_stats(dve, own, nc, X, st, mv, rs)
            ins.then_inc(s["var_ready"], 1)
            dve.wait_ge(s["idx"], 16)
            dve.wait_ge(s["const"], 16)
            own.link(nc.vector.tensor_copy(rif[:, :], ri_raw[:, :]))
            for k in range(KT):
                own.mark(nc.vector.tensor_scalar(hot[:, k, :], rif[:, :], iota[:, k:k + 1], None, ALU.is_equal))
            own.wait()
            dve.wait_ge(s["root_ready"], 1)
            own.link(nc.vector.reciprocal(rs[:, :], rs[:, :]))
            for t in range(NT):
                if t >= 2:
                    dve.wait_ge(s["xt_full"], t - 1)
                nc.vector.tensor_scalar(xn[:, t % 2, :], X[:, t, :], mv[:, t, 0:1], rs[:, t:t + 1],
                                        ALU.subtract, ALU.mult).then_inc(s["xn_ready"], 1)
                dve.wait_ge(s["xn_ready"], t + 1)
                own.mark(nc.vector.tensor_reduce(gmax[:, t:t + 1], xn[:, t % 2, :], AX.X, ALU.max,
                                                 apply_absolute_value=True))
            own.wait()
            nc.vector.tensor_reduce(g1[:, :], gmax[:, :], AX.X, ALU.max).then_inc(s["gmax_ready"], 1)
            dve.wait_ge(s["gall_ready"], 1)
            own.link(nc.vector.tensor_scalar(floor[:, :], gall[:, :], 1 / GSCALE, TINY, ALU.mult, ALU.max))
            own.link(nc.vector.tensor_scalar(floor[:, :], floor[:, :], TINY, None, ALU.mult))

            def scales(dst_s, dst_r, amax_, floor_):
                own.link(nc.vector.tensor_scalar(dst_s, amax_, 1 / FP8_MAX, floor_, ALU.mult, ALU.max))
                own.link(nc.vector.reciprocal(dst_r, dst_s))

            def second(rest, floor_):
                nb = SPLIT // QB16
                own.link(nc.vector.tensor_reduce(o_amax[:, 0, :], blocks(rest), AX.X, ALU.max,
                                                 apply_absolute_value=True))
                scales(o_amax[:, 1, :], o_amax[:, 2, :], o_amax[:, 0, :], floor_)
                own.link(nc.vector.tensor_tensor(blocks(rest), blocks(rest), spread(o_amax[:, 2, :], P, nb), ALU.mult))
                round_fp8(nc, own, rest, m2[:, :])
                own.link(nc.vector.tensor_tensor(blocks(rest), blocks(rest), spread(o_amax[:, 1, :], P, nb), ALU.mult))

            def a_lo(t):
                dve.wait_ge(s["a_hi"], t + 1)
                nc.vector.tensor_tensor(A16[:, 1, :, bass.ts(t, P)], TB[0][:, :, :], A16[:, 0, :, bass.ts(t, P)],
                                        ALU.subtract).then_inc(s["a_lo"], 1)

            def token_ratios(t):
                dve.wait_ge(s["xp_read"], t + 1)
                if not (type(t) is int and t == 0):
                    dve.wait_ge(s["at_full"], t)
                xb = H[:, bass.ds(t, 1), XP].rearrange("p o (b e) -> p (o b) e", e=QB16)
                own.link(nc.vector.tensor_reduce(amax[:, :], xb, AX.X, ALU.max, apply_absolute_value=True))
                scales(scale[:, :], rec[:, :], amax[:, :], floor[:, :])
                own.link(nc.vector.tensor_tensor(blocks(xq[:, :]), xb, spread(rec[:, :], P, NB), ALU.mult))

            def token_rounding():
                round_fp8(nc, own, xq[:, :], mm[:, 0:DM])

            def token_products(t):
                own.link(nc.vector.tensor_tensor(blocks(xq[:, :]), blocks(xq[:, :]), spread(scale[:, :], P, NB), ALU.mult))
                own.link(nc.vector.tensor_tensor(res[:, :], row(H[:, bass.ds(t, 1), 2 * DM - SPLIT:2 * DM]),
                                                 xq[:, DM - SPLIT:], ALU.subtract))
                second(res[:, :], floor[:, :])
                nc.vector.tensor_tensor(xq[:, DM - SPLIT:], xq[:, DM - SPLIT:], res[:, :], ALU.add)\
                    .then_inc(s["aq_ready"], 1)

            token_ratios(0)
            token_rounding()
            token_products(0)
            a_lo(0)

            PRO = own.n
            BODY = 4 + 4 + 2 + 9 + NC

            def hidden(t, c):
                dve.wait_ge(s["th_ready"], t * NC + c + 1)
                own.link(nc.vector.scalar_tensor_tensor(gate[:, c % 2, :], th[:, c % 2, :], 1.0, GA[c % 2][:, 0:CW],
                                                        ALU.add, ALU.mult))
                ht = row(H[:, bass.ds(t, 1), c * CW:(c + 1) * CW])
                nc.vector.scalar_tensor_tensor(ht, gate[:, c % 2, :], 0.5 / WS / WS, UA[c % 2][:, 0:CW],
                                               ALU.mult, ALU.mult).then_inc(s["gu_free"], 1)
                if c % 2:
                    dve.wait_ge(s["gu_free"], t * NC + c + 3)
                    hb = H[:, bass.ds(t, 1), (c - 1) * CW:(c + 1) * CW]\
                        .rearrange("p o (b e) -> p (o b) e", e=QB16)
                    nc.vector.tensor_reduce(row(hmax[:, bass.ds(t, 1), (c - 1) * CW // QB16:(c + 1) * CW // QB16]),
                                            hb, AX.X, ALU.max, apply_absolute_value=True).then_inc(s["max_ready"], 1)

            def body(t, last):
                own.enter(PRO, t, BODY)
                if not last:
                    token_ratios(t + 1)
                hidden(t, 0)
                if not last:
                    token_rounding()
                hidden(t, 1)
                if not last:
                    token_products(t + 1)
                hidden(t, 2)
                if not last:
                    a_lo(t + 1)
                hidden(t, 3)
                assert last or own.n == BODY, (own.n, BODY)

            with dve.Fori(0, NT - 1) as t:
                body(t, False)
            body(NT - 1, True)
            PRO1 = PRO + BODY * (NT - 1) + own.n
            own.enter(PRO1, 0, 0)
            dve.wait_ge(s["max_ready"], 2 * NT)
            nc.vector.tensor_reduce(h1[:, :], hmax[:, :, :], AX.XY, ALU.max).then_inc(s["hmax_ready"], 1)
            own.link(nc.vector.tensor_copy(h_split[:, :, :], H[:, :, FF - SPLIT:]))
            dve.wait_ge(s["hall_ready"], 1)
            own.link(nc.vector.tensor_scalar(gm[:, 0:1], hall[:, :], 1 / GSCALE, TINY, ALU.mult, ALU.max))
            own.link(nc.vector.tensor_scalar(hfloor[:, :], gm[:, 0:1], TINY, None, ALU.mult))
            own.link(nc.vector.reciprocal(gm[:, 1:2], gm[:, 0:1]))
            own.link(nc.vector.tensor_scalar(gm[:, 2:3], gm[:, 0:1], 1 / WS, None, ALU.mult))
            scales(hs[:, 0], hs[:, 1], hmax[:, :, :], hfloor[:, :])
            nc.vector.tensor_scalar(hs[:, 2], hs[:, 0], gm[:, 1:2], None, ALU.mult).then_inc(s["scales_ready"], 1)
            dve.wait_ge(s["scales_ready"], 1)
            PRO2 = PRO1 + own.n
            BODY2 = 1 + 2 + 1 + 1 + 9 + 1

            def x_add(t):
                dve.wait_ge(s["y_full"], t + 1)
                xt = row(X[:, bass.ds(t, 1), :])
                nc.vector.scalar_tensor_tensor(xt, YB[:, :], gm[:, 2:3], xt, ALU.mult, ALU.add)\
                    .then_inc(s["y_read"], 1)

            def h_lo(t):
                for c in range(3):
                    dve.wait_ge(s["ht_hi"], t * 3 + c + 1)
                    for n, w, lo in transposed_parts(c):
                        ins = nc.vector.tensor_tensor(hT[0:n, 1, lo:lo + w, :], TB[c][0:n, lo - 4 * c:lo - 4 * c + w, :],
                                                      hT[0:n, 0, lo:lo + w, :], ALU.subtract)
                    ins.then_inc(s["ht_lo"], 1)

            def quantise(t, before):
                own.enter(PRO2, t, BODY2)
                if before >= 2:
                    x_add(t - 2)
                dve.wait_ge(s["y8_ready"], t + 1)
                if before >= 1:
                    dve.wait_ge(s["hp_ready"], t)
                h = row(H[:, bass.ds(t, 1), :])
                own.link(nc.vector.tensor_scalar(mm[:, :].bitcast(I32), h.bitcast(I32), EXPONENT, None, ALU.bitwise_and))
                nc.vector.tensor_scalar(mm[:, :], mm[:, :], 2.0 ** -6, R4, ALU.max, ALU.mult).then_inc(s["m_ready"], 1)
                if before >= 1:
                    h_lo(t - 1)
                dve.wait_ge(s["m_ready"], t + 1)
                hw = row(H[:, bass.ds(t, 1), WP:])
                own.link(nc.vector.tensor_tensor(hw, hw, mm[:, WP:], ALU.add))
                own.link(nc.vector.tensor_tensor(hw, hw, mm[:, WP:], ALU.subtract))
                hsp = H[:, bass.ds(t, 1), FF - SPLIT:].rearrange("p o (b e) -> p (o b) e", e=QB16)
                own.link(nc.vector.tensor_tensor(blocks(res[:, :]), hsp, spread(row(hs[:, 0, bass.ds(t, 1), OH:]), P,
                                                                                SPLIT // QB16), ALU.mult))
                own.link(nc.vector.tensor_tensor(res[:, :], row(h_split[:, bass.ds(t, 1), :]), res[:, :], ALU.subtract))
                second(res[:, :], hfloor[:, :])
                if before >= 1:
                    dve.wait_ge(s["ht_full"], t * 3)
                hb = H[:, bass.ds(t, 1), WP:].rearrange("p o (b e) -> p (o b) e", e=QB16)
                own.link(nc.vector.tensor_tensor(blocks(hq[:, WP:]), hb,
                                                 spread(row(hs[:, 2, bass.ds(t, 1), WP // QB16:]), P, (FF - WP) // QB16),
                                                 ALU.mult))
                nc.vector.scalar_tensor_tensor(hq[:, FF - SPLIT:], res[:, :], gm[:, 1:2], hq[:, FF - SPLIT:],
                                               ALU.mult, ALU.add).then_inc(s["hq_ready"], 1)
                assert own.n == BODY2, (own.n, BODY2)

            quantise(0, 0)
            quantise(1, 1)
            with dve.Fori(2, NT) as t:
                quantise(t, 2)
            x_add(NT - 2)
            h_lo(NT - 1)
            x_add(NT - 1)

        @block.tensor
        def _(pe):
            PASSES = ((0, 0), (0, 1), (1, 0))

            for t in range(NT):
                pe.wait_ge(s["xn_ready"], t + 1)
                if t >= 2:
                    pe.wait_ge(s["xt_ready"], t - 1)
                for k in range(KT):
                    ins = nc.tensor.transpose(TB[t % 2][:, k, :], xn[:, t % 2, k * P:(k + 1) * P], ident)
                ins.then_inc(s["xt_full"], 1)

            def gather(t):
                pe.wait_ge(s["xt_ready"], t + 1)
                if t >= 2:
                    pe.wait_ge(s["xp_read"], t - 1)
                for k in range(KT):
                    ins = nc.tensor.matmul(GA[t % 2][:, :], xT[t][:, k, :], hot[:, k, :],
                                           start=(k == 0), stop=(k == KT - 1))
                ins.then_inc(s["xp_full"], 1)

            def transpose_tokens(t):
                pe.wait_ge(s["aq_ready"], t + 1)
                for k in range(KT):
                    ins = nc.tensor.transpose(TB[0][:, k, :], xq[:, k * P:(k + 1) * P], ident)
                ins.then_inc(s["at_full"], 1)

            for t in range(NT):
                gather(t)
            pe.wait_ge(s["xt_ready"], NT)
            transpose_tokens(0)
            pe.wait_ge(s["xp_read"], NT)

            def gate_up(t, last):
                pe.wait_ge(s["a_lo"], t + 1)
                for c in range(NC):
                    pe.wait_ge(s["gu_free"], t * NC + c + 1)
                    for m, bank in enumerate((GA[c % 2], UA[c % 2])):
                        for k in range(KT):
                            for q, (a, b) in enumerate(PASSES):
                                ins = nc.tensor.matmul(bank[:, 0:CW], A16[:, a, k, bass.ts(t, P)],
                                                       w16[:, m, b, k, c * CW:(c + 1) * CW],
                                                       start=(k == 0 and q == 0), stop=(k == KT - 1 and q == 2))
                        if m == 1:
                            ins.then_inc(s["gu_full"], 1)
                        elif c == NC - 1 and not last:
                            transpose_tokens(t + 1)

            with pe.Fori(0, NT - 1) as t:
                gate_up(t, False)
            gate_up(NT - 1, True)

            def transpose_hidden(t):
                pe.wait_ge(s["hq_ready"], t + 1)
                pe.wait_ge(s["hp_ready"], t + 1)
                for c in range(3):
                    for i in range(4 * c, min(4 * c + 4, FT)):
                        n = rows_of(i)
                        ins = nc.tensor.transpose(TB[c][0:n, i - 4 * c, :], hq[:, i * P:i * P + n], ident)
                    ins.then_inc(s["ht_full"], 1)

            def down_product(t, first):
                pe.wait_ge(s["ht_lo"], t * 3 + 3)
                if not first:
                    pe.wait_ge(s["y_read"], t)
                for i in range(FT):
                    n = rows_of(i)
                    for q, (a, b) in enumerate(PASSES):
                        ins = nc.tensor.matmul(YB[:, :], hT[0:n, a, i, :], wd16[0:n, b, i, :],
                                               start=(i == 0 and q == 0), stop=(i == FT - 1 and q == 2))
                ins.then_inc(s["y_full"], 1)

            transpose_hidden(0)
            down_product(0, True)
            transpose_hidden(1)
            with pe.Fori(2, NT) as t:
                down_product(t - 1, False)
                transpose_hidden(t)
            down_product(NT - 1, False)


def row(ap):
    return ap.rearrange("p o n -> p (o n)")


def decoder_layer(nc, const_in, x_in, ctx_in, ctxT_in, w_q, w_k, w_v, w_o, w_lq, w_lk, w_lv, w_lo,
                  x_WqT, x_WkT, x_Wv, x_WoT, x_bo, x_g, w_gateT, w_upT, w_downT, ri_in, ri_in_cols, ri_mid_cols, ri_mid_last, out):
    scratch = [nc.dram_tensor(f"scratch{m}", (FF, 2 * DM), F16, kind="Internal").ap() for m in range(2)]
    with ExitStack() as ctx:
        def sem(name):
            return ctx.enter_context(nc.semaphore(name))

        X = ctx.enter_context(nc.sbuf_tensor("X", [P, NT, DM], F32))
        const = ctx.enter_context(nc.sbuf_tensor("const", [P, C_COMMON], F32))
        attention_phase(nc, X, const, const_in, x_in, w_q, w_k, w_v, w_o, w_lq, w_lk, w_lv, w_lo, sem)
        cross_phase(nc, X, const, const_in, ctx_in, ctxT_in, x_WqT, x_WkT, x_Wv, x_WoT, x_bo, x_g, sem)
        w16 = ctx.enter_context(nc.sbuf_tensor("w16_ffn", [P, 2, 2, KT, FF], F16))
        wd16 = ctx.enter_context(nc.sbuf_tensor("wd16_ffn", [P, 2, FT, DM], F16))
        weight_phase(nc, const, w16, wd16, (w_gateT, w_upT), w_downT, scratch, ri_in_cols, ri_mid_cols, ri_mid_last, sem)
        feed_forward_phase(nc, X, const, const_in, w16, wd16, ri_in, out, sem)


def kernel(**inputs):
    import concourse.bacc as bacc
    from concourse.bass_utils import run_bass_kernel_spmd

    nc = bacc.Bacc("TRN2", target_bir_lowering=False, num_devices=1)
    arrays, args = {}, []

    def give(name, a):
        a = np.ascontiguousarray(a)
        arrays[name] = a
        args.append(nc.dram_tensor(name, a.shape, mybir.dt.from_np(a.dtype), kind="ExternalInput").ap())

    give("shape_constants", shape_constants())
    give("x", np.asarray(inputs["x"]).reshape(TOK, DM))
    give("ctx", np.asarray(inputs["ctx_4096"]).reshape(TOK, DM))
    give("ctxT", np.asarray(inputs["ctx_4096"]).transpose(0, 2, 1))
    for n in ("w_q", "w_k", "w_v", "w_o", "w_lq", "w_lk", "w_lv", "w_lo"):
        give(n, np.asarray(inputs["L0_attn_" + n]))
    for n, flip in (("Wq", True), ("Wk", True), ("Wv", False), ("Wo", True), ("bo", False), ("g", False)):
        a = np.asarray(inputs["L0_xattn_" + n])
        give("x_" + n, a.T if flip else a)
    for n in ("w_gate", "w_up", "w_down"):
        give(n, np.asarray(inputs["L0_ffn_" + n]).T)
    ri_in, ri_mid = np.asarray(inputs["L0_ffn_ri_in"]), np.asarray(inputs["L0_ffn_ri_mid"])
    whole = (FT - 1) * P
    give("ri_in", ri_in)
    give("ri_in_cols", ri_in.reshape(KT, P).T)
    give("ri_mid_cols", ri_mid[:whole].reshape(FT - 1, P).T)
    give("ri_mid_last", ri_mid[whole:].reshape(FF - whole, 1))
    args.append(nc.dram_tensor("out", (TOK, DM), F32, kind="ExternalOutput").ap())
    decoder_layer(nc, *args)
    r = run_bass_kernel_spmd(nc, [arrays], core_ids=[0])
    return r.results[0]["out"].reshape(BATCH, SEQ, DM)
```

```python
from contextlib import ExitStack

import numpy as np

import concourse.bass as bass
from concourse import mybir

P = 128
BATCH, SEQ, DM = 16, 64, 512
TOK = BATCH * SEQ
NT = TOK // P
KT = DM // P
HEADS, KVH, HD = 32, 8, 128
GROUP = HEADS // KVH
HB = 2 * GROUP
ITERS = HEADS // HB
SCALE = 1.0 / float(np.sqrt(HD))
WS = 64.0
EPS = 1e-5
HALF = 512

ALU = mybir.AluOpType
ACT = mybir.ActivationFunctionType
AX = mybir.AxisListType
F32 = mybir.dt.float32
F16 = mybir.dt.float16
I32 = mybir.dt.int32

C_ID, C_COS, C_SIN, C_MASK, C_ONES, C_PICK, C_IOTA, C_END = 0, 128, 192, 256, 320, 352, 480, 484
C_COMMON = C_ONES


def shape_constants():
    c = np.zeros((P, C_END), np.float32)
    c[:, C_ID:C_ID + P] = np.eye(P, dtype=np.float32)
    inv = (np.float32(1.0) / np.float32(10000.0) ** (np.arange(0, HD, 2, dtype=np.float32) / np.float32(HD)))
    freq = np.outer(np.arange(SEQ, dtype=np.float32), inv.astype(np.float32)).astype(np.float32)
    cos, sin = np.cos(freq).T, np.sin(freq).T
    c[0:64, C_COS:C_COS + SEQ] = cos / WS
    c[64:128, C_COS:C_COS + SEQ] = cos / WS
    c[0:64, C_SIN:C_SIN + SEQ] = sin / WS
    c[64:128, C_SIN:C_SIN + SEQ] = -sin / WS
    q = np.arange(P) % SEQ
    c[:, C_MASK:C_MASK + SEQ] = np.where(np.arange(SEQ)[None, :] <= q[:, None], 0.0, -1e30)
    p = np.arange(P)
    c[:, C_ONES:C_ONES + 32] = (p[:, None] // 64 == np.arange(32)[None, :] % 2)
    c[:, C_PICK:C_PICK + P] = (p[:, None] % 32 == p[None, :] // 64)
    c[:, C_IOTA:C_IOTA + KT] = p[:, None] + P * np.arange(KT)[None, :]
    return c


def row(ap):
    return ap.rearrange("p o n -> p (o n)")


class Chain:

    def __init__(self, engine, sem):
        self.engine, self.sem, self.base, self.n = engine, sem, 0, 0

    def link(self, instruction):
        self.mark(instruction)
        self.wait()

    def mark(self, instruction):
        self.n += 1
        instruction.then_inc(self.sem, 1)

    def wait(self):
        self.engine.wait_ge(self.sem, self.base + self.n)

    def enter(self, start, it, per_body):
        self.base, self.n = it * per_body + start, 0


def layernorm_tile(nc, X, st, t):
    return nc.vector.bn_stats(st[:, t, :], X[:, t, :])


def layernorm_finish(chain, nc, st, mv, rs):
    chain.wait()
    for t in range(NT):
        chain.mark(nc.vector.bn_aggr(mv[:, t, :], st[:, t, :]))
    chain.wait()
    return nc.vector.tensor_scalar(rs[:, :], mv[:, :, 1], EPS, None, ALU.add)


def layernorm_stats(dve, chain, nc, X, st, mv, rs, loaded=None):
    for t in range(NT):
        if loaded:
            dve.wait_ge(loaded[t], 16)
        chain.mark(layernorm_tile(nc, X, st, t))
    return layernorm_finish(chain, nc, st, mv, rs)


def attention_phase(nc, X, const, const_in, x_loaded, x_in, w_q, w_k, w_v, w_o, w_lq, w_lk, w_lv, w_lo, sem):
    with ExitStack() as ctx:
        def sb(name, shape, dt=F32):
            return ctx.enter_context(nc.sbuf_tensor(name, shape, dt))

        def ps(name, shape, dt=F32):
            return ctx.enter_context(nc.psum_tensor(name, shape, dt))

        ident = const[:, C_ID:C_ID + P]
        cos8 = const[:, C_COS:C_COS + SEQ].unsqueeze(1).to_broadcast([P, BATCH, SEQ])
        mask = const[:, C_MASK:C_MASK + SEQ].unsqueeze(1).to_broadcast([P, 2 * NT, SEQ])

        def sin_of(p0):
            return const[p0:p0 + 64, C_SIN:C_SIN + SEQ].unsqueeze(1).to_broadcast([64, BATCH, SEQ])

        XT = sb("XT", [P, 2, KT, TOK], F16)
        LQ = sb("LQ", [P, 2, TOK], F16)
        st = sb("st", [P, NT, 6])
        mv = sb("mv", [P, NT, 2])
        rs = sb("rs", [P, NT])
        NW = 2 * KT + 1
        w_raw = sb("w_raw", [P, 2, NW, P])
        w16 = sb("w16", [P, 2, 2, NW, P], F16)
        kv_raw = sb("kv_raw", [P, 2 * KT, P])
        kv16 = sb("kv16", [P, 2, 2 * KT, P], F16)
        o_raw = sb("o_raw", [P, GROUP, DM])
        o16 = sb("o16", [P, 2, 2 * GROUP, DM], F16)
        q_raw = sb("q_raw", [P, TOK])
        lk_raw = sb("lk_raw", [P, TOK])
        k_raw = sb("k_raw", [P, TOK])
        rt = sb("rt", [P, 2, TOK])
        gt = sb("gt", [P, 2, TOK])
        qT = sb("qT", [P, 2, TOK])
        lkT = sb("lkT", [P, 2, TOK])
        kT = sb("kT", [P, 2, TOK])
        v = sb("v", [P, 2, NT, HD])
        lv = sb("lv", [P, 2, NT, HD])
        s_sb = sb("s_sb", [P, 2 * NT, SEQ])
        rmax = sb("rmax", [P, 2 * NT])
        rsum = sb("rsum", [P, 2 * NT])
        pbd = sb("pbd", [P, 2 * NT, P])
        pT = sb("pT", [P, 2 * NT, P])
        xn = s_sb[:, :, :].rearrange("p a b -> p (a b)").rearrange("p (a b) -> p a b", a=2)
        wlq_raw = pT[:, 0:4, :]
        wlq = pT[:, 4:8, :].bitcast(F16).rearrange("p a (b c) -> p (a b) c", c=P).rearrange("p (a b) c -> p a b c", a=2)
        aT = sb("aT", [P, 2, 2 * GROUP, TOK], F16)

        PJ = [ps(f"PJ{i}", [P, HALF]) for i in range(2)]
        S = ps("S", [P, 2 * NT, SEQ])
        TB = [ps(f"TB{i}", [P, 4, P]) for i in range(2)]
        OB = [ps(f"OB{i}", [P, HALF]) for i in range(2)]

        const_loaded, wlq_loaded = sem("const_loaded"), sem("wlq_loaded")
        w_loaded = [sem("w_loaded0"), sem("w_loaded1")]
        kv_loaded, o_loaded = sem("kv_loaded"), sem("o_loaded")
        dve_own, pool_own = sem("dve_own"), sem("pool_own")
        var_ready, root_ready, xn_ready = sem("var_ready"), sem("root_ready"), sem("xn_ready")
        xt_psum, xt_hi, xt_lo = sem("xt_psum"), sem("xt_hi"), sem("xt_lo")
        wlq_hi, wlq_lo, lq_psum, lq_hi, lq_lo = (sem(n) for n in ("wlq_hi", "wlq_lo", "lq_psum", "lq_hi", "lq_lo"))
        wt_hi, wt_lo, kv_hi, kv_lo, o_hi, o_lo = (sem(n) for n in ("wt_hi", "wt_lo", "kv_hi", "kv_lo", "o_hi", "o_lo"))
        pj_full, pj_free = sem("pj_full"), sem("pj_free")
        q_roped, lk_roped, k_roped = sem("q_roped"), sem("lk_roped"), sem("k_roped")
        s_full, shifted, exp_done, pbd_ready = sem("s_full"), sem("shifted"), sem("exp_done"), sem("pbd_ready")
        t_full, t_free = sem("t_full"), sem("t_free")
        b_full, b_free, a_hi = sem("b_full"), sem("b_free"), sem("a_hi")
        pbd_zeroed = sem("pbd_zeroed")

        def pj_base(h):
            return 6 * h + (4 if h > 3 else 0)

        PJ_BODY, T_BODY, B_BODY = 6 * HB + 8, 4 * HB, 4 * HB + 2 * NT
        PJ_PRO = 10

        def b_base(h):
            return 4 * h + NT * (h // 4)

        wq_v = w_q.rearrange("(k p) n -> p k n", p=P)
        wlv_v = w_lv.rearrange("(k p) n -> p k n", p=P)
        wk_v = w_k.rearrange("(k p) n -> p k n", p=P)
        wv_v = w_v.rearrange("(k p) n -> p k n", p=P)
        wo_v = w_o.rearrange("(h p) n -> p h n", p=P)
        wlo_v = w_lo.rearrange("(h p) n -> p h n", p=P)

        block = ctx.enter_context(nc.Block())

        @block.sync
        def _(sp):
            def load_head(par, n):
                sp.dma_start(w_raw[:, par, 0:KT, :], wq_v[:, :, bass.ts(n, P)]).then_inc(w_loaded[par], 16)
                sp.dma_start(w_raw[:, par, KT, :], w_lk[:, bass.ts(n, P)]).then_inc(w_loaded[par], 16)
                sp.dma_start(w_raw[:, par, KT + 1:NW, :], wlv_v[:, :, bass.ts(n, P)]).then_inc(w_loaded[par], 16)

            def load_kv(g):
                sp.dma_start(kv_raw[:, 0:KT, :], wk_v[:, :, bass.ts(g, P)]).then_inc(kv_loaded, 16)
                sp.dma_start(kv_raw[:, KT:, :], wv_v[:, :, bass.ts(g, P)]).then_inc(kv_loaded, 16)

            def load_o(g, part):
                src = (wo_v, wlo_v)[part]
                sp.dma_start(o_raw[:, :, :], src[:, bass.ts(g, GROUP), :]).then_inc(o_loaded, 16)

            for t in range(NT):
                sp.dma_start(X[:, t, :], x_in[t * P:(t + 1) * P, :]).then_inc(x_loaded[t], 16)
            sp.dma_start(wlq_raw[:, :, :], w_lq.rearrange("(k p) n -> p k n", p=P)).then_inc(wlq_loaded, 16)
            load_kv(0)
            load_head(0, 0)
            load_head(1, 1)
            load_o(0, 0)

            def body(it, last):
                for h in range(HB):
                    if not (last and h >= HB - 2):
                        sp.wait_ge(wt_hi, it * HB + h + 1)
                        sp.wait_ge(wt_lo, it * HB + h + 1)
                        load_head(h % 2, it * HB + h + 2)
                    g = h // 4
                    if h % 4 == 0 and not (last and g == 1):
                        sp.wait_ge(kv_hi, it * 2 + g + 1)
                        sp.wait_ge(kv_lo, it * 2 + g + 1)
                        load_kv(it * 2 + g + 1)
                    if h % 4 == 1 or (h % 4 == 3 and not (last and g == 1)):
                        part = h % 4 // 2
                        sp.wait_ge(o_hi, it * 4 + 2 * g + part + 1)
                        sp.wait_ge(o_lo, it * 4 + 2 * g + part + 1)
                        load_o(it * 2 + g + part, 1 - part)

            with sp.Fori(0, ITERS - 1) as it:
                body(it, False)
            body(ITERS - 1, True)

        @block.scalar
        def _(act):
            def hi_of(dst, src, scale=WS):
                return nc.scalar.activation(dst, src, ACT.Copy, scale=scale)

            def split_head(par):
                act.wait_ge(w_loaded[par], 48)
                hi_of(w16[:, par, 0], w_raw[:, par]).then_inc(wt_hi, 1)

            act.dma_start(const[:, :], const_in[:, 0:C_COMMON]).then_inc(const_loaded, 16)
            act.sem_inc(pj_free, 2)
            act.sem_inc(t_free, 2)
            act.wait_ge(var_ready, 1)
            nc.scalar.activation(rs[:, :], rs[:, :], ACT.Sqrt).then_inc(root_ready, 1)
            for t in range(NT):
                act.wait_ge(xt_psum, t + 1)
                hi_of(XT[:, 0, :, t * P:(t + 1) * P], TB[t % 2][:, :, :], 1.0).then_inc(xt_hi, 1)
                if t == 3:
                    act.wait_ge(wlq_loaded, 16)
                    hi_of(wlq[:, 0], wlq_raw[:, :]).then_inc(wlq_hi, 1)
            act.wait_ge(kv_loaded, 32)
            hi_of(kv16[:, 0], kv_raw[:, :]).then_inc(kv_hi, 1)
            for c in range(2):
                act.wait_ge(lq_psum, c + 1)
                hi_of(LQ[:, 0, c * HALF:(c + 1) * HALF], OB[c][:, :], 1 / WS).then_inc(lq_hi, 1)
            split_head(0)
            split_head(1)

            def take(base, k, dst, scale, extra=None):
                act.wait_ge(pj_full, base + k + 1)
                src = PJ[k % 2][:, :]
                if len(dst.shape) == 3:
                    src = src.rearrange("p (t d) -> p t d", d=HD)
                ins = hi_of(dst, src, scale)
                ins.then_inc(pj_free, 1)
                return ins

            def kv_steps(base, k, gp, roped_need, between=lambda: None):
                if roped_need is not None:
                    act.wait_ge(k_roped, roped_need)
                take(base, k, k_raw[:, 0:HALF], 1.0)
                between()
                take(base, k + 1, k_raw[:, HALF:], 1.0)
                take(base, k + 2, v[:, gp, 0:4, :], 1 / WS)
                take(base, k + 3, v[:, gp, 4:8, :], 1 / WS)

            kv_steps(0, 0, 0, None)
            take(0, 4, q_raw[:, 0:HALF], 1.0)
            take(0, 5, q_raw[:, HALF:], 1.0)
            take(0, 6, lk_raw[:, 0:HALF], 1.0)
            take(0, 7, lk_raw[:, HALF:], 1.0)
            take(0, 8, lv[:, 0, 0:4, :], 1 / WS)
            take(0, 9, lv[:, 0, 4:8, :], 1 / WS)

            def body(it, last):
                for h in range(HB):
                    n = it * HB + h
                    g = h // 4
                    more = not (last and h == HB - 1)
                    base = it * PJ_BODY + PJ_PRO
                    k = pj_base(h)

                    def exponentials():
                        act.wait_ge(shifted, n + 1)
                        nc.scalar.activation(s_sb[:, :, :], s_sb[:, :, :], ACT.Exp, scale=SCALE).then_inc(exp_done, 1)

                    if more and h % 4 == 3:
                        kv_steps(base, k, (h // 4 + 1) % 2, it * 2 + h // 4 + 1, exponentials)
                        k += 4
                    if more:
                        act.wait_ge(q_roped, n + 1)
                        take(base, k, q_raw[:, 0:HALF], 1.0)
                    if not (more and h % 4 == 3):
                        exponentials()
                    if more:
                        take(base, k + 1, q_raw[:, HALF:], 1.0)
                        act.wait_ge(lk_roped, n + 1)
                        take(base, k + 2, lk_raw[:, 0:HALF], 1.0)
                        take(base, k + 3, lk_raw[:, HALF:], 1.0)
                        take(base, k + 4, lv[:, (h + 1) % 2, 0:4, :], 1 / WS)
                    for j in range(4):
                        act.wait_ge(t_full, it * T_BODY + 4 * h + j + 1)
                        nc.scalar.activation(pT[:, 4 * j:4 * j + 4, :], TB[j % 2][:, :, :], ACT.Copy)\
                            .then_inc(t_free, 1)
                    for j in range(4):
                        if j == 2 and not (last and h >= HB - 2):
                            act.wait_ge(w_loaded[h % 2], (it * (HB // 2) + h // 2 + 2) * 48)
                            hi_of(w16[:, h % 2, 0], w_raw[:, h % 2]).then_inc(wt_hi, 1)
                        if j == 2 and more:
                            take(base, k + 5, lv[:, (h + 1) % 2, 4:8, :], 1 / WS)
                        act.wait_ge(b_full, it * B_BODY + b_base(h) + j + 1)
                        kt = (h % 4) + GROUP * (j // 2)
                        hi_of(aT[:, 0, kt, (j % 2) * HALF:(j % 2 + 1) * HALF], OB[j % 2][:, :], 1.0)\
                            .then_inc(a_hi, 1)
                    if h % 4 == 1 and not (last and g == 1):
                        act.wait_ge(kv_loaded, (it * 2 + g + 2) * 32)
                        hi_of(kv16[:, 0], kv_raw[:, :]).then_inc(kv_hi, 1)
                    if h % 4 in (0, 2):
                        part = h % 4 // 2
                        act.wait_ge(o_loaded, (it * 4 + 2 * g + part + 1) * 16)
                        hi_of(o16[:, 0, part * GROUP:(part + 1) * GROUP], o_raw[:, :]).then_inc(o_hi, 1)

            with act.Fori(0, ITERS - 1) as it:
                body(it, False)
            body(ITERS - 1, True)

        @block.gpsimd
        def _(pool):
            own = Chain(pool, pool_own)
            nc.gpsimd.memset(pbd[:, :, :], 0.0).then_inc(pbd_zeroed, 1)
            pool.wait_ge(const_loaded, 16)

            def rope(dst, src, ready):
                s3 = src.rearrange("p (b t) -> p b t", t=SEQ)
                g3 = [gt[:, i, :].rearrange("p (b t) -> p b t", t=SEQ) for i in range(2)]
                own.link(nc.gpsimd.tensor_tensor(g3[0], s3, cos8, ALU.mult))
                own.link(nc.gpsimd.tensor_tensor(g3[1][0:64], s3[64:128], sin_of(64), ALU.mult))
                own.link(nc.gpsimd.tensor_tensor(g3[1][64:128], s3[0:64], sin_of(0), ALU.mult))
                nc.gpsimd.tensor_tensor(dst, gt[:, 0, :], gt[:, 1, :], ALU.add).then_inc(ready, 1)

            pool.wait_ge(pj_free, 2 + 8)
            rope(lkT[:, 0, :], lk_raw[:, :], lk_roped)

            def body(it, last):
                own.enter(3, it, 3 * HB)
                for h in range(HB):
                    if last and h == HB - 1:
                        break
                    k = pj_base(h) + (4 if h % 4 == 3 else 0) + 4
                    pool.wait_ge(pj_free, it * PJ_BODY + PJ_PRO + 2 + k)
                    pool.wait_ge(lk_roped, it * HB + h + 1)
                    pool.wait_ge(s_full, it * HB + h + 1)
                    rope(lkT[:, (h + 1) % 2, :], lk_raw[:, :], lk_roped)

            with pool.Fori(0, ITERS - 1) as it:
                body(it, False)
            body(ITERS - 1, True)

        @block.vector
        def _(dve):
            own = Chain(dve, dve_own)

            def lo_of(dst, src, hi, scale):
                return nc.vector.scalar_tensor_tensor(dst, src, scale, hi, ALU.mult, ALU.subtract)

            def rope(dst, src, ready):
                s3 = src.rearrange("p (b t) -> p b t", t=SEQ)
                g3 = [rt[:, i, :].rearrange("p (b t) -> p b t", t=SEQ) for i in range(2)]
                own.mark(nc.vector.tensor_tensor(g3[0], s3, cos8, ALU.mult))
                own.mark(nc.vector.tensor_tensor(g3[1][0:64], s3[64:128], sin_of(64), ALU.mult))
                own.mark(nc.vector.tensor_tensor(g3[1][64:128], s3[0:64], sin_of(0), ALU.mult))
                own.wait()
                ins = nc.vector.tensor_tensor(dst, rt[:, 0, :], rt[:, 1, :], ALU.add)
                ins.then_inc(ready, 1)

            dve.sem_inc(b_free, 2)
            ins = layernorm_stats(dve, own, nc, X, st, mv, rs, x_loaded)
            ins.then_inc(var_ready, 1)
            dve.wait_ge(root_ready, 1)
            own.link(nc.vector.reciprocal(rs[:, :], rs[:, :]))
            for t in range(NT):
                if t >= 2:
                    dve.wait_ge(xt_psum, t - 1)
                nc.vector.tensor_scalar(xn[:, t % 2, :], X[:, t, :], mv[:, t, 0:1], rs[:, t:t + 1],
                                        ALU.subtract, ALU.mult).then_inc(xn_ready, 1)
                if t >= 1:
                    dve.wait_ge(xt_hi, t)
                    lo_of(XT[:, 1, :, (t - 1) * P:t * P], TB[(t - 1) % 2][:, :, :],
                          XT[:, 0, :, (t - 1) * P:t * P], 1.0).then_inc(xt_lo, 1)
                if t == 5:
                    dve.wait_ge(wlq_hi, 1)
                    lo_of(wlq[:, 1], wlq_raw[:, :], wlq[:, 0], WS).then_inc(wlq_lo, 1)
            dve.wait_ge(xt_hi, NT)
            lo_of(XT[:, 1, :, (NT - 1) * P:], TB[(NT - 1) % 2][:, :, :],
                  XT[:, 0, :, (NT - 1) * P:], 1.0).then_inc(xt_lo, 1)
            dve.wait_ge(kv_hi, 1)
            lo_of(kv16[:, 1], kv_raw[:, :], kv16[:, 0], WS).then_inc(kv_lo, 1)
            for c in range(2):
                dve.wait_ge(lq_hi, c + 1)
                lo_of(LQ[:, 1, c * HALF:(c + 1) * HALF], OB[c][:, :],
                      LQ[:, 0, c * HALF:(c + 1) * HALF], 1 / WS).then_inc(lq_lo, 1)
            for par in range(2):
                dve.wait_ge(wt_hi, par + 1)
                lo_of(w16[:, par, 1], w_raw[:, par], w16[:, par, 0], WS).then_inc(wt_lo, 1)
            dve.wait_ge(const_loaded, 16)
            dve.wait_ge(pj_free, 2 + 2)
            rope(kT[:, 0, :], k_raw[:, :], k_roped)
            dve.wait_ge(k_roped, 1)
            dve.wait_ge(pj_free, 2 + 6)
            rope(qT[:, 0, :], q_raw[:, :], q_roped)
            dve.wait_ge(pbd_zeroed, 1)
            PRO = own.n
            D_BODY = 4 * HB + 3 * HB + 3 * 2

            def body(it, last):
                own.enter(PRO, it, D_BODY)
                for h in range(HB):
                    n = it * HB + h
                    more = not (last and h == HB - 1)
                    k = pj_base(h)
                    dve.wait_ge(s_full, n + 1)
                    own.link(nc.vector.tensor_tensor(s_sb[:, :, :], S[:, :, :], mask, ALU.add))
                    own.link(nc.vector.tensor_reduce(rmax[:, :], s_sb[:, :, :], AX.X, ALU.max))
                    nc.vector.tensor_tensor(s_sb[:, :, :], s_sb[:, :, :],
                                            rmax[:, :].unsqueeze(2).to_broadcast([P, 2 * NT, SEQ]),
                                            ALU.subtract).then_inc(shifted, 1)
                    dve.wait_ge(exp_done, n + 1)
                    own.link(nc.vector.tensor_reduce(rsum[:, :], s_sb[:, :, :], AX.X, ALU.add))
                    own.link(nc.vector.reciprocal(rsum[:, :], rsum[:, :]))
                    for s in range(2):
                        r = slice(64 * s, 64 * s + 64)
                        ins = nc.vector.tensor_tensor(pbd[r, :, 64 * s:64 * s + 64], s_sb[r, :, :],
                                                      rsum[r, :].unsqueeze(2).to_broadcast([64, 2 * NT, SEQ]),
                                                      ALU.mult)
                    ins.then_inc(pbd_ready, 1)
                    g = h // 4
                    if h % 4 in (1, 3):
                        part = h % 4 // 2
                        c = slice(part * GROUP, (part + 1) * GROUP)
                        dve.wait_ge(o_hi, it * 4 + 2 * g + part + 1)
                        lo_of(o16[:, 1, c], o_raw[:, :], o16[:, 0, c], WS).then_inc(o_lo, 1)
                    if h % 4 == 2 and not (last and g == 1):
                        dve.wait_ge(kv_hi, it * 2 + g + 2)
                        lo_of(kv16[:, 1], kv_raw[:, :], kv16[:, 0], WS).then_inc(kv_lo, 1)
                    base = it * PJ_BODY + PJ_PRO + 2
                    if more and h % 4 == 3:
                        g = h // 4
                        dve.wait_ge(pj_free, base + k + 2)
                        dve.wait_ge(q_roped, n + 1)
                        rope(kT[:, (g + 1) % 2, :], k_raw[:, :], k_roped)
                        dve.wait_ge(k_roped, it * 2 + g + 2)
                        k += 4
                    if more:
                        dve.wait_ge(pj_free, base + k + 2)
                        dve.wait_ge(q_roped, n + 1)
                        rope(qT[:, (h + 1) % 2, :], q_raw[:, :], q_roped)
                    for j in range(4):
                        if j == 2:
                            if not (last and h >= HB - 2):
                                dve.wait_ge(wt_hi, n + 3)
                                lo_of(w16[:, h % 2, 1], w_raw[:, h % 2], w16[:, h % 2, 0], WS).then_inc(wt_lo, 1)
                        kt = (h % 4) + GROUP * (j // 2)
                        c = slice((j % 2) * HALF, (j % 2 + 1) * HALF)
                        dve.wait_ge(a_hi, n * 4 + j + 1)
                        lo_of(aT[:, 1, kt, c], OB[j % 2][:, :], aT[:, 0, kt, c], 1.0).then_inc(b_free, 1)
                    if h % 4 == 3:
                        for t in range(NT):
                            dve.wait_ge(b_full, it * B_BODY + b_base(h) + 4 + t + 1)
                            nc.vector.scalar_tensor_tensor(X[:, t, :], OB[t % 2][:, :], 1 / WS, X[:, t, :],
                                                           ALU.mult, ALU.add).then_inc(b_free, 1)
                if last:
                    assert own.n == D_BODY - 6, (own.n, D_BODY)
                else:
                    assert own.n == D_BODY, (own.n, D_BODY)

            with dve.Fori(0, ITERS - 1) as it:
                body(it, False)
            body(ITERS - 1, True)

        @block.tensor
        def _(pe):
            PASSES = ((0, 0), (0, 1), (1, 0))

            def project(out, pairs, done=None):
                n, last = 0, None
                for lhs, rhs in pairs:
                    for a, b in PASSES:
                        last = nc.tensor.matmul(out, lhs(a), rhs(b), start=(n == 0), stop=(n == 3 * len(pairs) - 1))
                        n += 1
                return last

            def head_w(par, i):
                return lambda a: w16[:, par, a, i, :]

            def kv_w(i):
                return lambda a: kv16[:, a, i, :]

            def xt(kt, c, w):
                return lambda b: XT[:, b, kt, c:c + w]

            pe.wait_ge(const_loaded, 16)
            for t in range(NT):
                pe.wait_ge(xn_ready, t + 1)
                if t >= 2:
                    pe.wait_ge(xt_lo, t - 1)
                for c in range(KT):
                    ins = nc.tensor.transpose(TB[t % 2][:, c, :], xn[:, t % 2, c * P:(c + 1) * P], ident)
                ins.then_inc(xt_psum, 1)
            pe.wait_ge(xt_lo, NT)
            pe.wait_ge(wlq_lo, 1)
            for c in range(2):
                project(OB[c][:, :], [(lambda a, i=i: wlq[:, a, i, :], xt(i, c * HALF, HALF)) for i in range(KT)])\
                    .then_inc(lq_psum, 1)

            def step(base, k, emit):
                pe.wait_ge(pj_free, base + k + 1)
                emit(PJ[k % 2]).then_inc(pj_full, 1)

            def feature_major(w, c):
                return lambda out: project(out[:, :], [(w(i), xt(i, c * HALF, HALF)) for i in range(KT)])

            def token_major(w, c):
                def emit(out):
                    for t in range(4):
                        ins = project(out[:, t * HD:(t + 1) * HD],
                                      [(xt(i, (4 * c + t) * P, P), w(i)) for i in range(KT)])
                    return ins
                return emit

            def kv_steps(base, k):
                step(base, k, feature_major(kv_w, 0))
                step(base, k + 1, feature_major(kv_w, 1))
                step(base, k + 2, token_major(lambda i: kv_w(KT + i), 0))
                step(base, k + 3, token_major(lambda i: kv_w(KT + i), 1))

            def q_lk_steps(base, k, par):
                step(base, k, feature_major(lambda i: head_w(par, i), 0))
                step(base, k + 1, feature_major(lambda i: head_w(par, i), 1))
                for c in range(2):
                    step(base, k + 2 + c, lambda out, c=c: project(
                        out[:, :], [(head_w(par, KT), lambda b: LQ[:, b, c * HALF:(c + 1) * HALF])]))

            def lv_half(base, k, par, half):
                if half == 0:
                    pe.wait_ge(pj_free, base + k + 1)
                for t in range(2 * half, 2 * half + 2):
                    ins = project(PJ[k % 2][:, t * HD:(t + 1) * HD],
                                  [(xt(i, (4 + t) * P, P), head_w(par, KT + 1 + i)) for i in range(KT)])
                if half == 1:
                    ins.then_inc(pj_full, 1)

            def lv_step(base, k, par, c):
                step(base, k, token_major(lambda i: head_w(par, KT + 1 + i), c))

            pe.wait_ge(kv_lo, 1)
            kv_steps(0, 0)
            pe.wait_ge(wt_lo, 1)
            pe.wait_ge(lq_lo, 2)
            q_lk_steps(0, 4, 0)
            lv_step(0, 8, 0, 0)
            lv_step(0, 9, 0, 1)

            def body(it, last):
                for h in range(HB):
                    n = it * HB + h
                    g = h // 4
                    par = h % 2
                    more = not (last and h == HB - 1)
                    base = it * PJ_BODY + PJ_PRO
                    k = pj_base(h)
                    pe.wait_ge(k_roped, it * 2 + g + 1)
                    pe.wait_ge(q_roped, n + 1)
                    pe.wait_ge(lk_roped, n + 1)
                    for t in range(NT):
                        for kind, keys in enumerate((kT[:, g % 2, :], lkT[:, par, :])):
                            for s in range(2):
                                c = slice(t * P + 64 * s, t * P + 64 * s + 64)
                                ins = nc.tensor.matmul(S[64 * s:64 * s + 64, 2 * t + kind, :], qT[:, par, c],
                                                       keys[:, c], start=True, stop=True)
                    ins.then_inc(s_full, 1)
                    if more:
                        if h % 4 == 3:
                            pe.wait_ge(kv_lo, it * 2 + g + 2)
                            kv_steps(base, k)
                            k += 4
                        pe.wait_ge(wt_lo, n + 2)
                        q_lk_steps(base, k, 1 - par)
                        lv_step(base, k + 4, 1 - par, 0)
                    pe.wait_ge(pbd_ready, n + 1)
                    for j in range(4):
                        if j == 2 and more:
                            lv_half(base, k + 5, 1 - par, 0)
                        pe.wait_ge(t_free, it * T_BODY + 4 * h + j + 1)
                        for u in range(4):
                            ins = nc.tensor.transpose(TB[j % 2][:, u, :], pbd[:, 4 * j + u, :], ident)
                        ins.then_inc(t_full, 1)
                    for j in range(4):
                        if j == 2 and more:
                            lv_half(base, k + 5, 1 - par, 1)
                        pe.wait_ge(b_free, it * B_BODY + b_base(h) + j + 1)
                        if j < 2:
                            pe.wait_ge(t_free, it * T_BODY + 4 * h + 2 * j + 2 + 2)
                        for t in range(4 * (j % 2), 4 * (j % 2) + 4):
                            vals = v[:, g % 2, t, :] if j < 2 else lv[:, par, t, :]
                            ins = nc.tensor.matmul(OB[j % 2][:, (t % 4) * P:(t % 4 + 1) * P], vals,
                                                   pT[:, 2 * t + j // 2, :], start=True, stop=True)
                        ins.then_inc(b_full, 1)
                    if h % 4 == 3:
                        pe.wait_ge(o_lo, it * 4 + 2 * g + 2)
                        order = [0, GROUP, 1, GROUP + 1, 2, GROUP + 2, 3, GROUP + 3]
                        for t in range(NT):
                            pe.wait_ge(b_free, it * B_BODY + b_base(h) + 4 + t + 1)
                            project(OB[t % 2][:, :], [
                                (lambda a, i=i: aT[:, a, i, t * P:(t + 1) * P],
                                 lambda b, i=i: o16[:, b, i, :]) for i in order]).then_inc(b_full, 1)

            with pe.Fori(0, ITERS - 1) as it:
                body(it, False)
            body(ITERS - 1, True)


def cross_phase(nc, X, const, const_in, early, ctx_loaded, ctx_in, ctxT_in, WqT, WkT, Wv, WoT, bo, gain, sem):
    with ExitStack() as stack:
        def sb(name, shape, dt=F32):
            return stack.enter_context(nc.sbuf_tensor(name, shape, dt))

        def ps(name, shape, dt=F32):
            return stack.enter_context(nc.psum_tensor(name, shape, dt))

        CH = SEQ
        XH, XD = 8, 64
        HID = XH * XD
        JT = HID // P
        NN = DM // P
        ident = const[:, C_ID:C_ID + P]
        const_x = sb("x_const", [P, C_END - C_ONES])
        ones2 = const_x[:, 0:32]
        pick2 = const_x[:, 32:32 + P]

        st = sb("x_st", [P, NT, 6])
        mv = sb("x_mv", [P, NT, 2])
        rs = sb("x_rs", [P, NT])
        xn = sb("x_xn", [P, DM])
        ctx_raw = sb("x_ctx", [P, NT, DM])
        XS = sb("x_XS", [P, BATCH, DM], F16)
        CS = sb("x_CS", [P, BATCH, DM], F16)
        w_raw = sb("x_wraw", [P, 2, HID])
        w16 = sb("x_w16", [P, 2, 2, HID], F16)
        wv_sb = sb("x_wv", [64, XH, CH])
        wo_sb = sb("x_wo", [64, XH, CH])
        U = sb("x_U_sb", [64, HID])
        bo_sb = sb("x_bias", [P, 1])
        g_raw = sb("x_graw", [P, 1])
        g8 = sb("x_g8", [P, 1])
        ct = sb("x_ct", [P, 2, NN, CH])
        kmax = sb("x_kmax", [P, 2, JT])
        knmax = sb("x_knmax", [P, 2, JT])
        ksum = sb("x_ksum", [P, 2, JT])
        krec = sb("x_krec", [P, JT])
        ek = sb("x_ek", [P, 2, JT, DM])
        eT = sb("x_eT", [P, NN, HID])
        qmax = sb("x_qmax", [P, NN, XH])
        qsum = sb("x_qsum", [P, 2, NN, XH])
        qs = sb("x_qs", [P, 2, NN, HID])
        qT = sb("x_qT", [P, JT, DM])
        GT = sb("x_GT", [64, HID])
        MT = sb("x_MT", [P, JT, CH])
        y = sb("x_y", [P, NT, DM])
        sq = ctx_raw
        root = sb("x_root", [P, 2, DM])
        scaled = sb("x_scaled", [P, 2, DM])

        KB = [ps(f"x_KB{i}", [P, DM]) for i in range(2)]
        QB = [ps(f"x_QB{i}", [P, DM]) for i in range(2)]
        TB = [ps(f"x_TB{i}", [P, 4, P]) for i in range(2)]
        GB = ps("x_GB", [P, DM])
        YB = ps("x_YB", [P, DM])

        names = ("wqk_loaded wvo_loaded small_loaded own var_ready root_ready xn_ready xs_hi xs_lo cs_hi cs_lo "
                 "wqk_hi wqk_lo u_full u_ready k_full k_free kneg_ready q_full q_free q_exp "
                 "qrec_ready q_normed t_full t_free g_full gt_ready m_full mt_ready y_full y_free sq_ready "
                 "ss_full rec_ready bc_full bc_free ssroot_ready const2").split()
        s = {n: sem("x_" + n) for n in names}
        ct_loaded = [sem("x_ct_loaded0"), sem("x_ct_loaded1")]
        block = stack.enter_context(nc.Block())

        @block.sync
        def _(sp):
            sp.dma_start(w_raw[0:64, 0, :], WqT).then_inc(s["wqk_loaded"], 16)
            sp.dma_start(w_raw[64:128, 0, :], WqT).then_inc(s["wqk_loaded"], 16)
            sp.dma_start(w_raw[0:64, 1, :], WkT).then_inc(s["wqk_loaded"], 16)
            sp.dma_start(w_raw[64:128, 1, :], WkT).then_inc(s["wqk_loaded"], 16)
            for t in range(NT):
                sp.dma_start(ctx_raw[:, t, :], ctx_in[t * P:(t + 1) * P, :]).then_inc(ctx_loaded[t], 16)
                if t == 0:
                    sp.dma_start(wv_sb[:, :, :], Wv.rearrange("(h e) c -> e h c", e=XD)).then_inc(s["wvo_loaded"], 16)
                    sp.dma_start(wo_sb[:, :, :], WoT.rearrange("(h e) c -> e h c", e=XD)).then_inc(s["wvo_loaded"], 16)
            for r in range(2):
                sp.dma_start(bo_sb[64 * r:64 * r + 64, :], bo.rearrange("(c o) -> c o", o=1)).then_inc(s["small_loaded"], 16)
                sp.dma_start(g_raw[64 * r:64 * r + 64, :], gain.rearrange("a c o -> (a c) o")).then_inc(s["small_loaded"], 16)

            sp.dma_start(const_x[:, :], const_in[:, C_ONES:C_END]).then_inc(s["const2"], 16)

            def load_ct(par, b):
                src = ctxT_in[bass.ds(b, 1), :, :].rearrange("o (k p) c -> p (o k) c", p=P)
                sp.dma_start(ct[:, par], src).then_inc(ct_loaded[par], 16)

            load_ct(0, 0)
            load_ct(1, 1)
            with sp.Fori(0, NT - 1) as it:
                for par in range(2):
                    sp.wait_ge(s["g_full"], it * 2 + par + 1)
                    load_ct(par, it * 2 + par + 2)

        @block.scalar
        def _(act):
            def copy(dst, src, scale=1.0):
                return nc.scalar.activation(dst, src, ACT.Copy, scale=scale)

            act.sem_inc(s["k_free"], 2)
            act.sem_inc(s["t_free"], 2)
            act.wait_ge(s["wqk_loaded"], 64)
            copy(w16[:, :, 0, :], w_raw[:, :, :], WS).then_inc(s["wqk_hi"], 1)

            def context_high(n):
                t, r = divmod(n, 2)
                c = slice(64 * r, 64 * r + 64)
                act.wait_ge(ctx_loaded[t], 32)
                copy(CS[c, n, :], ctx_raw[c, t, :]).then_inc(s["cs_hi"], 1)

            context_high(0)
            context_high(1)
            act.wait_ge(s["var_ready"], 1)
            nc.scalar.activation(rs[:, :], rs[:, :], ACT.Sqrt).then_inc(s["root_ready"], 1)

            def x_high(t):
                act.wait_ge(s["xn_ready"], t + 1)
                for r in range(2):
                    c = slice(64 * r, 64 * r + 64)
                    copy(row(XS[c, bass.ds(2 * t + r, 1), :]), xn[c, :]).then_inc(s["xs_hi"], 1)

            def k_exp(n, par, j):
                act.wait_ge(s["kneg_ready"], n * JT + j + 1)
                nc.scalar.activation(ek[:, par, j, :], KB[j % 2][:, :], ACT.Exp, scale=1 / WS,
                                     bias=knmax[:, par, j:j + 1],
                                     accum_out=ksum[:, par, j:j + 1]).then_inc(s["k_free"], 1)

            def q_exp(n, par, half):
                act.wait_ge(s["q_free"], n * NN + 2 * half + 2 + 2)
                c = slice(2 * half, 2 * half + 2)
                nc.scalar.activation(qs[:, par, c, :], qs[:, par, c, :], ACT.Exp, scale=1 / WS)\
                    .then_inc(s["q_exp"], 1)

            def square(t):
                act.wait_ge(s["y_free"], t + 2)
                act.wait_ge(s["cs_lo"], BATCH)
                nc.scalar.activation(sq[:, t, :], y[:, t, :], ACT.Square).then_inc(s["sq_ready"], 1)

            def root_of(i):
                act.wait_ge(s["ss_full"], 4 * i + 4)
                nc.scalar.activation(root[:, i, :], (KB[0], QB[0])[i][:, :], ACT.Sqrt).then_inc(s["ssroot_ready"], 1)

            def transposed(n, k, dst):
                act.wait_ge(s["t_full"], n * 8 + k + 1)
                copy(dst, TB[k % 2][:, :, :]).then_inc(s["t_free"], 1)

            for j in range(JT):
                if j == 2:
                    x_high(0)
                k_exp(0, 0, j)
            for half in range(2):
                q_exp(0, 0, half)
            act.wait_ge(s["u_full"], 1)
            copy(U[:, :], GB[0:64, :]).then_inc(s["u_ready"], 1)
            context_high(2)
            context_high(3)

            def body(it, first, last):
                for par in range(2):
                    n = it * 2 + par
                    more = not (last and par == 1)
                    for k in range(4):
                        transposed(n, k, eT[:, k, :].rearrange("p (a b) -> p a b", b=P))
                        if more and k % 2:
                            k_exp(n + 1, 1 - par, k // 2)
                    if more:
                        q_exp(n + 1, 1 - par, 0)
                        if par == 0 and not last:
                            x_high(it + 1)
                        k_exp(n + 1, 1 - par, 2)
                        k_exp(n + 1, 1 - par, 3)
                    else:
                        for t in range(4):
                            square(t)
                        root_of(0)
                    if first:
                        for m in range(6 * par + 4, 6 * par + 7):
                            context_high(m)
                    act.wait_ge(s["g_full"], n + 1)
                    copy(GT[:, :], GB[0:64, :]).then_inc(s["gt_ready"], 1)
                    for k in range(4):
                        transposed(n, 4 + k, qT[:, k, :].rearrange("p (a b) -> p a b", b=P))
                    if more:
                        q_exp(n + 1, 1 - par, 1)
                    if first:
                        for m in range(6 * par + 7, 6 * par + 10):
                            context_high(m)

            body(0, True, False)
            with act.Fori(1, NT - 1) as it:
                body(it, False, False)
            body(NT - 1, False, True)
            for t in range(4, NT):
                square(t)
            root_of(1)

        @block.gpsimd
        def _(pool):
            def norm(n, par, half):
                pool.wait_ge(s["qrec_ready"], n * 2 + half + 1)
                c = slice(2 * half, 2 * half + 2)
                v3 = qs[:, par, c, :].rearrange("p a (h d) -> p (a h) d", d=XD)
                r3 = qsum[:, par, c, :].rearrange("p a h -> p (a h)").unsqueeze(2).to_broadcast([P, 2 * XH, XD])
                nc.gpsimd.tensor_tensor(v3, v3, r3, ALU.mult).then_inc(s["q_normed"], 1)

            def context_low(n):
                t, r = divmod(n, 2)
                a, b = slice(64 * r, 64 * r + 64), slice(64 - 64 * r, 128 - 64 * r)
                pool.wait_ge(s["cs_hi"], n + 1)
                nc.gpsimd.tensor_tensor(CS[b, n, :], ctx_raw[a, t, :], CS[a, n, :], ALU.subtract).then_inc(s["cs_lo"], 1)
                pool.wait_ge(s["cs_lo"], n + 1)

            for n in range(2):
                context_low(n)
            norm(0, 0, 0)
            norm(0, 0, 1)
            pool.wait_ge(s["q_normed"], 2)
            context_low(2)
            context_low(3)
            for i in range(4):
                norm(1 + i // 2, 1 - i // 2, i % 2)
                pool.wait_ge(s["q_normed"], 3 + i)
                for n in range(3 * i + 4, 3 * i + 7):
                    context_low(n)

            def body(it, last):
                for par in range(2):
                    if not (last and par == 1):
                        norm(it * 2 + par + 1, 1 - par, 0)
                        norm(it * 2 + par + 1, 1 - par, 1)

            with pool.Fori(1, NT - 1) as it:
                body(it, False)
            body(NT - 1, True)
            early(pool)

        @block.vector
        def _(dve):
            own = Chain(dve, s["own"])
            dve.sem_inc(s["q_free"], 2)
            dve.sem_inc(s["y_free"], 1)
            dve.sem_inc(s["mt_ready"], 1)
            dve.sem_inc(s["bc_free"], 2)
            def normed(t):
                if not (type(t) is int and t == 0):
                    dve.wait_ge(s["xs_lo"], 2 * t)
                    dve.wait_ge(s["xs_hi"], 2 * t)
                mean = mv[:, bass.ds(t, 1), 0:1].rearrange("p o n -> p (o n)")
                nc.vector.tensor_scalar(xn[:, :], row(X[:, bass.ds(t, 1), :]), mean, rs[:, bass.ds(t, 1)],
                                        ALU.subtract, ALU.mult).then_inc(s["xn_ready"], 1)

            def x_low(t):
                dve.wait_ge(s["xn_ready"], t + 1)
                for r in range(2):
                    a, b = slice(64 * r, 64 * r + 64), slice(64 - 64 * r, 128 - 64 * r)
                    dve.wait_ge(s["xs_hi"], 2 * t + r + 1)
                    nc.vector.tensor_tensor(row(XS[b, bass.ds(2 * t + r, 1), :]), xn[a, :],
                                            row(XS[a, bass.ds(2 * t + r, 1), :]), ALU.subtract).then_inc(s["xs_lo"], 1)


            def k_max(n, par, j):
                dve.wait_ge(s["k_full"], n * JT + j + 1)
                own.link(nc.vector.tensor_reduce(kmax[:, par, j:j + 1], KB[j % 2][:, :], AX.X, ALU.max))
                nc.vector.tensor_scalar(knmax[:, par, j:j + 1], kmax[:, par, j:j + 1], -1 / WS, None,
                                        ALU.mult).then_inc(s["kneg_ready"], 1)

            def q_shift(n, par, i):
                dve.wait_ge(s["q_full"], n * NN + i + 1)
                v3 = QB[i % 2][:, :].rearrange("p (h d) -> p h d", d=XD)
                own.link(nc.vector.tensor_reduce(qmax[:, i, :], v3, AX.X, ALU.max))
                nc.vector.tensor_tensor(qs[:, par, i, :].rearrange("p (h d) -> p h d", d=XD), v3,
                                        qmax[:, i, :].unsqueeze(2).to_broadcast([P, XH, XD]),
                                        ALU.subtract).then_inc(s["q_free"], 1)

            def q_sum(n, par, half):
                dve.wait_ge(s["q_exp"], n * 2 + half + 1)
                c = slice(2 * half, 2 * half + 2)
                v3 = qs[:, par, c, :].rearrange("p a (h d) -> p (a h) d", d=XD)
                r2 = qsum[:, par, c, :].rearrange("p a h -> p (a h)")
                own.link(nc.vector.tensor_reduce(r2, v3, AX.X, ALU.add))
                nc.vector.reciprocal(r2, r2).then_inc(s["qrec_ready"], 1)

            for t in range(NT):
                if t == 3:
                    dve.wait_ge(s["wqk_hi"], 1)
                    nc.vector.scalar_tensor_tensor(w16[:, :, 1, :], w_raw[:, :, :], WS, w16[:, :, 0, :],
                                                   ALU.mult, ALU.subtract).then_inc(s["wqk_lo"], 1)
                own.mark(layernorm_tile(nc, X, st, t))
            layernorm_finish(own, nc, st, mv, rs).then_inc(s["var_ready"], 1)
            k_max(0, 0, 0)
            k_max(0, 0, 1)
            dve.wait_ge(s["root_ready"], 1)
            own.link(nc.vector.reciprocal(rs[:, :], rs[:, :]))
            normed(0)
            k_max(0, 0, 2)
            k_max(0, 0, 3)
            x_low(0)
            dve.wait_ge(s["small_loaded"], 64)
            own.link(nc.vector.tensor_scalar(g8[:, :], g_raw[:, :], float(np.sqrt(CH)), None, ALU.mult))
            for i in range(NN):
                q_shift(0, 0, i)
                if i % 2:
                    q_sum(0, 0, i // 2)
            PRO = own.n
            BODY = 2 * (JT + NN + 2) + 2 * 2

            def read_y(it):
                dve.wait_ge(s["y_full"], it + 1)
                nc.vector.tensor_scalar(row(y[:, bass.ds(it, 1), :]), YB[:, :], bo_sb[:, :], None, ALU.add)\
                    .then_inc(s["y_free"], 1)

            def inverse_norm(i):
                dve.wait_ge(s["ssroot_ready"], i + 1)
                own.link(nc.vector.tensor_scalar(root[:, i, :], root[:, i, :], 1e-12, None, ALU.max))
                nc.vector.reciprocal(root[:, i, :], root[:, i, :]).then_inc(s["rec_ready"], 1)

            def body(it, first, last):
                own.enter(PRO, it, BODY)
                for par in range(2):
                    n = it * 2 + par
                    more = not (last and par == 1)
                    if more:
                        k_max(n + 1, 1 - par, 0)
                        k_max(n + 1, 1 - par, 1)
                        q_shift(n + 1, 1 - par, 0)
                        q_shift(n + 1, 1 - par, 1)
                    if par == 0 and not last:
                        normed(it + 1)
                    if more:
                        k_max(n + 1, 1 - par, 2)
                        k_max(n + 1, 1 - par, 3)
                        q_sum(n + 1, 1 - par, 0)
                        q_shift(n + 1, 1 - par, 2)
                        q_shift(n + 1, 1 - par, 3)
                    if par == 0 and not first:
                        read_y(it - 1)
                    if par == 0 and not last:
                        x_low(it + 1)
                    if not more:
                        inverse_norm(0)
                    dve.wait_ge(s["k_free"], n * JT + JT + 2)
                    own.link(nc.vector.reciprocal(krec[:, :], ksum[:, par, :]))
                    own.link(nc.vector.tensor_scalar(krec[:, :], krec[:, :], XD ** -0.5, None, ALU.mult))
                    dve.wait_ge(s["m_full"], n + 1)
                    for r in range(2):
                        c = slice(64 * r, 64 * r + 64)
                        ins = nc.vector.tensor_tensor(
                            MT[c, :, :], GB[c, :].rearrange("p (j a o) -> p j a o", a=2, o=CH)[:, :, r, :],
                            krec[c, :].unsqueeze(2).to_broadcast([64, JT, CH]), ALU.mult)
                    ins.then_inc(s["mt_ready"], 1)
                    if more:
                        q_sum(n + 1, 1 - par, 1)
                if not last:
                    assert own.n == BODY, (own.n, BODY)

            body(0, True, False)
            with dve.Fori(1, NT - 1) as it:
                body(it, False, False)
            body(NT - 1, False, True)
            read_y(NT - 1)
            for t in range(NT):
                if t == 4:
                    inverse_norm(1)
                dve.wait_ge(s["bc_full"], t + 1)
                ins = nc.vector.scalar_tensor_tensor(scaled[:, t % 2, :], y[:, t, :], g8[:, :], (KB[1], QB[1])[t % 2][:, :],
                                                     ALU.mult, ALU.mult)
                ins.then_inc(s["bc_free"], 1)
                dve.wait_ge(s["bc_free"], t + 3)
                own.mark(nc.vector.tensor_tensor(X[:, t, :], X[:, t, :], scaled[:, t % 2, :], ALU.add))
            own.wait()

        @block.tensor
        def _(pe):
            pe.wait_ge(s["wqk_lo"], 1)

            def k_proj(n, j):
                if j == 0:
                    pe.wait_ge(s["cs_lo"], n + 1)
                pe.wait_ge(s["k_free"], n * JT + j + 1)
                mov = CS[:, bass.ds(n, 1), :].rearrange("p o n -> p (o n)")
                for a in range(2):
                    ins = nc.tensor.matmul(KB[j % 2][:, :], w16[:, 1, a, j * P:(j + 1) * P], mov,
                                           start=(a == 0), stop=(a == 1))
                ins.then_inc(s["k_full"], 1)

            def q_proj(n, i):
                if i == 0:
                    pe.wait_ge(s["xs_lo"], n + 1)
                pe.wait_ge(s["q_free"], n * NN + i + 1)
                stat = XS[:, bass.ds(n, 1), i * P:(i + 1) * P].rearrange("p o n -> p (o n)")
                for a in range(2):
                    ins = nc.tensor.matmul(QB[i % 2][:, :], stat, w16[:, 0, a, :], start=(a == 0), stop=(a == 1))
                ins.then_inc(s["q_full"], 1)

            def k_transposes(n, par, k):
                pe.wait_ge(s["t_free"], n * 8 + k + 1)
                for j in range(JT):
                    ins = nc.tensor.transpose(TB[k % 2][:, j, :], ek[:, par, j, k * P:(k + 1) * P], ident)
                ins.then_inc(s["t_full"], 1)

            def q_transposes(n, par, k):
                pe.wait_ge(s["t_free"], n * 8 + 4 + k + 1)
                for i in range(NN):
                    ins = nc.tensor.transpose(TB[k % 2][:, i, :], qs[:, par, i, k * P:(k + 1) * P], ident)
                ins.then_inc(s["t_full"], 1)

            for j in range(JT):
                k_proj(0, j)
            for i in range(NN):
                q_proj(0, i)
            pe.wait_ge(s["wvo_loaded"], 32)
            for h in range(XH):
                ins = nc.tensor.matmul(GB[0:64, h * CH:(h + 1) * CH], wv_sb[:, h, :], wo_sb[:, h, :],
                                       start=True, stop=True)
            ins.then_inc(s["u_full"], 1)

            def out_proj(n, par, it):
                pe.wait_ge(s["mt_ready"], n + 2)
                pe.wait_ge(s["t_free"], n * 8 + 8 + 2)
                if par == 0:
                    pe.wait_ge(s["y_free"], it + 1)
                for j in range(JT):
                    ins = nc.tensor.matmul(YB[64 * par:64 * par + 64, :], MT[:, j, :], qT[:, j, :],
                                           start=(j == 0), stop=(j == JT - 1))
                if par == 1:
                    ins.then_inc(s["y_full"], 1)

            def squares(t):
                pe.wait_ge(s["sq_ready"], t + 1)
                r = 32 * (t % 4)
                nc.tensor.matmul((KB[0], QB[0])[t // 4][r:r + 32, :], ones2, sq[:, t, :],
                                 start=True, stop=True).then_inc(s["ss_full"], 1)

            def broadcast(t):
                pe.wait_ge(s["rec_ready"], t // 4 + 1)
                pe.wait_ge(s["bc_free"], t + 1)
                r = 32 * (t % 4)
                nc.tensor.matmul((KB[1], QB[1])[t % 2][:, :], pick2[r:r + 32, :], root[r:r + 32, t // 4, :],
                                 start=True, stop=True).then_inc(s["bc_full"], 1)

            def body(it, first, last):
                for par in range(2):
                    n = it * 2 + par
                    more = not (last and par == 1)
                    if more:
                        k_proj(n + 1, 0)
                        k_proj(n + 1, 1)
                        q_proj(n + 1, 0)
                        q_proj(n + 1, 1)
                    pe.wait_ge(s["k_free"], n * JT + JT + 2)
                    for k in range(NN):
                        k_transposes(n, par, k)
                    if par == 1:
                        out_proj(n - 1, 0, it)
                    elif not first:
                        out_proj(n - 1, 1, it - 1)
                    if more:
                        k_proj(n + 1, 2)
                        k_proj(n + 1, 3)
                        q_proj(n + 1, 2)
                        q_proj(n + 1, 3)
                    else:
                        pe.wait_ge(s["const2"], 16)
                        pe.wait_ge(s["k_free"], BATCH * JT + 2)
                        pe.wait_ge(s["q_free"], BATCH * NN + 2)
                        for t in range(4):
                            squares(t)
                    if first and par == 0:
                        pe.wait_ge(s["u_ready"], 1)
                    pe.wait_ge(s["t_free"], n * 8 + 4 + 2)
                    pe.wait_ge(ct_loaded[par], (it + 1) * 16)
                    pe.wait_ge(s["mt_ready"], n + 1)
                    for k in range(NN):
                        ins = nc.tensor.matmul(GB[0:64, :], ct[:, par, k, :], eT[:, k, :],
                                               start=(k == 0), stop=(k == NN - 1))
                    ins.then_inc(s["g_full"], 1)
                    pe.wait_ge(s["q_normed"], n * 2 + 2)
                    q_transposes(n, par, 0)
                    q_transposes(n, par, 1)
                    pe.wait_ge(s["gt_ready"], n + 1)
                    for j in range(JT):
                        ins = nc.tensor.matmul(GB[:, j * P:(j + 1) * P], GT[:, j * P:(j + 1) * P],
                                               U[:, j * P:(j + 1) * P], start=True, stop=True)
                    ins.then_inc(s["m_full"], 1)
                    q_transposes(n, par, 2)
                    q_transposes(n, par, 3)

            body(0, True, False)
            with pe.Fori(1, NT - 1) as it:
                body(it, False, False)
            body(NT - 1, False, True)
            for t in range(4, NT - 1):
                squares(t)
            out_proj(BATCH - 1, 1, NT - 1)
            for t in range(4):
                broadcast(t)
            squares(NT - 1)
            for t in range(4, NT):
                broadcast(t)


FF = 1376
FT = -(-FF // P)
QB16 = 16
SPLIT = 128
FP8_MAX = 448.0
GSCALE = 448.0 * 6.0
TINY = 1e-8
ROUND = 1.5 * 2.0 ** 23
R4 = 1.5 * 2.0 ** 20
EXPONENT = 0x7F800000
RMAX = bass.bass_isa.ReduceOp.max


def rows_of(i):
    return min(P, FF - i * P)


def blocks(ap):
    return ap.rearrange("p (b e) -> p b e", e=QB16)


def spread(scales, parts, n):
    return scales.unsqueeze(2).to_broadcast([parts, n, QB16])


def start_gathers(pool, gathered, idx_in, idx_mid, idx_loaded, g_in, wT, ri_in_cols, ri_mid_cols, ri_mid_last):
    pool.dma_start(idx_in[:, :], ri_in_cols).then_inc(idx_loaded, 16)
    pool.dma_start(idx_mid[:, 0:FT - 1], ri_mid_cols).then_inc(idx_loaded, 16)
    pool.dma_start(idx_mid[0:rows_of(FT - 1), FT - 1:FT], ri_mid_last).then_inc(idx_loaded, 16)
    pool.wait_ge(idx_loaded, 48)
    for m in range(2):
        for k in range(KT):
            pool.indirect_dma_start(
                out=gathered[:, m, k * FF:(k + 1) * FF], out_offset=None, in_=wT[m][:, :],
                in_offset=bass.IndirectOffsetOnAxis(ap=idx_in[:, k:k + 1], axis=0)).then_inc(g_in[m], 16)


def weight_phase(nc, X, st, mv, rs, const, w16, wd16, gathered, idx_mid, g_in, wdT, scratch, sem):
    with ExitStack() as stack:
        def sb(name, shape, dt=F32):
            return stack.enter_context(nc.sbuf_tensor(name, shape, dt))

        def ps(name, shape, dt=F32):
            return stack.enter_context(nc.psum_tensor(name, shape, dt))

        MID = 6
        RING = 3
        ident = const[:, C_ID:C_ID + P]
        ident16 = sb("p_ident16", [P, P], F16)
        halves = [gathered[:, m, :].bitcast(F16).rearrange("p (i a k) -> p i a k", i=FT, a=2) for m in range(2)]
        down = sb("p_down", [P, FT, DM])
        down16 = sb("p_down16", [P, 2, KT, FF], F16)
        amax = sb("p_amax", [P, 2, 32])
        scale = sb("p_scale", [P, RING, 32])
        rec = sb("p_rec", [P, 2, 32])
        ratio = sb("p_ratio", [P, RING, DM])
        quant = sb("p_quant", [P, RING, DM])
        rows16 = sb("p_rows16", [P, 4, 2, DM], F16)
        AB = [ps(f"p_AB{i}", [P, DM]) for i in range(4)]
        BB = [ps(f"p_BB{i}", [P, 2, KT, P], F16) for i in range(4)]

        g_down, var_ready, root_ready = sem("p_g_down"), sem("p_var_ready"), sem("p_root_ready")
        stored = [[sem(f"p_stored{m}{r}") for r in range(4)] for m in range(2)]
        g_mid = [[sem(f"p_g_mid{m}{part}") for part in range(2)] for m in range(2)]
        a_full, a_read, rounded, q_ready, own_sem = (sem("p_a_full"), sem("p_a_read"), sem("p_rounded"),
                                                     sem("p_q_ready"), sem("p_own"))
        hi_ready, lo_ready, id_ready = sem("p_hi_ready"), sem("p_lo_ready"), sem("p_id_ready")
        b_full, b_act, b_dve = sem("p_b_full"), sem("p_b_act"), sem("p_b_dve")
        ROWS = [(m, i) for m in range(2) for i in range(FT)]
        DOWN = [(o, c) for c in range(3) for o in range(KT)]
        NR, NQ = len(ROWS), len(ROWS) + len(DOWN)
        BACK = ([(0, i) for i in range(FT)] + [(2, i) for i in range(8)] + [(1, i) for i in range(MID)] +
                [(2, i) for i in range(8, FT)] + [(1, i) for i in range(MID, FT)])
        BACK_FROM = NR + 5

        def back_after(j):
            if j < BACK_FROM:
                return range(0)
            return range(2 * (j - BACK_FROM), 2 * (j - BACK_FROM) + 2)

        TAIL = range(back_after(NQ - 1).stop, len(BACK))

        def shape_of(j):
            if j < NR:
                n = rows_of(ROWS[j][1])
                return n, DM, [rows16[0:n, j % 4, a, :] for a in range(2)]
            o, c = DOWN[j - NR]
            w = min(512, FF - 512 * c)
            return P, w, [down16[:, a, o, 512 * c:512 * c + w] for a in range(2)]

        def stores_before(m, r, j):
            return len([1 for q in range(min(j, NR)) if ROWS[q][0] == m and q % 4 == r])

        def back_banks(b):
            m, i = BACK[b]
            n = rows_of(i)
            if m < 2:
                return BB[b % 4][:, :, :, 0:n], w16[:, m, :, :, i * P:i * P + n]
            return (BB[b % 4][0:n].rearrange("p a k c -> p a (k c)"), wd16[0:n, :, i, :])

        block = stack.enter_context(nc.Block())

        @block.gpsimd
        def _(pool):
            for i in range(FT):
                n = rows_of(i)
                pool.indirect_dma_start(
                    out=down[0:n, i, :], out_offset=None, in_=wdT[:, :],
                    in_offset=bass.IndirectOffsetOnAxis(ap=idx_mid[0:n, i:i + 1], axis=0)).then_inc(g_down, 16)

            def gather_halves(m, i):
                if i == 0:
                    for r in range(4):
                        pool.wait_ge(stored[m][r], 16 * stores_before(m, r, NR))
                    pool.wait_ge(a_full, (m + 1) * FT)
                n = rows_of(i)
                pool.indirect_dma_start(
                    out=halves[m][0:n, i].rearrange("p a k -> p (a k)"), out_offset=None, in_=scratch[m][:, :],
                    in_offset=bass.IndirectOffsetOnAxis(ap=idx_mid[0:n, i:i + 1], axis=0)).then_inc(g_mid[m][i // MID], 16)

            for j in range(NQ):
                n, w, dst = shape_of(j)
                pool.wait_ge(hi_ready, j + 1)
                nc.gpsimd.tensor_tensor(dst[1], quant[0:n, j % RING, 0:w], dst[0], ALU.subtract).then_inc(lo_ready, 1)
                if FT + 2 <= j < 2 * FT + 2:
                    gather_halves(0, j - FT - 2)
                elif NR + 2 <= j < NQ:
                    gather_halves(1, j - NR - 2)
            gather_halves(1, FT - 1)

        @block.sync
        def _(sp):
            for j, (m, i) in enumerate(ROWS):
                n = rows_of(i)
                sp.wait_ge(lo_ready, j + 1)
                sp.dma_start(scratch[m][i * P:i * P + n, :], rows16[0:n, j % 4].rearrange("p a k -> p (a k)"))\
                    .then_inc(stored[m][j % 4], 16)

        @block.tensor
        def _(pe):
            def back(b):
                m, i = BACK[b]
                n = rows_of(i)
                if b == 0:
                    pe.wait_ge(id_ready, 1)
                if m < 2:
                    pe.wait_ge(g_mid[m][i // MID], 16 * (MID if i < MID else FT - MID))
                if m == 2:
                    pe.wait_ge(lo_ready, NR + KT * (i // 4 + 1))
                if b >= 4:
                    pe.wait_ge(b_dve if b % 2 else b_act, (b - 4) // 2 + 1)
                for a in range(2):
                    for k in range(KT):
                        if m < 2:
                            ins = nc.tensor.transpose(BB[b % 4][:, a, k, 0:n], halves[m][0:n, i, a, k * P:(k + 1) * P],
                                                      ident16[0:n, 0:n])
                        else:
                            ins = nc.tensor.transpose(BB[b % 4][0:n, a, k, :], down16[:, a, k, i * P:i * P + n],
                                                      ident16[:, :])
                ins.then_inc(b_full, 1)

            for j in range(NQ):
                if j >= 4:
                    pe.wait_ge(a_read, j - 3)
                if j < NR:
                    m, i = ROWS[j]
                    n = rows_of(i)
                    pe.wait_ge(g_in[m], 16 * KT)
                    for k in range(KT):
                        ins = nc.tensor.transpose(AB[j % 4][0:n, k * P:(k + 1) * P],
                                                  gathered[:, m, k * FF + i * P:k * FF + i * P + n], ident)
                else:
                    o, c = DOWN[j - NR]
                    pe.wait_ge(g_down, 16 * FT)
                    for i in range(4 * c, min(4 * c + 4, FT)):
                        n = rows_of(i)
                        ins = nc.tensor.transpose(AB[j % 4][:, (i - 4 * c) * P:(i - 4 * c) * P + n],
                                                  down[0:n, i, o * P:(o + 1) * P], ident[0:n, 0:n])
                ins.then_inc(a_full, 1)
                for b in back_after(j):
                    back(b)
            for b in TAIL:
                back(b)

        @block.scalar
        def _(act):
            nc.scalar.activation(ident16[:, :], ident, ACT.Copy).then_inc(id_ready, 1)

            def high(j):
                n, w, dst = shape_of(j)
                act.wait_ge(q_ready, j + 1)
                if 4 <= j < NR + 4 and j < NR:
                    m = ROWS[j - 4][0]
                    act.wait_ge(stored[m][j % 4], 16 * stores_before(m, j % 4, j - 3))
                nc.scalar.activation(dst[0], quant[0:n, j % RING, 0:w], ACT.Copy).then_inc(hi_ready, 1)

            def back(b):
                if b % 2 == 0:
                    bank, dst = back_banks(b)
                    act.wait_ge(b_full, b + 1)
                    nc.scalar.activation(dst, bank, ACT.Copy).then_inc(b_act, 1)

            for j in range(NQ):
                n, w, dst = shape_of(j)
                act.wait_ge(a_read, j + 1)
                r = ratio[0:n, j % RING, 0:w]
                nc.scalar.activation(r, r, ACT.Copy, scale=WS, bias=ROUND).then_inc(rounded, 1)
                if j >= 1:
                    high(j - 1)
                for b in back_after(j):
                    back(b)
            high(NQ - 1)
            for b in TAIL:
                back(b)
            act.wait_ge(var_ready, 1)
            nc.scalar.activation(rs[:, :], rs[:, :], ACT.Sqrt).then_inc(root_ready, 1)

        @block.vector
        def _(dve):
            own = Chain(dve, own_sem)

            def largest(j):
                n, w, dst = shape_of(j)
                dve.wait_ge(a_full, j + 1)
                own.mark(nc.vector.tensor_reduce(amax[0:n, j % 2, 0:w // QB16], blocks(AB[j % 4][0:n, 0:w]), AX.X,
                                                 ALU.max, apply_absolute_value=True))

            def scales(j):
                n, w, dst = shape_of(j)
                nb = w // QB16
                dve.wait_ge(own_sem, 3 * j + 1)
                own.mark(nc.vector.tensor_scalar(scale[0:n, j % RING, 0:nb], amax[0:n, j % 2, 0:nb], WS / 7.0,
                                                 WS * TINY, ALU.mult, ALU.max))

            def reciprocals(j):
                n, w, dst = shape_of(j)
                nb = w // QB16
                dve.wait_ge(own_sem, 3 * j + 2)
                own.mark(nc.vector.reciprocal(rec[0:n, j % 2, 0:nb], scale[0:n, j % RING, 0:nb]))

            def ratios(j):
                n, w, dst = shape_of(j)
                nb = w // QB16
                dve.wait_ge(own_sem, 3 * j + 3)
                nc.vector.tensor_tensor(blocks(ratio[0:n, j % RING, 0:w]), blocks(AB[j % 4][0:n, 0:w]),
                                        spread(rec[0:n, j % 2, 0:nb], n, nb), ALU.mult).then_inc(a_read, 1)

            def products(j):
                n, w, dst = shape_of(j)
                nb = w // QB16
                dve.wait_ge(rounded, j + 1)
                if j >= RING:
                    dve.wait_ge(lo_ready, j - RING + 1)
                nc.vector.scalar_tensor_tensor(blocks(quant[0:n, j % RING, 0:w]), blocks(ratio[0:n, j % RING, 0:w]),
                                               ROUND, spread(scale[0:n, j % RING, 0:nb], n, nb),
                                               ALU.subtract, ALU.mult).then_inc(q_ready, 1)

            def back(b):
                if b % 2:
                    bank, dst = back_banks(b)
                    dve.wait_ge(b_full, b + 1)
                    nc.vector.tensor_copy(dst, bank).then_inc(b_dve, 1)

            for j in range(NQ + 2):
                if j < NQ:
                    largest(j)
                if 1 <= j <= NQ:
                    if j >= 4:
                        dve.wait_ge(q_ready, j - 3)
                    ratios(j - 1)
                if j < NQ:
                    if j >= 3:
                        dve.wait_ge(q_ready, j - 2)
                    scales(j)
                if j >= 2:
                    products(j - 2)
                if j < NQ:
                    if j >= 2:
                        dve.wait_ge(a_read, j - 1)
                    reciprocals(j)
                    for b in back_after(j):
                        back(b)
            tiles = list(range(NT))
            for b in TAIL:
                back(b)
                if b % 2 and tiles:
                    own.mark(layernorm_tile(nc, X, st, tiles.pop(0)))
            assert not tiles
            layernorm_finish(own, nc, st, mv, rs).then_inc(var_ready, 1)
            dve.wait_ge(root_ready, 1)
            own.link(nc.vector.reciprocal(rs[:, :], rs[:, :]))


def round_fp8(nc, own, y, m):
    own.link(nc.vector.tensor_scalar(m.bitcast(I32), y.bitcast(I32), EXPONENT, None, ALU.bitwise_and))
    own.link(nc.vector.tensor_scalar(m, m, 2.0 ** -6, R4, ALU.max, ALU.mult))
    own.link(nc.vector.tensor_tensor(y, y, m, ALU.add))
    own.link(nc.vector.tensor_tensor(y, y, m, ALU.subtract))


def transposed_parts(c):
    return [(P, 4, 4 * c)] if c < 2 else [(P, FT - 9, 8), (rows_of(FT - 1), 1, FT - 1)]


def feed_forward_phase(nc, X, st, mv, rs, const, const_in, space, w16, wd16, ri_in, out, sem):
    with ExitStack() as stack:
        def sb(name, shape, dt=F32):
            return stack.enter_context(nc.sbuf_tensor(name, shape, dt))

        def ps(name, shape, dt=F32):
            return stack.enter_context(nc.psum_tensor(name, shape, dt))

        ident = const[:, C_ID:C_ID + P]
        NB = DM // QB16
        NBH = FF // QB16
        ON = (DM - SPLIT) // QB16
        OH = (FF - SPLIT) // QB16
        CW = 344
        NC = FF // CW
        assert NC * CW == FF

        iota = sb("f_iota", [P, KT])
        ri_raw = sb("f_ri", [P, DM], I32)
        rif = sb("f_rif", [P, DM])
        hot = sb("f_hot", [P, KT, DM])
        xn = sb("f_xn", [P, 2, DM])
        gmax = sb("f_gmax", [P, NT])
        g1 = sb("f_g1", [P, 1])
        gall = sb("f_gall", [P, 1])
        floor = sb("f_floor", [P, 1])
        amax = sb("f_amax", [P, NB])
        scale = sb("f_scale", [P, NB])
        rec = sb("f_rec", [P, NB])
        xq = sb("f_xq", [P, DM])
        mm = sb("f_mm", [P, FF])
        m2 = sb("f_m2", [P, SPLIT])
        A16 = sb("f_A16", [P, 2, KT, TOK], F16)
        th = sb("f_th", [P, 2, CW])
        gate = sb("f_gate", [P, 2, CW])
        H = space.rearrange("p m n -> p (m n)")[:, 0:NT * FF].rearrange("p (t n) -> p t n", t=NT)
        xT = [H[:, t, 0:DM].rearrange("p (k c) -> p k c", c=P) for t in range(NT)]
        XP = slice(DM, 2 * DM)
        hmax = sb("f_hmax", [P, NT, NBH])
        h1 = sb("f_h1", [P, 1])
        hall = sb("f_hall", [P, 1])
        hfloor = sb("f_hfloor", [P, 1])
        gm = sb("f_gm", [P, 3])
        hs = sb("f_hs", [P, 3, NT, NBH])
        h_split = sb("f_h_split", [P, NT, SPLIT])
        o_amax = sb("f_o_amax", [P, 3, SPLIT // QB16])
        res = sb("f_res", [P, SPLIT])
        hq = sb("f_hq", [P, FF])
        hT = sb("f_hT", [P, 2, FT, P], F16)
        WP = 58 * QB16

        TB = [ps(f"f_TB{i}", [P, 4, P]) for i in range(3)]
        GA = [ps(f"f_GA{i}", [P, DM]) for i in range(2)]
        UA = [ps(f"f_UA{i}", [P, DM]) for i in range(2)]
        YB = ps("f_YB", [P, DM])

        names = ("idx const own hot_ready xn_ready xt_full xt_ready xp_full xp_read gmax_ready gall_ready "
                 "aq_ready at_full a_hi a_lo gu_full th_ready gu_free hmax_ready hall_ready hq_ready ht_full ht_hi "
                 "ht_lo y_full y_read y_stored max_ready scales_ready y8_ready m_ready mt_ready xq_rounded hp_ready pool_own").split()
        s = {n: sem("f_" + n) for n in names}
        block = stack.enter_context(nc.Block())

        @block.sync
        def _(sp):
            sp.dma_start(ri_raw[:, :], ri_in.rearrange("(o n) -> o n", o=1).to_broadcast([P, DM])).then_inc(s["idx"], 16)
            sp.dma_start(iota[:, :], const_in[:, C_IOTA:C_IOTA + KT]).then_inc(s["const"], 16)
            with sp.Fori(0, NT) as t:
                sp.wait_ge(s["y_read"], t + 1)
                sp.dma_start(out[bass.ts(t, P), :], X[:, bass.ds(t, 1), :].rearrange("p o n -> p (o n)"))\
                    .then_inc(s["y_stored"], 16)
            sp.wait_ge(s["y_stored"], 16 * NT)

        @block.gpsimd
        def _(pool):
            pool.wait_ge(s["gmax_ready"], 1)
            nc.gpsimd.partition_all_reduce(gall[:, :], g1[:, :], P, RMAX).then_inc(s["gall_ready"], 1)
            own = Chain(pool, s["pool_own"])
            for t in range(NT):
                pool.wait_ge(s["mt_ready"], t + 1)
                own.link(nc.gpsimd.tensor_tensor(xq[:, :], xq[:, :], mm[:, 0:DM], ALU.add))
                own.link(nc.gpsimd.tensor_tensor(xq[:, :], xq[:, :], mm[:, 0:DM], ALU.subtract))
                nc.gpsimd.tensor_tensor(blocks(xq[:, :]), blocks(xq[:, :]), spread(scale[:, :], P, NB), ALU.mult)\
                    .then_inc(s["xq_rounded"], 1)
            pool.wait_ge(s["hmax_ready"], 1)
            nc.gpsimd.partition_all_reduce(hall[:, :], h1[:, :], P, RMAX).then_inc(s["hall_ready"], 1)

            def over_scale(t):
                hb = H[:, bass.ds(t, 1), :].rearrange("p o (b e) -> p (o b) e", e=QB16)
                nc.gpsimd.tensor_tensor(hb, hb, spread(row(hs[:, 1, bass.ds(t, 1), :]), P, NBH), ALU.mult)\
                    .then_inc(s["y8_ready"], 1)

            def body(t, last):
                if not last:
                    over_scale(t + 1)
                pool.wait_ge(s["m_ready"], t + 1)
                h = row(H[:, bass.ds(t, 1), 0:WP])
                own.link(nc.gpsimd.tensor_tensor(h, h, mm[:, 0:WP], ALU.add))
                own.link(nc.gpsimd.tensor_tensor(h, h, mm[:, 0:WP], ALU.subtract))
                if t >= 1:
                    pool.wait_ge(s["ht_full"], t * 3)
                hb = H[:, bass.ds(t, 1), 0:WP].rearrange("p o (b e) -> p (o b) e", e=QB16)
                nc.gpsimd.tensor_tensor(blocks(hq[:, 0:WP]), hb,
                                        spread(row(hs[:, 2, bass.ds(t, 1), 0:WP // QB16]), P, WP // QB16),
                                        ALU.mult).then_inc(s["hp_ready"], 1)

            pool.wait_ge(s["scales_ready"], 1)
            for t in range(NT):
                body(t, t == NT - 1)

        @block.scalar
        def _(act):
            def copy(dst, src, scale=1.0):
                return nc.scalar.activation(dst, src, ACT.Copy, scale=scale)

            for t in range(NT):
                act.wait_ge(s["xt_full"], t + 1)
                copy(xT[t], TB[t % 2][:, :, :]).then_inc(s["xt_ready"], 1)
            for t in range(NT):
                act.wait_ge(s["xp_full"], t + 1)
                copy(H[:, t, XP], GA[t % 2][:, :]).then_inc(s["xp_read"], 1)

            def high(t):
                act.wait_ge(s["at_full"], t + 1)
                copy(A16[:, 0, :, bass.ts(t, P)], TB[0][:, :, :]).then_inc(s["a_hi"], 1)

            def body(t, last):
                for c in range(NC):
                    if c == NC - 1 and not last:
                        high(t + 1)
                    act.wait_ge(s["gu_full"], t * NC + c + 1)
                    nc.scalar.activation(th[:, c % 2, :], GA[c % 2][:, 0:CW], ACT.Tanh, scale=0.5 / WS)\
                        .then_inc(s["th_ready"], 1)

            high(0)
            with act.Fori(0, NT - 1) as t:
                body(t, False)
            body(NT - 1, True)
            with act.Fori(0, NT) as t:
                for c in range(3):
                    act.wait_ge(s["ht_full"], t * 3 + c + 1)
                    for n, w, lo in transposed_parts(c):
                        ins = copy(hT[0:n, 0, lo:lo + w, :], TB[c][0:n, lo - 4 * c:lo - 4 * c + w, :])
                    ins.then_inc(s["ht_hi"], 1)

        @block.vector
        def _(dve):
            own = Chain(dve, s["own"])
            dve.sem_inc(s["gu_free"], 2)
            for t in range(NT):
                if t >= 2:
                    dve.wait_ge(s["xt_full"], t - 1)
                nc.vector.tensor_scalar(xn[:, t % 2, :], X[:, t, :], mv[:, t, 0:1], rs[:, t:t + 1],
                                        ALU.subtract, ALU.mult).then_inc(s["xn_ready"], 1)
                dve.wait_ge(s["xn_ready"], t + 1)
                own.mark(nc.vector.tensor_reduce(gmax[:, t:t + 1], xn[:, t % 2, :], AX.X, ALU.max,
                                                 apply_absolute_value=True))
                if t == NT // 2:
                    dve.wait_ge(s["idx"], 16)
                    dve.wait_ge(s["const"], 16)
                    own.link(nc.vector.tensor_copy(rif[:, :], ri_raw[:, :]))
                    for k in range(KT):
                        ins = nc.vector.tensor_scalar(hot[:, k, :], rif[:, :], iota[:, k:k + 1], None, ALU.is_equal)
                    ins.then_inc(s["hot_ready"], 1)
            own.wait()
            nc.vector.tensor_reduce(g1[:, :], gmax[:, :], AX.X, ALU.max).then_inc(s["gmax_ready"], 1)
            dve.wait_ge(s["gall_ready"], 1)
            own.link(nc.vector.tensor_scalar(floor[:, :], gall[:, :], 1 / GSCALE, TINY, ALU.mult, ALU.max))
            own.link(nc.vector.tensor_scalar(floor[:, :], floor[:, :], TINY, None, ALU.mult))

            def scales(dst_s, dst_r, amax_, floor_):
                own.link(nc.vector.tensor_scalar(dst_s, amax_, 1 / FP8_MAX, floor_, ALU.mult, ALU.max))
                own.link(nc.vector.reciprocal(dst_r, dst_s))

            def second(rest, floor_):
                nb = SPLIT // QB16
                own.link(nc.vector.tensor_reduce(o_amax[:, 0, :], blocks(rest), AX.X, ALU.max,
                                                 apply_absolute_value=True))
                scales(o_amax[:, 1, :], o_amax[:, 2, :], o_amax[:, 0, :], floor_)
                own.link(nc.vector.tensor_tensor(blocks(rest), blocks(rest), spread(o_amax[:, 2, :], P, nb), ALU.mult))
                round_fp8(nc, own, rest, m2[:, :])
                own.link(nc.vector.tensor_tensor(blocks(rest), blocks(rest), spread(o_amax[:, 1, :], P, nb), ALU.mult))

            def a_lo(t):
                dve.wait_ge(s["a_hi"], t + 1)
                nc.vector.tensor_tensor(A16[:, 1, :, bass.ts(t, P)], TB[0][:, :, :], A16[:, 0, :, bass.ts(t, P)],
                                        ALU.subtract).then_inc(s["a_lo"], 1)

            def token_ratios(t):
                dve.wait_ge(s["xp_read"], t + 1)
                if not (type(t) is int and t == 0):
                    dve.wait_ge(s["at_full"], t)
                xb = H[:, bass.ds(t, 1), XP].rearrange("p o (b e) -> p (o b) e", e=QB16)
                own.link(nc.vector.tensor_reduce(amax[:, :], xb, AX.X, ALU.max, apply_absolute_value=True))
                scales(scale[:, :], rec[:, :], amax[:, :], floor[:, :])
                own.link(nc.vector.tensor_tensor(blocks(xq[:, :]), xb, spread(rec[:, :], P, NB), ALU.mult))

            def token_rounding():
                own.link(nc.vector.tensor_scalar(mm[:, 0:DM].bitcast(I32), xq[:, :].bitcast(I32), EXPONENT, None,
                                                 ALU.bitwise_and))
                nc.vector.tensor_scalar(mm[:, 0:DM], mm[:, 0:DM], 2.0 ** -6, R4, ALU.max, ALU.mult)\
                    .then_inc(s["mt_ready"], 1)

            def token_products(t):
                dve.wait_ge(s["xq_rounded"], t + 1)
                own.link(nc.vector.tensor_tensor(res[:, :], row(H[:, bass.ds(t, 1), 2 * DM - SPLIT:2 * DM]),
                                                 xq[:, DM - SPLIT:], ALU.subtract))
                second(res[:, :], floor[:, :])
                nc.vector.tensor_tensor(xq[:, DM - SPLIT:], xq[:, DM - SPLIT:], res[:, :], ALU.add)\
                    .then_inc(s["aq_ready"], 1)

            token_ratios(0)
            token_rounding()
            token_products(0)
            a_lo(0)

            PRO = own.n
            BODY = 4 + 1 + 1 + 9 + NC

            def hidden(t, c):
                dve.wait_ge(s["th_ready"], t * NC + c + 1)
                own.link(nc.vector.scalar_tensor_tensor(gate[:, c % 2, :], th[:, c % 2, :], 1.0, GA[c % 2][:, 0:CW],
                                                        ALU.add, ALU.mult))
                ht = row(H[:, bass.ds(t, 1), c * CW:(c + 1) * CW])
                nc.vector.scalar_tensor_tensor(ht, gate[:, c % 2, :], 0.5 / WS / WS, UA[c % 2][:, 0:CW],
                                               ALU.mult, ALU.mult).then_inc(s["gu_free"], 1)

            def largest(t, c):
                dve.wait_ge(s["gu_free"], t * NC + c + 3)
                hb = H[:, bass.ds(t, 1), (c - 1) * CW:(c + 1) * CW].rearrange("p o (b e) -> p (o b) e", e=QB16)
                nc.vector.tensor_reduce(row(hmax[:, bass.ds(t, 1), (c - 1) * CW // QB16:(c + 1) * CW // QB16]),
                                        hb, AX.X, ALU.max, apply_absolute_value=True).then_inc(s["max_ready"], 1)

            def body(t, last):
                own.enter(PRO, t, BODY)
                if not last:
                    token_ratios(t + 1)
                    token_rounding()
                hidden(t, 0)
                hidden(t, 1)
                if not last:
                    token_products(t + 1)
                largest(t, 1)
                hidden(t, 2)
                if not last:
                    a_lo(t + 1)
                hidden(t, 3)
                largest(t, 3)
                assert last or own.n == BODY, (own.n, BODY)

            with dve.Fori(0, NT - 1) as t:
                body(t, False)
            body(NT - 1, True)
            PRO1 = PRO + BODY * (NT - 1) + own.n
            own.enter(PRO1, 0, 0)
            dve.wait_ge(s["max_ready"], 2 * NT)
            nc.vector.tensor_reduce(h1[:, :], hmax[:, :, :], AX.XY, ALU.max).then_inc(s["hmax_ready"], 1)
            own.link(nc.vector.tensor_copy(h_split[:, :, :], H[:, :, FF - SPLIT:]))
            dve.wait_ge(s["hall_ready"], 1)
            own.link(nc.vector.tensor_scalar(gm[:, 0:1], hall[:, :], 1 / GSCALE, TINY, ALU.mult, ALU.max))
            own.link(nc.vector.tensor_scalar(hfloor[:, :], gm[:, 0:1], TINY, None, ALU.mult))
            own.link(nc.vector.reciprocal(gm[:, 1:2], gm[:, 0:1]))
            own.link(nc.vector.tensor_scalar(gm[:, 2:3], gm[:, 0:1], 1 / WS, None, ALU.mult))
            scales(hs[:, 0], hs[:, 1], hmax[:, :, :], hfloor[:, :])
            nc.vector.tensor_scalar(hs[:, 2], hs[:, 0], gm[:, 1:2], None, ALU.mult).then_inc(s["scales_ready"], 1)
            dve.wait_ge(s["scales_ready"], 1)
            BODY2 = 1 + 2 + 1 + 1 + 9 + 1

            def x_add(t):
                dve.wait_ge(s["y_full"], t + 1)
                xt = row(X[:, bass.ds(t, 1), :])
                nc.vector.scalar_tensor_tensor(xt, YB[:, :], gm[:, 2:3], xt, ALU.mult, ALU.add)\
                    .then_inc(s["y_read"], 1)

            def h_lo(t):
                for c in range(3):
                    dve.wait_ge(s["ht_hi"], t * 3 + c + 1)
                    for n, w, lo in transposed_parts(c):
                        ins = nc.vector.tensor_tensor(hT[0:n, 1, lo:lo + w, :], TB[c][0:n, lo - 4 * c:lo - 4 * c + w, :],
                                                      hT[0:n, 0, lo:lo + w, :], ALU.subtract)
                    ins.then_inc(s["ht_lo"], 1)

            def quantise(t, before):
                own.enter(PRO2, t, BODY2)
                if before >= 1:
                    dve.wait_ge(s["y8_ready"], t)
                    dve.wait_ge(s["hp_ready"], t)
                h = row(H[:, bass.ds(t, 1), :])
                own.mark(nc.vector.tensor_scalar(mm[:, :].bitcast(I32), h.bitcast(I32), EXPONENT, None, ALU.bitwise_and))
                if before >= 2:
                    x_add(t - 2)
                if before >= 1:
                    h_lo(t - 1)
                own.wait()
                nc.vector.tensor_scalar(mm[:, :], mm[:, :], 2.0 ** -6, R4, ALU.max, ALU.mult).then_inc(s["m_ready"], 1)
                dve.wait_ge(s["m_ready"], t + 1)
                hw = row(H[:, bass.ds(t, 1), WP:])
                own.link(nc.vector.tensor_tensor(hw, hw, mm[:, WP:], ALU.add))
                own.link(nc.vector.tensor_tensor(hw, hw, mm[:, WP:], ALU.subtract))
                hsp = H[:, bass.ds(t, 1), FF - SPLIT:].rearrange("p o (b e) -> p (o b) e", e=QB16)
                own.link(nc.vector.tensor_tensor(blocks(res[:, :]), hsp, spread(row(hs[:, 0, bass.ds(t, 1), OH:]), P,
                                                                                SPLIT // QB16), ALU.mult))
                own.link(nc.vector.tensor_tensor(res[:, :], row(h_split[:, bass.ds(t, 1), :]), res[:, :], ALU.subtract))
                second(res[:, :], hfloor[:, :])
                if before >= 1:
                    dve.wait_ge(s["ht_full"], t * 3)
                hb = H[:, bass.ds(t, 1), WP:].rearrange("p o (b e) -> p (o b) e", e=QB16)
                own.link(nc.vector.tensor_tensor(blocks(hq[:, WP:]), hb,
                                                 spread(row(hs[:, 2, bass.ds(t, 1), WP // QB16:]), P, (FF - WP) // QB16),
                                                 ALU.mult))
                nc.vector.scalar_tensor_tensor(hq[:, FF - SPLIT:], res[:, :], gm[:, 1:2], hq[:, FF - SPLIT:],
                                               ALU.mult, ALU.add).then_inc(s["hq_ready"], 1)
                assert own.n == BODY2, (own.n, BODY2)

            h0 = H[:, 0, :]
            own.link(nc.vector.tensor_tensor(blocks(h0), blocks(h0), spread(hs[:, 1, 0, :], P, NBH), ALU.mult))
            PRO2 = PRO1 + own.n
            quantise(0, 0)
            quantise(1, 1)
            with dve.Fori(2, NT) as t:
                quantise(t, 2)
            x_add(NT - 2)
            h_lo(NT - 1)
            x_add(NT - 1)

        @block.tensor
        def _(pe):
            PASSES = ((0, 0), (0, 1), (1, 0))

            for t in range(NT):
                pe.wait_ge(s["xn_ready"], t + 1)
                if t >= 2:
                    pe.wait_ge(s["xt_ready"], t - 1)
                for k in range(KT):
                    ins = nc.tensor.transpose(TB[t % 2][:, k, :], xn[:, t % 2, k * P:(k + 1) * P], ident)
                ins.then_inc(s["xt_full"], 1)

            def gather(t):
                pe.wait_ge(s["xt_ready"], t + 1)
                if t >= 2:
                    pe.wait_ge(s["xp_read"], t - 1)
                for k in range(KT):
                    ins = nc.tensor.matmul(GA[t % 2][:, :], xT[t][:, k, :], hot[:, k, :],
                                           start=(k == 0), stop=(k == KT - 1))
                ins.then_inc(s["xp_full"], 1)

            def transpose_tokens(t):
                pe.wait_ge(s["aq_ready"], t + 1)
                for k in range(KT):
                    ins = nc.tensor.transpose(TB[0][:, k, :], xq[:, k * P:(k + 1) * P], ident)
                ins.then_inc(s["at_full"], 1)

            pe.wait_ge(s["hot_ready"], 1)
            for t in range(NT):
                gather(t)
            pe.wait_ge(s["xt_ready"], NT)
            transpose_tokens(0)
            pe.wait_ge(s["xp_read"], NT)

            def gate_up(t, last):
                pe.wait_ge(s["a_lo"], t + 1)
                for c in range(NC):
                    pe.wait_ge(s["gu_free"], t * NC + c + 1)
                    for m, bank in enumerate((GA[c % 2], UA[c % 2])):
                        for k in range(KT):
                            for q, (a, b) in enumerate(PASSES):
                                ins = nc.tensor.matmul(bank[:, 0:CW], A16[:, a, k, bass.ts(t, P)],
                                                       w16[:, m, b, k, c * CW:(c + 1) * CW],
                                                       start=(k == 0 and q == 0), stop=(k == KT - 1 and q == 2))
                        if m == 1:
                            ins.then_inc(s["gu_full"], 1)
                        elif c == NC - 1 and not last:
                            transpose_tokens(t + 1)

            with pe.Fori(0, NT - 1) as t:
                gate_up(t, False)
            gate_up(NT - 1, True)

            def transpose_hidden(t):
                pe.wait_ge(s["hq_ready"], t + 1)
                pe.wait_ge(s["hp_ready"], t + 1)
                for c in range(3):
                    for i in range(4 * c, min(4 * c + 4, FT)):
                        n = rows_of(i)
                        ins = nc.tensor.transpose(TB[c][0:n, i - 4 * c, :], hq[:, i * P:i * P + n], ident)
                    ins.then_inc(s["ht_full"], 1)

            def down_product(t, first):
                pe.wait_ge(s["ht_lo"], t * 3 + 3)
                if not first:
                    pe.wait_ge(s["y_read"], t)
                for i in range(FT):
                    n = rows_of(i)
                    for q, (a, b) in enumerate(PASSES):
                        ins = nc.tensor.matmul(YB[:, :], hT[0:n, a, i, :], wd16[0:n, b, i, :],
                                               start=(i == 0 and q == 0), stop=(i == FT - 1 and q == 2))
                ins.then_inc(s["y_full"], 1)

            transpose_hidden(0)
            down_product(0, True)
            transpose_hidden(1)
            with pe.Fori(2, NT) as t:
                down_product(t - 1, False)
                transpose_hidden(t)
            down_product(NT - 1, False)


def decoder_layer(nc, const_in, x_in, ctx_in, ctxT_in, w_q, w_k, w_v, w_o, w_lq, w_lk, w_lv, w_lo,
                  x_WqT, x_WkT, x_Wv, x_WoT, x_bo, x_g, w_gateT, w_upT, w_downT, ri_in, ri_in_cols, ri_mid_cols, ri_mid_last, out):
    scratch = [nc.dram_tensor(f"scratch{m}", (FF, 2 * DM), F16, kind="Internal").ap() for m in range(2)]
    with ExitStack() as ctx:
        def sem(name):
            return ctx.enter_context(nc.semaphore(name))

        tile_loaded = [sem(f"tile_loaded{t}") for t in range(NT)]
        X = ctx.enter_context(nc.sbuf_tensor("X", [P, NT, DM], F32))
        const = ctx.enter_context(nc.sbuf_tensor("const", [P, C_COMMON], F32))
        attention_phase(nc, X, const, const_in, tile_loaded, x_in, w_q, w_k, w_v, w_o, w_lq, w_lk, w_lv, w_lo, sem)
        idx_in = ctx.enter_context(nc.sbuf_tensor("p_idx_in", [P, KT], I32))
        idx_mid = ctx.enter_context(nc.sbuf_tensor("p_idx_mid", [P, FT], I32))
        gathered = ctx.enter_context(nc.sbuf_tensor("p_gathered", [P, 2, FT * DM], F32))
        idx_loaded, g_in = sem("p_idx_loaded"), [sem("p_g_in0"), sem("p_g_in1")]

        def early(pool):
            start_gathers(pool, gathered, idx_in, idx_mid, idx_loaded, g_in, (w_gateT, w_upT),
                          ri_in_cols, ri_mid_cols, ri_mid_last)

        cross_phase(nc, X, const, const_in, early, tile_loaded, ctx_in, ctxT_in, x_WqT, x_WkT, x_Wv, x_WoT,
                    x_bo, x_g, sem)
        st = ctx.enter_context(nc.sbuf_tensor("f_st", [P, NT, 6], F32))
        mv = ctx.enter_context(nc.sbuf_tensor("f_mv", [P, NT, 2], F32))
        rs = ctx.enter_context(nc.sbuf_tensor("f_rs", [P, NT], F32))
        w16 = ctx.enter_context(nc.sbuf_tensor("w16_ffn", [P, 2, 2, KT, FF], F16))
        wd16 = ctx.enter_context(nc.sbuf_tensor("wd16_ffn", [P, 2, FT, DM], F16))
        weight_phase(nc, X, st, mv, rs, const, w16, wd16, gathered, idx_mid, g_in, w_downT, scratch, sem)
        feed_forward_phase(nc, X, st, mv, rs, const, const_in, gathered[:, :, :], w16, wd16, ri_in, out, sem)


def kernel(**inputs):
    import concourse.bacc as bacc
    from concourse.bass_utils import run_bass_kernel_spmd

    nc = bacc.Bacc("TRN2", target_bir_lowering=False, num_devices=1)
    arrays, args = {}, []

    def give(name, a):
        a = np.ascontiguousarray(a)
        arrays[name] = a
        args.append(nc.dram_tensor(name, a.shape, mybir.dt.from_np(a.dtype), kind="ExternalInput").ap())

    give("shape_constants", shape_constants())
    give("x", np.asarray(inputs["x"]).reshape(TOK, DM))
    give("ctx", np.asarray(inputs["ctx_4096"]).reshape(TOK, DM))
    give("ctxT", np.asarray(inputs["ctx_4096"]).transpose(0, 2, 1))
    for n in ("w_q", "w_k", "w_v", "w_o", "w_lq", "w_lk", "w_lv", "w_lo"):
        give(n, np.asarray(inputs["L0_attn_" + n]))
    for n, flip in (("Wq", True), ("Wk", True), ("Wv", False), ("Wo", True), ("bo", False), ("g", False)):
        a = np.asarray(inputs["L0_xattn_" + n])
        give("x_" + n, a.T if flip else a)
    for n in ("w_gate", "w_up", "w_down"):
        give(n, np.asarray(inputs["L0_ffn_" + n]).T)
    ri_in, ri_mid = np.asarray(inputs["L0_ffn_ri_in"]), np.asarray(inputs["L0_ffn_ri_mid"])
    whole = (FT - 1) * P
    give("ri_in", ri_in)
    give("ri_in_cols", ri_in.reshape(KT, P).T)
    give("ri_mid_cols", ri_mid[:whole].reshape(FT - 1, P).T)
    give("ri_mid_last", ri_mid[whole:].reshape(FF - whole, 1))
    args.append(nc.dram_tensor("out", (TOK, DM), F32, kind="ExternalOutput").ap())
    decoder_layer(nc, *args)
    r = run_bass_kernel_spmd(nc, [arrays], core_ids=[0])
    return r.results[0]["out"].reshape(BATCH, SEQ, DM)
```
